# Optimizing a Trainium2 kernel written in Bass

```python
import numpy as np
import jax
import jax.numpy as jnp

def _softmax(x, axis=-1):
    return jax.nn.softmax(x, axis=axis)

def _gelu(x):
    return jax.nn.gelu(x, approximate=True)

def _silu(x):
    return jax.nn.silu(x)

def _sigmoid(x):
    return jax.nn.sigmoid(x)

def _layernorm(x, axis=-1, eps=1e-05):
    m = jnp.mean(x, axis=axis, keepdims=True)
    v = jnp.var(x, axis=axis, keepdims=True)
    return (x - m) / jnp.sqrt(v + eps)

def _scatter_add(tgt, idx, src, axis=0):
    return tgt.at[idx].add(src)

def _segment_sum(src, seg, n):
    return jax.ops.segment_sum(src, seg, n)
kernel_name = 'mk_gnn_preln_d1_gnn_r32_3dbe6e'

def setup_inputs(seed: int=0):
    np.random.seed(seed)
    _w = jnp.asarray

    def _rec_inputs():
        import jax
        import jax.numpy as jnp
        _gk = jax.random.key(seed)
        x = -0.000364 + 1 * jax.random.normal(jax.random.fold_in(_gk, 1), (625, 768), jnp.float32)
        src = jax.random.randint(jax.random.fold_in(_gk, 2), (20000,), 0, 625, jnp.int32)
        dst = jnp.minimum((625 * jax.random.uniform(jax.random.fold_in(_gk, 3), (20000,)) ** 2.0).astype(jnp.int32), 19999)
        _o = jnp.argsort(dst, stable=True)
        src = src[_o]
        dst = dst[_o]
        return (x, src, dst)
    x, src, dst = _rec_inputs()

    def _L0_gnn_setup():
        import jax, jax.numpy as jnp
        import numpy as np
        N, E, DIM, HEADS = (625, 10000, 768, 8)
        HD = DIM // HEADS
        EPS = 1e-05

        def layer_norm(x, w, b):
            mu = jnp.mean(x, axis=-1, keepdims=True)
            var = jnp.var(x, axis=-1, keepdims=True)
            return (x - mu) * jax.lax.rsqrt(var + EPS) * w + b

        def gatv2(x, src, dst, Ws, bs, Wd, bd, attn):
            H, D = attn.shape
            fs = (x @ Ws + bs).reshape(-1, H, D)
            fd = (x @ Wd + bd).reshape(-1, H, D)
            e = jax.nn.leaky_relu(fs[src] + fd[dst], 0.2)
            logits = jnp.einsum('ehd,hd->eh', e, attn)
            m = jax.ops.segment_max(logits, dst, num_segments=N)
            ex = jnp.exp(logits - m[dst])
            denom = jax.ops.segment_sum(ex, dst, num_segments=N)
            alpha = ex / denom[dst]
            out = jax.ops.segment_sum(alpha[:, :, None] * fs[src], dst, num_segments=N)
            return jax.nn.elu(out)
        key = jax.random.key(seed)
        ks = jax.random.split(key, 10)
        s = 1.0 / np.sqrt(DIM)
        return {'x': jax.random.normal(ks[0], (N, DIM), jnp.float32), 'src': jax.random.randint(ks[1], (E,), 0, N, jnp.int32), 'dst': jax.random.randint(ks[2], (E,), 0, N, jnp.int32), 'W1s': jax.random.normal(ks[3], (DIM, DIM), jnp.float32) * s, 'b1s': jnp.zeros((DIM,), jnp.float32), 'W1d': jax.random.normal(ks[4], (DIM, DIM), jnp.float32) * s, 'b1d': jnp.zeros((DIM,), jnp.float32), 'attn1': jax.random.normal(ks[5], (HEADS, HD), jnp.float32) * s, 'ln1_w': jnp.ones((DIM,), jnp.float32), 'ln1_b': jnp.zeros((DIM,), jnp.float32), 'Wos': jax.random.normal(ks[6], (DIM, DIM), jnp.float32) * s, 'bos': jnp.zeros((DIM,), jnp.float32), 'Wod': jax.random.normal(ks[7], (DIM, DIM), jnp.float32) * s, 'bod': jnp.zeros((DIM,), jnp.float32), 'attno': jax.random.normal(ks[8], (1, DIM), jnp.float32) * s, 'lno_w': jnp.ones((DIM,), jnp.float32), 'lno_b': jnp.zeros((DIM,), jnp.float32)}
    _L0_gnn_all = _L0_gnn_setup()
    _L0_gnn_in = {k: v for k, v in _L0_gnn_all.items() if k in ('W1s', 'b1s', 'W1d', 'b1d', 'attn1', 'ln1_w', 'ln1_b', 'Wos', 'bos', 'Wod', 'bod', 'attno', 'lno_w', 'lno_b')}
    del _L0_gnn_all
    return {'x': x, 'src': src, 'dst': dst, 'L0_gnn_W1s': _L0_gnn_in['W1s'], 'L0_gnn_b1s': _L0_gnn_in['b1s'], 'L0_gnn_W1d': _L0_gnn_in['W1d'], 'L0_gnn_b1d': _L0_gnn_in['b1d'], 'L0_gnn_attn1': _L0_gnn_in['attn1'], 'L0_gnn_ln1_w': _L0_gnn_in['ln1_w'], 'L0_gnn_ln1_b': _L0_gnn_in['ln1_b'], 'L0_gnn_Wos': _L0_gnn_in['Wos'], 'L0_gnn_bos': _L0_gnn_in['bos'], 'L0_gnn_Wod': _L0_gnn_in['Wod'], 'L0_gnn_bod': _L0_gnn_in['bod'], 'L0_gnn_attno': _L0_gnn_in['attno'], 'L0_gnn_lno_w': _L0_gnn_in['lno_w'], 'L0_gnn_lno_b': _L0_gnn_in['lno_b']}

def reference(x, src, dst, L0_gnn_W1s, L0_gnn_b1s, L0_gnn_W1d, L0_gnn_b1d, L0_gnn_attn1, L0_gnn_ln1_w, L0_gnn_ln1_b, L0_gnn_Wos, L0_gnn_bos, L0_gnn_Wod, L0_gnn_bod, L0_gnn_attno, L0_gnn_lno_w, L0_gnn_lno_b):
    import jax
    import jax.numpy as jnp

    def _L0_gnn_ref(x, src, dst, W1s, b1s, W1d, b1d, attn1, ln1_w, ln1_b, Wos, bos, Wod, bod, attno, lno_w, lno_b):
        import jax, jax.numpy as jnp
        import numpy as np
        N, E, DIM, HEADS = (625, 10000, 768, 8)
        HD = DIM // HEADS
        EPS = 1e-05

        def layer_norm(x, w, b):
            mu = jnp.mean(x, axis=-1, keepdims=True)
            var = jnp.var(x, axis=-1, keepdims=True)
            return (x - mu) * jax.lax.rsqrt(var + EPS) * w + b

        def gatv2(x, src, dst, Ws, bs, Wd, bd, attn):
            H, D = attn.shape
            fs = (x @ Ws + bs).reshape(-1, H, D)
            fd = (x @ Wd + bd).reshape(-1, H, D)
            e = jax.nn.leaky_relu(fs[src] + fd[dst], 0.2)
            logits = jnp.einsum('ehd,hd->eh', e, attn)
            m = jax.ops.segment_max(logits, dst, num_segments=N)
            ex = jnp.exp(logits - m[dst])
            denom = jax.ops.segment_sum(ex, dst, num_segments=N)
            alpha = ex / denom[dst]
            out = jax.ops.segment_sum(alpha[:, :, None] * fs[src], dst, num_segments=N)
            return jax.nn.elu(out)
        h = gatv2(x, src, dst, W1s, b1s, W1d, b1d, attn1).reshape(N, DIM)
        h = layer_norm(h + x, ln1_w, ln1_b)
        out = gatv2(h, src, dst, Wos, bos, Wod, bod, attno).reshape(N, DIM)
        return layer_norm(out, lno_w, lno_b)
    h = jnp.maximum(_layernorm(x, axis=-1), 0.0)
    x = x + _L0_gnn_ref(h, src, dst, L0_gnn_W1s, L0_gnn_b1s, L0_gnn_W1d, L0_gnn_b1d, L0_gnn_attn1, L0_gnn_ln1_w, L0_gnn_ln1_b, L0_gnn_Wos, L0_gnn_bos, L0_gnn_Wod, L0_gnn_bod, L0_gnn_attno, L0_gnn_lno_w, L0_gnn_lno_b)
    return x

_drawn_inputs = setup_inputs


def setup_inputs(seed=0):
    import zlib

    import numpy as np

    out = dict(_drawn_inputs(seed))
    spreads = {'L0_gnn_b1s': (0.0, 0.1),
     'L0_gnn_b1d': (0.0, 0.8),
     'L0_gnn_ln1_w': (1.0, 0.2),
     'L0_gnn_ln1_b': (0.0, 0.1),
     'L0_gnn_bos': (0.0, 0.1),
     'L0_gnn_bod': (0.0, 0.8),
     'L0_gnn_lno_w': (1.0, 0.2),
     'L0_gnn_lno_b': (0.0, 0.1)}
    factors = {'L0_gnn_W1d': 8.0, 'L0_gnn_attn1': 3.432}
    for name, (base, spread) in spreads.items():
        noise = np.random.default_rng([zlib.crc32(name.encode()), seed]).standard_normal(out[name].shape)
        drawn = base * np.exp(spread * noise) if base else spread * noise
        out[name] = jnp.asarray(drawn.astype(out[name].dtype))
    for name, factor in factors.items():
        out[name] = (out[name] * factor).astype(out[name].dtype)
    return out
```

```python
import concourse.bass as bass
from concourse import mybir
from contextlib import ExitStack


def gnn_kernel(nc, x, src, dst, W1s, b1s, W1d, b1d, attn1, ln1_w, ln1_b,
               Wos, bos, Wod, bod, attno, lno_w, lno_b, out):
    f32, bf16, i32 = mybir.dt.float32, mybir.dt.bfloat16, mybir.dt.int32
    ALU, ACT, AX = mybir.AluOpType, mybir.ActivationFunctionType, mybir.AxisListType
    ds = bass.ds

    P = 128
    N, D = x.shape
    E = src.shape[0]
    NC = -(-N // P)
    NLAST = N - (NC - 1) * P
    KC = D // P
    H1 = attn1.shape[0]
    G = 4
    QT = -(-((E + (G - 1) * N) // G) // P)
    ROW = D + 8
    HALF = ROW // 2
    EP = 125
    ET = E // EP
    assert EP * ET == E and N <= NC * P and QT * P * G >= E
    NEG = -1.0e30
    EPS = 1e-5
    RING = 3
    LOOPS = QT // RING
    ITEMS = QT + NC - 1

    src_sorted = nc.dram_tensor("src_sorted", [E + ET, 1], i32).ap()
    src_win = nc.dram_tensor("src_win", [E + 1, G], i32).ap()
    fs_table = [nc.dram_tensor(f"fs_table{l}", [NC * P, ROW], f32).ap() for l in range(2)]
    fd_table = [nc.dram_tensor(f"fd_table{l}", [NC * P, ROW], f32).ap() for l in range(2)]
    h_saved = nc.dram_tensor("h_saved", [P, NC * D], f32).ap()

    ctx = ExitStack()
    with ctx:
        def sb(name, shape, dt=f32):
            return ctx.enter_context(nc.sbuf_tensor(name, shape, dt))

        def sem(name):
            return ctx.enter_context(nc.semaphore(name))

        vres = sb("vres", [P, QT, ROW])
        gring = sb("gring", [P, RING, G, ROW])
        fring = sb("fring", [P, RING, ROW])
        z = sb("z", [P, 2, D])
        a08 = sb("a08", [P, D])
        gmax = sb("gmax", [P, QT, H1])
        mask = sb("mask", [P, QT, G])
        srcq = sb("srcq", [P, QT, G], i32)
        dstrow = sb("dstrow", [P, QT], i32)
        dstq = sb("dstq", [P, QT])
        ident = sb("ident", [P, P])
        slotidx = sb("slotidx", [P, RING, G + 1], i32)
        redu = sb("redu", [P, G, H1])
        lgt = sb("lgt", [P, G, H1])
        lin = sb("lin", [P, RING, G, H1])
        dlt = sb("dlt", [P, RING, G, H1])
        diag_hi = sb("diag_hi", [P, 2, P])
        thr = sb("thr", [1, 16])
        items = sb("items", [1, 2, ITEMS + 1], i32)
        flag = sb("flag", [P, 1], i32)
        turn = sb("turn", [1, 2], i32)
        mnow = sb("mnow", [P, H1])

        ps = ctx.enter_context(nc.psum_tensor("ps", [P, 8, 512], f32))
        psf = ps[:, :, :].rearrange("p b n -> p (b n)")

        vflat = vres[:, :, :].rearrange("p t n -> p (t n)")
        gflat = gring[:, :, :, :].rearrange("p r g n -> p (r g n)")
        fflat = fring[:, :, :].rearrange("p r n -> p (r n)")
        zflat = z[:, :, :].rearrange("p r n -> p (r n)")

        class Carve:
            def __init__(self, flat):
                self.flat, self.at = flat, 0

            def __call__(self, shape, dt=f32):
                n = 1
                for k in shape:
                    n *= k
                words = -(-n * (2 if dt == bf16 else 4) // 4)
                v = self.flat[:, self.at:self.at + words]
                self.at += words
                assert self.at <= self.flat.shape[1]
                if dt != f32:
                    v = v.bitcast(dt)
                v = v[:, 0:n]
                if len(shape) == 2:
                    v = v.rearrange("p (a b) -> p a b", a=shape[0])
                if len(shape) == 3:
                    v = v.rearrange("p (a b c) -> p a b c", a=shape[0], b=shape[1])
                return v

        cv = Carve(vflat)
        xt = cv([NC, D])
        ht = cv([NC, D])
        hT = cv([KC, NC * P])
        tbl = cv([4, ROW])
        tmp = cv([2, D])
        bias = cv([2, D])
        a02 = cv([D])
        lnw = cv([D])
        lnb = cv([D])
        stats = cv([NC, 12])
        mv = cv([NC, 2])
        rstd = cv([NC])
        den = cv([NC, H1])
        ones = cv([P])
        tri_strict = cv([P])
        tri_incl = cv([P])
        oh_lo = cv([ET, P], bf16)
        oh_hi = cv([ET, NC], bf16)
        srcwin = cv([ET + G - 1], i32)
        win4 = cv([ET, G], i32)
        ch = Carve(hT.rearrange("p a b -> p (a b)"))
        dst_e = ch([ET], i32)
        dst_n = ch([ET], i32)
        digit = ch([2, ET], i32)
        digitf = ch([2, ET])
        unsorted_e = ch([ET])
        src_e = ch([ET], i32)
        nodecnt = ch([1])
        joint = ch([NC, P])
        base = ch([NC, P])
        rank = ch([NC, P])
        pos_f = ch([1])
        pos_i = ch([1], i32)
        src_c = ch([1], i32)
        cf = Carve(fflat)
        ohA = cf([2 * NC, P])
        ohB = cf([2 * NC, QT])
        cz = Carve(zflat)
        wB = cz([NC, 3, QT])
        wB2 = cz([NC, QT])
        cnt = cz([2, NC])
        cnt_i = cz([NC], i32)
        tot = cz([2, NC])
        run = cz([2, NC])
        first = cz([2, NC])
        posn = cz([2, NC])
        posi = cz([2 * NC], i32)
        posj = cz([2 * NC], i32)
        pdig = cz([2, 2 * NC])
        zero8 = cz([8])
        ct = Carve(tbl.rearrange("p a b -> p (a b)"))
        imp = ct([4, QT])
        ctot = ct([4, QT])
        crun = ct([4, QT])
        q = ct([4, QT])
        qidx = ct([QT])
        e0 = ct([QT])
        left = ct([QT])
        e0i = gmax[:, :, :].rearrange("p t h -> p (t h)")[:, 0:QT].bitcast(i32)
        iota4 = ct([G])
        zeroQ = ct([QT])
        iota_lo = ct([P])

        def combine_views(H):
            cg = Carve(gflat)
            v = {}
            v["mT"] = cg([H, P])
            v["fwd"] = cg([H, P])
            v["seg"] = cg([H, P])
            v["brk"] = cg([H * P + 1])
            v["dq"] = cg([P])
            v["outer"] = cg([2, P])
            v["edge"] = cg([4, H])
            v["val"] = cg([QT, 2])
            v["dqe"] = cg([QT, 2])
            v["link"] = cg([2 * QT + 1])
            v["sf"] = cg([QT, 2])
            v["sm"] = cg([QT, 2])
            v["back"] = cg([2, H])
            v["w"] = cg([QT, H])
            v["iota"] = cg([NC * P])
            v["hot"] = cg([RING, P])
            v["zrow"] = cg([512])
            return v

        wts = gflat[:, 0:2 * KC * D].rearrange("p (m k n) -> p m k n", m=2, k=KC)
        diag_lo = z[:, 1, :].rearrange("p (a b) -> p a b", b=P)

        def diag(t_mod2, j):
            k = t_mod2 * G + j
            return diag_lo[:, k, :] if k < KC else diag_hi[:, k - KC, :]

        edges_in = sem("edges_in")
        x_in = sem("x_in")
        pad_ready = sem("pad_ready")
        params_in = [sem(f"params_in{l}") for l in range(2)]
        weights_in = [sem(f"weights_in{l}") for l in range(2)]
        consts_ready = sem("consts_ready")
        pool_step = sem("pool_step")
        dve_step = sem("dve_step")
        act_step = sem("act_step")
        digits_ready = sem("digits_ready")
        hist_done = sem("hist_done")
        prep_in = sem("prep_in")
        prep_mm = sem("prep_mm")
        flag_ready = sem("flag_ready")
        src_copied = sem("src_copied")
        base_in = sem("base_in")
        base_mm = sem("base_mm")
        joint_ready = sem("joint_ready")
        joint_mm = sem("joint_mm")
        pos_ready = sem("pos_ready")
        scattered = sem("scattered")
        order_known = sem("order_known")
        win_in = sem("win_in")
        win4_ready = sem("win4_ready")
        win_stored = sem("win_stored")
        e0_ready = sem("e0_ready")
        srcq_in = sem("srcq_in")
        var_ready = sem("var_ready")
        sd_ready = sem("sd_ready")
        h_ready = sem("h_ready")
        h_stored = sem("h_stored")
        hT_mm = sem("hT_mm")
        hT_ready = sem("hT_ready")
        proj_mm = sem("proj_mm")
        proj_read = sem("proj_read")
        tbl_ready = sem("tbl_ready")
        tbl_stored = [sem(f"tbl_stored{k}") for k in range(4)]
        prep_done = sem("prep_done")
        idx_ready = [sem(f"idx_ready{l}") for l in range(2)]
        rows_in = [[sem(f"rows_in{l}_{r}") for r in range(RING)] for l in range(2)]
        lin_step = [sem(f"lin_step{l}") for l in range(2)]
        lin_ready = [sem(f"lin_ready{l}") for l in range(2)]
        dlt_ready = [sem(f"dlt_ready{l}") for l in range(2)]
        exp_done = [sem(f"exp_done{l}") for l in range(2)]
        prod_ready = [sem(f"prod_ready{l}") for l in range(2)]
        sum_mm = [sem(f"sum_mm{l}") for l in range(2)]
        sum_saved = [sem(f"sum_saved{l}") for l in range(2)]
        seg_in = sem("seg_in")
        seg_mm = sem("seg_mm")
        loop_step = [sem(f"loop_step{l}") for l in range(2)]
        gmax_saved = [sem(f"gmax_saved{l}") for l in range(2)]
        w_arg = sem("w_arg")
        w_mm = sem("w_mm")
        w_ready = sem("w_ready")
        wT_ready = sem("wT_ready")
        comb_const = sem("comb_const")
        hot_ready = [sem(f"hot_ready{l}") for l in range(2)]
        item_mm = [sem(f"item_mm{l}") for l in range(2)]
        neg_ready = sem("neg_ready")
        elu_exp = sem("elu_exp")
        h_back = sem("h_back")
        x_back = sem("x_back")
        y_ready = sem("y_ready")
        y_stored = sem("y_stored")

        heads = (H1, 1)
        params = ((W1s, b1s, W1d, b1d, attn1, ln1_w, ln1_b), (Wos, bos, Wod, bod, attno, lno_w, lno_b))

        class Link:
            def __init__(self, eng, s):
                self.eng, self.s, self.n = eng, s, 0

            def __call__(self, ins, trips=0):
                self.n += 1
                ins.then_inc(self.s, 1)
                self.eng.wait_ge(self.s, self.n + trips)

        def bc(ap, axis, n):
            v = ap.unsqueeze(axis)
            shape = list(v.shape)
            shape[axis] = n
            return v.to_broadcast(shape)

        def stored_target(l, k):
            per_layer = len([n for n in range(2 * NC) if n % 4 == k])
            return 16 * per_layer * (l + 1)

        def gmx(l):
            return gmax[:, :, :] if l == 0 else gmax[:, :, :].rearrange("p t h -> p (t h)")[:, 0:QT].unsqueeze(2)

        block = ctx.enter_context(nc.Block())

        @block.sync
        def _(sp):
            sp.dma_start(dst_e[0:EP, :], dst.rearrange("(p t) -> p t", t=ET)).then_inc(edges_in, 16)
            sp.wait_ge(consts_ready, 1)
            sp.dma_start(dst_n[0:EP - 1, :], dst[1:1 + (EP - 1) * ET].rearrange("(p t) -> p t", t=ET))\
                .then_inc(edges_in, 16)
            sp.dma_start(dst_n[EP - 1:EP, 0:ET - 1], dst[1 + (EP - 1) * ET:E].rearrange("(a t) -> a t", a=1))\
                .then_inc(edges_in, 16)
            sp.dma_start(src_e[0:EP, :], src.rearrange("(p t) -> p t", t=ET)).then_inc(edges_in, 16)
            sp.dma_start(xt[:, 0:NC - 1, :], x[0:(NC - 1) * P, :].rearrange("(c p) d -> p c d", p=P))\
                .then_inc(x_in, 16)
            sp.wait_ge(pad_ready, 1)
            sp.dma_start(xt[0:NLAST, NC - 1, :], x[(NC - 1) * P:N, :]).then_inc(x_in, 16)

            def load_params(l):
                _, bs, _, bd, at, _, _ = params[l]
                if l:
                    sp.wait_ge(item_mm[l - 1], ITEMS)
                for to, of in ((bias[:, 0, :], bs), (bias[:, 1, :], bd)):
                    sp.dma_start(to, of.partition_broadcast(P)).then_inc(params_in[l], 16)
                sp.dma_start(a08[:, :], at.rearrange("h d -> (h d)").partition_broadcast(P))\
                    .then_inc(params_in[l], 16)

            def load_weights(l):
                if l:
                    sp.wait_ge(item_mm[l - 1], ITEMS)
                for m in range(2):
                    sp.dma_start(wts[:, m, :, :], params[l][2 * m].rearrange("(k p) n -> p k n", p=P))\
                        .then_inc(weights_in[l], 16)

            load_params(0)
            load_weights(0)
            sp.wait_ge(edges_in, 64)
            sp.dma_start(src_sorted[0:E, :].rearrange("(p t) a -> p (t a)", t=ET), src_e[0:EP, :])\
                .then_inc(src_copied, 16)
            sp.dma_start(src_sorted[E:E + ET, :].rearrange("(a t) o -> a (t o)", a=1), srcwin[0:1, 0:ET])\
                .then_inc(src_copied, 16)
            sp.wait_ge(order_known, 1)
            sp.dma_start(srcwin[0:EP, 0:ET], src_sorted[0:E, :].rearrange("(p t) a -> p (t a)", t=ET))\
                .then_inc(win_in, 16)
            sp.dma_start(srcwin[0:EP, ET:ET + G - 1],
                         src_sorted[ET:E + ET, :].rearrange("(p t) a -> p (t a)", t=ET)[:, 0:G - 1])\
                .then_inc(win_in, 16)
            sp.wait_ge(win4_ready, 1)
            sp.dma_start(src_win[0:E, :].rearrange("(p t) g -> p (t g)", t=ET),
                         win4[0:EP, :, :].rearrange("p t g -> p (t g)")).then_inc(win_stored, 16)
            sp.dma_start(src_win[E:E + 1, :], srcwin[EP:EP + 1, 0:G]).then_inc(win_stored, 16)
            sp.wait_ge(h_ready, NC)
            sp.dma_start(h_saved, ht[:, :, :].rearrange("p c d -> p (c d)")).then_inc(h_stored, 16)

            for l in range(2):
                for n in range(2 * NC):
                    c, m = n // 2, n % 2
                    to = (fs_table, fd_table)[m][l]
                    sp.wait_ge(tbl_ready, 2 * NC * l + n + 1)
                    sp.dma_start(to[c * P:(c + 1) * P, :], tbl[:, n % 4, :]).then_inc(tbl_stored[n % 4], 16)
                if l == 0:
                    load_params(1)
                    load_weights(1)
                    sp.wait_ge(h_stored, 16)
                    sp.dma_start(ht[:, :, :].rearrange("p c d -> p (c d)"), h_saved).then_inc(h_back, 16)
                    sp.dma_start(lnw, ln1_w.partition_broadcast(P)).then_inc(h_back, 16)
                    sp.dma_start(lnb, ln1_b.partition_broadcast(P)).then_inc(h_back, 16)
            sp.wait_ge(item_mm[1], ITEMS)
            sp.dma_start(ht[:, 0:NC - 1, :], x[0:(NC - 1) * P, :].rearrange("(c p) d -> p c d", p=P))\
                .then_inc(x_back, 16)
            sp.dma_start(ht[0:NLAST, NC - 1, :], x[(NC - 1) * P:N, :]).then_inc(x_back, 16)
            sp.dma_start(lnw, lno_w.partition_broadcast(P)).then_inc(x_back, 16)
            sp.dma_start(lnb, lno_b.partition_broadcast(P)).then_inc(x_back, 16)
            for c in range(NC):
                k = P if c < NC - 1 else NLAST
                sp.wait_ge(y_ready, c + 1)
                sp.dma_start(out[c * P:c * P + k, :], xt[0:k, c, :]).then_inc(y_stored, 16)
            sp.wait_ge(y_stored, 16 * NC)

        @block.gpsimd
        def _(po):
            step = Link(po, pool_step)

            def take_wait():
                nc.gpsimd.tensor_tensor(turn[:, 1:2], turn[:, 0:1], turn[:, 0:1], ALU.add)

            step(nc.gpsimd.memset(turn[:, :], 0))
            step(nc.gpsimd.memset(dst_n[96:P, :], 1 << 20))
            nc.gpsimd.memset(srcwin[:, :], 0).then_inc(consts_ready, 1)
            step(nc.gpsimd.memset(ident[:, :], 0.0))
            step(nc.gpsimd.affine_select(out=ident[:, :], in_=ident[:, :], compare_op=ALU.not_equal, fill=1.0,
                                         base=0, pattern=[[-1, P]], channel_multiplier=1))
            step(nc.gpsimd.memset(ones, 1.0))
            for tri, op in ((tri_strict, ALU.is_gt), (tri_incl, ALU.is_ge)):
                step(nc.gpsimd.affine_select(out=tri, in_=ones, compare_op=op, fill=0.0,
                                             base=0, pattern=[[1, P]], channel_multiplier=-1))
            nc.gpsimd.iota(iota_lo, pattern=[[1, P]], base=0, channel_multiplier=0,
                           allow_small_or_imprecise_dtypes=True)
            nc.gpsimd.iota(iota4, pattern=[[1, G]], base=0, channel_multiplier=0,
                           allow_small_or_imprecise_dtypes=True)
            step(nc.gpsimd.iota(qidx, pattern=[[P, QT]], base=0, channel_multiplier=1,
                                allow_small_or_imprecise_dtypes=True))
            nc.gpsimd.memset(zeroQ, 0.0).then_inc(consts_ready, 1)

            po.wait_ge(src_copied, 32)
            po.wait_ge(flag_ready, 1)
            not_sorted = po.value_load(flag[0:1, 0:1])
            with po.If(not_sorted > 0):
                with po.Fori(0, ET) as i:
                    po.wait_ge(pos_ready, i + 1)
                    take_wait()
                    po.indirect_dma_start(src_sorted, bass.IndirectOffsetOnAxis(ap=pos_i[0:EP, :], axis=0),
                                          src_c[0:EP, :], None).then_inc(scattered, 16)
                po.wait_ge(scattered, 16 * ET)
                po.sem_inc(order_known, 1)
            with po.Else():
                po.sem_inc(order_known, 1)

            po.wait_ge(win_stored, 32)
            po.wait_ge(e0_ready, 1)
            for t in range(QT):
                po.indirect_dma_start(srcq[:, t, :], None, src_win,
                                      bass.IndirectOffsetOnAxis(ap=e0i[:, t:t + 1], axis=0)).then_inc(srcq_in, 16)
            po.wait_ge(srcq_in, 16 * QT)

            def gathers(l, t, u, trip, first):
                if first:
                    for k in range(4):
                        po.wait_ge(tbl_stored[k], stored_target(l, k))
                else:
                    po.wait_ge(sum_mm[l], t - (RING - 1))
                    take_wait()
                nc.gpsimd.tensor_copy(slotidx[:, u, 0:G],
                                      srcq[:, ds(t, 1), :].rearrange("p a g -> p (a g)"))\
                    .then_inc(idx_ready[l], 1)
                nc.gpsimd.tensor_copy(slotidx[:, u, G:G + 1], dstrow[:, ds(t, 1)]).then_inc(idx_ready[l], 1)
                po.wait_ge(idx_ready[l], t * 2 + 2)
                take_wait()
                po.indirect_dma_start(fring[:, u, :], None, fd_table[l],
                                      bass.IndirectOffsetOnAxis(ap=slotidx[:, u, G:G + 1], axis=0))\
                    .then_inc(rows_in[l][u], 16)
                for j in range(G):
                    po.indirect_dma_start(gring[:, u, j, :], None, fs_table[l],
                                          bass.IndirectOffsetOnAxis(ap=slotidx[:, u, j:j + 1], axis=0))\
                        .then_inc(rows_in[l][u], 16)

            def linear(l, t, u, trip):
                H = heads[l]
                po.wait_ge(rows_in[l][u], (trip + 1) * (16 * (G + 1)))
                po.wait_ge(prep_done, 1)
                nc.gpsimd.tensor_tensor(lin[:, u, :, 0:H], gring[:, u, :, D:D + H],
                                        bc(fring[:, u, D:D + H], 1, G), ALU.add).then_inc(lin_step[l], 1)
                po.wait_ge(lin_step[l], t + 1)
                po.wait_ge(prep_done, 1)
                mk = mask[:, ds(t, 1), :].rearrange("p a g -> p (a g)")
                nc.gpsimd.tensor_tensor(lin[:, u, :, 0:H], lin[:, u, :, 0:H],
                                        bc(mk, 2, H), ALU.add).then_inc(lin_ready[l], 1)

            for l in range(2):
                gathers(l, 0, 0, 0, True)
                gathers(l, 1, 1, 0, True)
                linear(l, 0, 0, 0)
                gathers(l, 2, 2, 0, True)
                linear(l, 1, 1, 0)
                with po.Fori(1, LOOPS) as i:
                    for u in range(RING):
                        gathers(l, i * RING + u, u, i, False)
                        prev = (u - 1) % RING
                        linear(l, i * RING + (u - 1), prev, i if u else i - 1)
                for t in range(LOOPS * RING, QT):
                    gathers(l, t, t % RING, t // RING, False)
                    linear(l, t - 1, (t - 1) % RING, (t - 1) // RING)
                linear(l, QT - 1, (QT - 1) % RING, (QT - 1) // RING)

                cb = combine_views(heads[l])
                po.wait_ge(sum_mm[l], QT)
                nc.gpsimd.memset(cb["zrow"][0:1, :], 0.0).then_inc(comb_const, 1)
                nc.gpsimd.iota(cb["iota"], pattern=[[1, NC * P]], base=0, channel_multiplier=0,
                               allow_small_or_imprecise_dtypes=True).then_inc(comb_const, 1)

        @block.scalar
        def _(act):
            step = Link(act, act_step)

            def sqrt_var(n):
                act.wait_ge(var_ready, n)
                nc.scalar.activation(rstd, rstd, ACT.Sqrt).then_inc(sd_ready, 1)

            def copy_hT(l):
                for c in range(NC):
                    act.wait_ge(hT_mm, NC * l + c + 1)
                    b = 2 * (c % 2)
                    nc.scalar.activation(hT[:, :, c * P:(c + 1) * P],
                                         psf[:, b * 512:b * 512 + D].rearrange("p (k n) -> p k n", k=KC),
                                         ACT.Copy).then_inc(hT_ready, 1)

            def weigh(l, t, u, trip, first):
                H = heads[l]
                act.wait_ge(dlt_ready[l], t + 1)
                if l == 0:
                    step_n = nc.scalar.activation(gring[:, u, :, D:D + H], dlt[:, u, :, 0:H], ACT.Exp)
                    step_n.then_inc(exp_done[l], 1)
                    act.wait_ge(exp_done[l], t + 1)
                    for j in range(G):
                        for h in range(H):
                            part = gring[:, u, j, h * (D // H):(h + 1) * (D // H)]
                            last = nc.scalar.activation(part, part, ACT.Copy,
                                                        scale=gring[:, u, j, D + h:D + h + 1])
                    last.then_inc(prod_ready[l], 1)

            def save(l, t, u):
                act.wait_ge(sum_mm[l], t + 1)
                b = 2 * u
                row = vres[:, ds(t, 1), :].rearrange("p a n -> p (a n)")
                nc.scalar.activation(row[:, 0:HALF], ps[:, b, 0:HALF], ACT.Copy)
                nc.scalar.activation(row[:, HALF:ROW], ps[:, b + 1, 0:HALF], ACT.Copy).then_inc(sum_saved[l], 1)

            def weigh2(l, t, u, par, trip, first):
                act.wait_ge(dlt_ready[l], t + 1)
                nc.scalar.activation(dlt[:, u, :, 0:1], dlt[:, u, :, 0:1], ACT.Exp).then_inc(exp_done[l], 1)
                if not first:
                    act.wait_ge(sum_mm[l], t - 1)
                act.wait_ge(exp_done[l], t + 1)
                for j in range(G):
                    last = nc.scalar.activation(diag(par, j), ident[:, :], ACT.Copy, scale=dlt[:, u, j, 0:1])
                last.then_inc(prod_ready[l], 1)

            sqrt_var(1)
            for l in range(2):
                copy_hT(l)
                for k in range(4):
                    act.wait_ge(tbl_stored[k], stored_target(l, k))
                if l == 0:
                    weigh(l, 0, 0, 0, True)
                    for t in range(1, RING):
                        weigh(l, t, t, 0, True)
                        save(l, t - 1, t - 1)
                    with act.Fori(1, LOOPS) as i:
                        for u in range(RING):
                            weigh(l, i * RING + u, u, i, False)
                            save(l, i * RING + (u - 1), (u - 1) % RING)
                    for t in range(LOOPS * RING, QT):
                        weigh(l, t, t % RING, t // RING, False)
                        save(l, t - 1, (t - 1) % RING)
                    save(l, QT - 1, (QT - 1) % RING)
                else:
                    SIX = 2 * RING
                    weigh2(l, 0, 0, 0, 0, True)
                    for t in range(1, SIX):
                        weigh2(l, t, t % RING, t % 2, 0, t < 2)
                        save(l, t - 1, (t - 1) % RING)
                    with act.Fori(1, QT // SIX) as i:
                        for u in range(SIX):
                            weigh2(l, i * SIX + u, u % RING, u % 2, i, False)
                            save(l, i * SIX + (u - 1), (u - 1) % RING)
                    for t in range(QT // SIX * SIX, QT):
                        weigh2(l, t, t % RING, t % 2, 0, False)
                        save(l, t - 1, (t - 1) % RING)
                    save(l, QT - 1, (QT - 1) % RING)
                cb = combine_views(heads[l])
                act.wait_ge(w_arg, l + 1)
                nc.scalar.activation(cb["mT"][0:QT, :, :], cb["mT"][0:QT, :, :], ACT.Exp).then_inc(wT_ready, 1)
                for c in range(NC):
                    act.wait_ge(neg_ready, NC * l + c + 1)
                    nc.scalar.activation(tmp[:, c % 2, :], tmp[:, c % 2, :], ACT.Exp).then_inc(elu_exp, 1)
                sqrt_var(l + 2)

        @block.vector
        def _(ve):
            step = Link(ve, dve_step)
            tt, ts = nc.vector.tensor_tensor, nc.vector.tensor_scalar

            def norm(n_call):
                for c in range(NC):
                    for k in range(2):
                        step(nc.vector.bn_stats(stats[:, c, 6 * k:6 * k + 6], xt[:, c, k * (D // 2):(k + 1) * (D // 2)]))
                    step(nc.vector.bn_aggr(mv[:, c, :], stats[:, c, :]))
                ts(rstd.unsqueeze(2), mv[:, :, 1:2], EPS, None, ALU.add).then_inc(var_ready, 1)
                ve.wait_ge(sd_ready, n_call)
                step(nc.vector.reciprocal(rstd, rstd))

            nc.vector.memset(xt[96:P, NC - 1, :], 0.0).then_inc(pad_ready, 1)
            step(nc.vector.memset(zero8, 0.0))
            ve.wait_ge(edges_in, 64)
            ve.wait_ge(consts_ready, 2)

            step(tt(unsorted_e[0:EP, :], dst_e[0:EP, :], dst_n[0:EP, :], ALU.is_gt))
            step(nc.vector.reduce_sum(nodecnt[0:EP, :], unsorted_e[0:EP, :], axis=AX.X))
            step(ts(digit[0:EP, 0, :], dst_e[0:EP, :], P - 1, None, ALU.bitwise_and))
            step(ts(digit[0:EP, 1, :], dst_e[0:EP, :], P.bit_length() - 1, None, ALU.logical_shift_right))
            step(nc.vector.tensor_copy(digitf[0:EP, :, :], digit[0:EP, :, :]))
            step(tt(oh_lo[0:EP, :, :], bc(iota_lo[0:EP, :], 1, ET), bc(digitf[0:EP, 0, :], 2, P), ALU.is_equal))
            tt(oh_hi[0:EP, :, :], bc(iota_lo[0:EP, 0:NC], 1, ET), bc(digitf[0:EP, 1, :], 2, NC),
               ALU.is_equal).then_inc(digits_ready, 1)

            ve.wait_ge(hist_done, 1)
            nc.vector.tensor_copy(flag[0:1, :], ps[0:1, 1, 0:1]).then_inc(flag_ready, 1)
            step(nc.vector.tensor_copy(cnt[:, 0, :], ps[:, 0, 0:NC]))
            step(ts(cnt_i, cnt[:, 0, :], float(G - 1), None, ALU.add))
            step(ts(cnt_i, cnt_i, G.bit_length() - 1, None, ALU.logical_shift_right))
            nc.vector.tensor_copy(cnt[:, 1, :], cnt_i).then_inc(prep_in, 1)
            ve.wait_ge(prep_mm, 1)
            step(nc.vector.tensor_copy(tot.rearrange("p a b -> p (a b)"), ps[:, 2, 0:2 * NC]))
            for k in range(2):
                step(nc.vector.tensor_tensor_scan(run[:, k, :], tot[:, k, :], zero8[:, 0:NC], 0.0, ALU.add, ALU.add))
            step(tt(run, run, tot, ALU.subtract))
            step(tt(first.rearrange("p a b -> p (a b)"), run.rearrange("p a b -> p (a b)"),
                    ps[:, 3, 0:2 * NC], ALU.add))
            step(tt(posn[:, 0, :], first[:, 1, :], cnt[:, 1, :], ALU.add))
            step(nc.vector.tensor_copy(posn[:, 1, :], first[:, 1, :]))

            ve.wait_ge(flag_ready, 1)
            not_sorted = ve.value_load(flag[0:1, 0:1])
            with ve.If(not_sorted > 0):
                for c in range(NC):
                    ts(rank[:, c, :], ident[:, :], first[:, 0, c:c + 1], None, ALU.mult).then_inc(base_in, 1)
                ve.wait_ge(base_mm, 1)
                nc.vector.tensor_copy(base.rearrange("p a b -> p (a b)"), psf[:, 2048:2048 + NC * P])\
                    .then_inc(base_in, 1)
                with ve.Fori(0, ET) as i:
                    ve.wait_ge(base_in, NC + 1 + i * 7)
                    ve.wait_ge(base_in, NC + 1)
                    tt(joint[0:EP, :, :], oh_lo[0:EP, ds(i, 1), :].to_broadcast([EP, NC, P]),
                       bc(oh_hi[0:EP, ds(i, 1), :].rearrange("p a c -> p (a c)"), 2, P),
                       ALU.mult).then_inc(joint_ready, 1)
                    ve.wait_ge(joint_mm, i + 1)
                    flat = lambda v: v[0:EP, :, :].rearrange("p a b -> p (a b)")
                    tt(flat(rank), psf[0:EP, 2048:2048 + NC * P], flat(base), ALU.add).then_inc(base_in, 1)
                    ve.wait_ge(base_in, NC + 2 + i * 7)
                    tt(flat(rank), flat(rank), flat(joint), ALU.mult).then_inc(base_in, 1)
                    ve.wait_ge(base_in, NC + 3 + i * 7)
                    nc.vector.reduce_sum(pos_f[0:EP, :], flat(rank), axis=AX.X).then_inc(base_in, 1)
                    ve.wait_ge(base_in, NC + 4 + i * 7)
                    nc.vector.tensor_copy(pos_i[0:EP, :], pos_f[0:EP, :]).then_inc(base_in, 1)
                    ve.wait_ge(base_in, NC + 5 + i * 7)
                    nc.vector.tensor_copy(src_c[0:EP, :], src_e[0:EP, ds(i, 1)]).then_inc(base_in, 1)
                    ve.wait_ge(base_in, NC + 6 + i * 7)
                    tt(base.rearrange("p a b -> p (a b)"), base.rearrange("p a b -> p (a b)"),
                       psf[:, 3072:3072 + NC * P], ALU.add).then_inc(base_in, 1)
                    ve.wait_ge(base_in, NC + 7 + i * 7)
                    nc.vector.memset(rank[:, 0, 0:1], 0.0).then_inc(base_in, 1)
                    ve.sem_inc(pos_ready, 1)
                    ve.wait_ge(scattered, i * 16 + 16)
            with ve.Else():
                ve.wait_ge(flag_ready, 1)

            step(nc.vector.tensor_copy(posi, posn.rearrange("p a b -> p (a b)")))
            step(ts(posj, posi, P - 1, None, ALU.bitwise_and))
            step(nc.vector.tensor_copy(pdig[:, 0, :], posj))
            step(ts(posi, posi, P.bit_length() - 1, None, ALU.logical_shift_right))
            step(nc.vector.tensor_copy(pdig[:, 1, :], posi))
            step(tt(ohA, bc(iota_lo, 1, 2 * NC), bc(pdig[:, 0, :], 2, P), ALU.is_equal))
            step(tt(ohB, bc(iota_lo[:, 0:QT], 1, 2 * NC), bc(pdig[:, 1, :], 2, QT), ALU.is_equal))
            step(nc.vector.tensor_copy(wB[:, :, 0, :], ohB[:, 0:NC, :]))
            step(tt(wB[:, :, 1, :], ohB[:, 0:NC, :], bc(cnt[:, 0, :], 2, QT), ALU.mult))
            step(tt(wB[:, :, 2, :], ohB[:, 0:NC, :], bc(cnt[:, 1, :], 2, QT), ALU.mult))
            tt(wB2, ohB[:, NC:2 * NC, :], bc(cnt[:, 0, :], 2, QT), ALU.mult).then_inc(prep_in, 1)
            ve.wait_ge(prep_mm, 2)
            step(nc.vector.tensor_copy(imp[:, 0:3, :].rearrange("p a b -> p (a b)"), ps[:, 0, 0:3 * QT]))
            nc.vector.tensor_copy(imp[:, 3, :], ps[:, 1, 0:QT]).then_inc(prep_in, 1)
            ve.wait_ge(prep_mm, 3)
            step(nc.vector.tensor_copy(ctot.rearrange("p a b -> p (a b)"), ps[:, 2, 0:4 * QT]))
            for k in range(4):
                step(nc.vector.tensor_tensor_scan(crun[:, k, :], ctot[:, k, :], zeroQ, 0.0, ALU.add, ALU.add))
            step(tt(crun, crun, ctot, ALU.subtract))
            step(tt(q.rearrange("p a b -> p (a b)"), crun.rearrange("p a b -> p (a b)"), ps[:, 3, 0:4 * QT], ALU.add))
            step(nc.vector.tensor_copy(dstq[:, :], q[:, 0, :]))
            step(ts(dstrow[:, :], q[:, 0, :], float(N - 1), None, ALU.min))
            step(tt(e0, qidx, q[:, 2, :], ALU.subtract))
            step(ts(e0, e0, float(G), None, ALU.mult))
            step(tt(e0, e0, q[:, 1, :], ALU.add))
            step(tt(left, q[:, 3, :], e0, ALU.subtract))
            ts(e0i, e0, float(E), None, ALU.min).then_inc(e0_ready, 1)
            step(tt(mask[:, :, :], bc(iota4, 1, QT), bc(left, 2, G), ALU.is_ge))
            step(ts(mask[:, :, :], mask[:, :, :], NEG, None, ALU.mult))
            step(ts(posi[0:1, 0:NC], posn[0:1, 1, :], float(QT * P - 1), None, ALU.min))
            step(ts(posi[0:1, 0:NC], posi[0:1, 0:NC], P.bit_length() - 1, None, ALU.logical_shift_right))
            step(nc.vector.tensor_copy(thr[0:1, 0:NC], posi[0:1, 0:NC]))
            step(tt(thr[0:1, 0:NC], thr[0:1, 0:NC], iota_lo[0:1, 0:NC], ALU.add))
            step(ts(crun[0:1, 0, 0:QT], qidx[0:1, :], 0.0, None, ALU.mult))
            itf = wB.rearrange("p a b c -> p (a b c)")
            step(nc.vector.memset(itf[0:1, 0:ITEMS], 0.0))
            for c in range(1, NC):
                step(nc.vector.scalar_tensor_tensor(itf[0:1, 0:ITEMS], iota_lo[0:1, 0:ITEMS], thr[0:1, c:c + 1],
                                                    itf[0:1, 0:ITEMS], ALU.is_ge, ALU.add))
            step(nc.vector.tensor_copy(items[0:1, 1, 0:ITEMS], itf[0:1, 0:ITEMS]))
            step(tt(items[0:1, 0, 0:ITEMS], iota_lo[0:1, 0:ITEMS], itf[0:1, 0:ITEMS], ALU.subtract))
            nc.vector.memset(redu[:, :, :], 0.0).then_inc(prep_done, 1)
            ve.wait_ge(win_in, 32)
            for j in range(G):
                last = nc.vector.tensor_copy(win4[0:EP, :, j], srcwin[0:EP, j:j + ET])
            last.then_inc(win4_ready, 1)

            ve.wait_ge(x_in, 32)
            norm(1)
            for c in range(NC):
                step(ts(ht[:, c, :], xt[:, c, :], mv[:, c, 0:1], rstd[:, c:c + 1], ALU.subtract, ALU.mult))
                ts(ht[:, c, :], ht[:, c, :], 0.0, None, ALU.max).then_inc(h_ready, 1)

            def tables(l):
                H = heads[l]
                ve.wait_ge(params_in[l], 48)
                step(ts(a02, a08[:, :], 0.2, None, ALU.mult))
                step(ts(a08[:, :], a08[:, :], 0.8, None, ALU.mult))
                for k in range(4):
                    step(nc.vector.memset(tbl[:, k, D:ROW], 1.0))
                for n in range(2 * NC):
                    m, k = n % 2, n % 4
                    if n >= 4:
                        ve.wait_ge(tbl_stored[k], stored_target(l, k) - 16 * (len(range(n, 2 * NC, 4))))
                    ve.wait_ge(proj_mm, 2 * NC * l + n + 1)
                    b = 4 + 2 * (n % 2)
                    for hf in range(2):
                        last = tt(tbl[:, k, hf * (D // 2):(hf + 1) * (D // 2)], ps[:, b + hf, 0:D // 2],
                                  bias[:, m, hf * (D // 2):(hf + 1) * (D // 2)], ALU.add)
                        if hf == 0:
                            step(last)
                    last.then_inc(proj_read, 1)
                    ve.wait_ge(proj_read, 2 * NC * l + n + 1)
                    step(tt(tmp[:, m, :], tbl[:, k, 0:D], a02, ALU.mult))
                    nc.vector.reduce_sum(tbl[:, k, D:D + H], tmp[:, m, :].rearrange("p (h d) -> p h d", h=H),
                                         axis=AX.X).then_inc(tbl_ready, 1)

            def logits(l, t, u, trip, cnt0, per):
                H = heads[l]
                ve.wait_ge(rows_in[l][u], (trip + 1) * (16 * (G + 1)))
                k = [0]

                def link(ins):
                    k[0] += 1
                    ins.then_inc(loop_step[l], 1)
                    ve.wait_ge(loop_step[l], t * per + k[0])
                if l == 0:
                    for hf in range(2):
                        link(tt(z[:, :, :], gring[:, u, 2 * hf:2 * hf + 2, 0:D], bc(fring[:, u, 0:D], 1, 2), ALU.add))
                        link(nc.vector.scalar_tensor_tensor(z[:, :, :], z[:, :, :], 0.0, bc(a08[:, :], 1, 2),
                                                            ALU.max, ALU.mult))
                        link(nc.vector.tensor_reduce(redu[:, 2 * hf:2 * hf + 2, :].rearrange("p g h -> p (g h)"),
                                                     z[:, :, :].rearrange("p g (h d) -> p (g h) d", h=H),
                                                     axis=AX.X, op=ALU.add))
                else:
                    for j in range(G):
                        link(tt(z[:, 0, :], gring[:, u, j, 0:D], fring[:, u, 0:D], ALU.add))
                        link(nc.vector.scalar_tensor_tensor(z[:, 0, :], z[:, 0, :], 0.0, a08[:, :],
                                                            ALU.max, ALU.mult, accum_out=redu[:, j, 0:1]))
                ve.wait_ge(lin_ready[l], t + 1)
                link(tt(lgt[:, :, 0:H], redu[:, :, 0:H], lin[:, u, :, 0:H], ALU.add))
                ve.wait_ge(prep_done, 1)
                gm = gmx(l)[:, ds(t, 1), :].rearrange("p a h -> p (a h)")
                link(nc.vector.tensor_reduce(mnow[:, 0:H], lgt[:, :, 0:H].rearrange("p g h -> p h g"),
                                             axis=AX.X, op=ALU.max))
                tt(dlt[:, u, :, 0:H], lgt[:, :, 0:H], bc(mnow[:, 0:H], 1, G), ALU.subtract)\
                    .then_inc(dlt_ready[l], 1)
                nc.vector.tensor_copy(gm, mnow[:, 0:H]).then_inc(gmax_saved[l], 1)
                assert k[0] == per

            def segments(l):
                H = heads[l]
                cb = combine_views(H)
                T = QT
                ve.wait_ge(seg_mm, 3 * l + 1)
                step(nc.vector.tensor_copy(cb["mT"][0:T, :, :].rearrange("p h n -> p (h n)"), psf[0:T, 0:H * P]))
                step(nc.vector.tensor_copy(cb["dq"][0:T, :], ps[0:T, 2, 0:P]))
                dq = cb["dq"][0:T, :]
                brk = cb["brk"]
                b3 = brk[0:T, 0:H * P].rearrange("p (h n) -> p h n", h=H)
                step(nc.vector.memset(brk[0:T, :], 1.0))
                step(tt(b3[:, :, 1:P], bc(dq[:, 1:P], 1, H), bc(dq[:, 0:P - 1], 1, H), ALU.not_equal))
                step(ts(brk[0:T, :], brk[0:T, :], NEG, None, ALU.mult))
                fl = lambda v: v[0:T, :, :].rearrange("p h n -> p (h n)")
                step(nc.vector.tensor_tensor_scan(fl(cb["fwd"]), brk[0:T, 0:H * P], fl(cb["mT"]), NEG, ALU.add, ALU.max))
                step(nc.vector.tensor_tensor_scan(fl(cb["seg"])[:, ::-1], brk[0:T, 1:H * P + 1][:, ::-1],
                                                  fl(cb["fwd"])[:, ::-1], NEG, ALU.add, ALU.max))
                for k, at in ((0, 0), (1, P - 1)):
                    step(ts(cb["outer"][0:T, k, :], dq, dq[:, at:at + 1], NEG, ALU.not_equal, ALU.mult))
                    step(nc.vector.tensor_copy(cb["edge"][0:T, k, :], cb["seg"][0:T, :, at]))
                    last = nc.vector.tensor_copy(cb["edge"][0:T, 2 + k, :], dq[:, at:at + 1].to_broadcast([T, H]))
                    if k == 0:
                        step(last)
                last.then_inc(seg_in, 1)
                ve.wait_ge(seg_mm, 3 * l + 2)
                for k in range(2):
                    step(nc.vector.tensor_copy(cb["val"][0:H, :, k], ps[0:H, 3, k * T:(k + 1) * T]))
                    step(nc.vector.tensor_copy(cb["dqe"][0:H, :, k], ps[0:H, 3, (2 + k) * T:(3 + k) * T]))
                fe = lambda v: v[0:H, :, :].rearrange("p t k -> p (t k)")
                link = cb["link"]
                step(nc.vector.memset(link[0:H, :], 1.0))
                step(tt(link[0:H, 1:2 * T], fe(cb["dqe"])[:, 1:2 * T], fe(cb["dqe"])[:, 0:2 * T - 1], ALU.not_equal))
                step(ts(link[0:H, :], link[0:H, :], NEG, None, ALU.mult))
                step(nc.vector.tensor_tensor_scan(fe(cb["sf"]), link[0:H, 0:2 * T], fe(cb["val"]), NEG, ALU.add, ALU.max))
                nc.vector.tensor_tensor_scan(fe(cb["sm"])[:, ::-1], link[0:H, 1:2 * T + 1][:, ::-1],
                                             fe(cb["sf"])[:, ::-1], NEG, ALU.add, ALU.max).then_inc(seg_in, 1)
                ve.wait_ge(seg_mm, 3 * l + 3)
                step(nc.vector.tensor_copy(cb["back"][0:T, :, :].rearrange("p k h -> p (k h)"), ps[0:T, 4, 0:2 * H]))
                for k in range(2):
                    step(tt(cb["fwd"][0:T, :, :], bc(cb["outer"][0:T, k, :], 1, H), bc(cb["back"][0:T, k, :], 2, P), ALU.add))
                    step(tt(cb["seg"][0:T, :, :], cb["seg"][0:T, :, :], cb["fwd"][0:T, :, :], ALU.max))
                tt(cb["mT"][0:T, :, :], cb["mT"][0:T, :, :], cb["seg"][0:T, :, :], ALU.subtract).then_inc(w_arg, 1)
                ve.wait_ge(w_mm, l + 1)
                nc.vector.tensor_copy(cb["w"].rearrange("p t h -> p h t"),
                                      ps[:, 5, 0:H * T].rearrange("p (h t) -> p h t", h=H)).then_inc(w_ready, 1)
                ve.wait_ge(w_ready, l + 1)

            def hot(l, i, u, first, scale_tile):
                H = heads[l]
                cb = combine_views(H)
                if scale_tile and l == 0:
                    row = vres[:, ds(i, 1), :].rearrange("p a n -> p (a n)")
                    wt = cb["w"][:, ds(i, 1), :].rearrange("p a h -> p (a h)")
                    fe = row[:, 0:D].rearrange("p (h d) -> p h d", h=H)
                    ve.wait_ge(w_ready, l + 1)
                    tt(fe, fe, bc(wt, 2, D // H), ALU.mult)
                    tt(row[:, D:ROW], row[:, D:ROW], wt, ALU.mult)
                T = ve.value_load(items[0:1, 0, ds(i, 1)], min_val=0, max_val=QT - 1)
                C = ve.value_load(items[0:1, 1, ds(i, 1)], min_val=0, max_val=NC - 1)
                if not first:
                    ve.wait_ge(item_mm[l], i - (RING - 1))
                ve.wait_ge(comb_const, 2 * l + 2)
                if l == 0:
                    last = ts(cb["hot"][:, u, :], cb["iota"][:, ds(C * P, P)], dstq[:, ds(T, 1)], None, ALU.is_equal)
                else:
                    last = ts(cb["hot"][:, u, :], cb["iota"][:, ds(C * P, P)], dstq[:, ds(T, 1)],
                              cb["w"][:, ds(T, 1), 0], ALU.is_equal, ALU.mult)
                last.then_inc(hot_ready[l], 1)

            def nodes(l):
                H = heads[l]
                ve.wait_ge(item_mm[l], ITEMS)
                dcol = psf[:, NC * D:NC * D + NC * 8].rearrange("p (c h) -> p c h", h=8)[:, :, 0:H]
                dn = den[:, :, 0:H]
                step(ts(dn, dcol, 1e-30, None, ALU.max))
                step(nc.vector.reciprocal(dn, dn))
                if l == 0:
                    ve.wait_ge(h_back, 48)
                else:
                    ve.wait_ge(x_back, 64)
                for c in range(NC):
                    pc = psf[:, c * D:(c + 1) * D].rearrange("p (h d) -> p h d", h=H)
                    step(tt(xt[:, c, :].rearrange("p (h d) -> p h d", h=H), pc, bc(dn[:, c, :], 2, D // H), ALU.mult))
                    ts(tmp[:, c % 2, :], xt[:, c, :], 0.0, None, ALU.min).then_inc(neg_ready, 1)
                    step(ts(xt[:, c, :], xt[:, c, :], 0.0, None, ALU.max))
                    ve.wait_ge(elu_exp, NC * l + c + 1)
                    step(nc.vector.scalar_tensor_tensor(xt[:, c, :], tmp[:, c % 2, :], -1.0, xt[:, c, :], ALU.add, ALU.add))
                    if l == 0:
                        step(tt(xt[:, c, :], xt[:, c, :], ht[:, c, :], ALU.add))
                norm(l + 2)
                for c in range(NC):
                    step(ts(xt[:, c, :], xt[:, c, :], mv[:, c, 0:1], rstd[:, c:c + 1], ALU.subtract, ALU.mult))
                    step(tt(xt[:, c, :], xt[:, c, :], lnw, ALU.mult))
                    if l == 0:
                        tt(ht[:, c, :], xt[:, c, :], lnb, ALU.add).then_inc(h_ready, 1)
                    else:
                        step(tt(xt[:, c, :], xt[:, c, :], lnb, ALU.add))
                        tt(xt[:, c, :], xt[:, c, :], ht[:, c, :], ALU.add).then_inc(y_ready, 1)

            for l in range(2):
                tables(l)
                per = 8 if l == 0 else 10
                for t in range(RING):
                    logits(l, t, t, 0, None, per)
                with ve.Fori(1, LOOPS) as i:
                    for u in range(RING):
                        logits(l, i * RING + u, u, i, None, per)
                for t in range(LOOPS * RING, QT):
                    logits(l, t, t % RING, t // RING, None, per)
                segments(l)
                for k in range(RING):
                    hot(l, k, k, True, True)
                with ve.Fori(1, LOOPS) as i:
                    for u in range(RING):
                        hot(l, i * RING + u, u, False, True)
                for k in range(LOOPS * RING, ITEMS):
                    hot(l, k, k % RING, False, k < QT)
                nodes(l)

        @block.tensor
        def _(te):
            mm = nc.tensor.matmul

            te.wait_ge(digits_ready, 1)
            mm(ps[:, 0, 0:NC], oh_lo[0:EP, 0, :], oh_hi[0:EP, 0, :], start=True, stop=False)
            with te.Fori(0, (ET - 2) // 2) as i:
                for k in range(2):
                    mm(ps[:, 0, 0:NC], oh_lo[0:EP, ds(i * 2 + (1 + k), 1), :].rearrange("p a n -> p (a n)"),
                       oh_hi[0:EP, ds(i * 2 + (1 + k), 1), :].rearrange("p a n -> p (a n)"), start=False, stop=False)
            mm(ps[:, 0, 0:NC], oh_lo[0:EP, ET - 1, :], oh_hi[0:EP, ET - 1, :], start=False, stop=True)
            mm(ps[:, 1, 0:1], ones[0:EP, :], nodecnt[0:EP, :], start=True, stop=True).then_inc(hist_done, 1)
            te.wait_ge(prep_in, 1)
            c2 = cnt.rearrange("p a b -> p (a b)")
            mm(ps[:, 2, 0:2 * NC], ones, c2, start=True, stop=True)
            mm(ps[:, 3, 0:2 * NC], tri_strict, c2, start=True, stop=True).then_inc(prep_mm, 1)

            te.wait_ge(flag_ready, 1)
            not_sorted = te.value_load(flag[0:1, 0:1])
            with te.If(not_sorted > 0):
                te.wait_ge(base_in, NC)
                for c in range(NC):
                    last = mm(psf[:, 2048 + c * P:2048 + (c + 1) * P], ones, rank[:, c, :], start=True, stop=True)
                last.then_inc(base_mm, 1)
                with te.Fori(0, ET) as i:
                    te.wait_ge(joint_ready, i + 1)
                    te.wait_ge(base_in, NC + 1)
                    fj = joint[0:EP, :, :].rearrange("p a b -> p (a b)")
                    for lhs, at, m in ((tri_strict[0:EP, 0:EP], 2048, EP), (ones[0:EP, :], 3072, P)):
                        mm(psf[0:m, at:at + 512], lhs, fj[:, 0:512], start=True, stop=True)
                        last = mm(psf[0:m, at + 512:at + NC * P], lhs, fj[:, 512:NC * P], start=True, stop=True)
                    last.then_inc(joint_mm, 1)
            with te.Else():
                te.wait_ge(flag_ready, 1)

            te.wait_ge(prep_in, 2)
            for c in range(NC):
                mm(ps[:, 0, 0:3 * QT], ohA[:, c, :], wB[:, c, :, :].rearrange("p a b -> p (a b)"),
                   start=(c == 0), stop=(c == NC - 1))
            for c in range(NC):
                last = mm(ps[:, 1, 0:QT], ohA[:, NC + c, :], wB2[:, c, :], start=(c == 0), stop=(c == NC - 1))
            last.then_inc(prep_mm, 1)
            te.wait_ge(prep_in, 3)
            fi = imp.rearrange("p a b -> p (a b)")
            mm(ps[:, 2, 0:4 * QT], ones, fi, start=True, stop=True)
            mm(ps[:, 3, 0:4 * QT], tri_incl, fi, start=True, stop=True).then_inc(prep_mm, 1)

            def project(l):
                for c in range(NC):
                    te.wait_ge(h_ready, NC * l + c + 1)
                    if c == 0 and l == 0:
                        te.wait_ge(prep_done, 1)
                    if c >= 2:
                        te.wait_ge(hT_ready, NC * l + c - 1)
                    for k in range(KC):
                        b = 2 * (c % 2) * 512 + k * P
                        last = nc.tensor.transpose(psf[:, b:b + P], ht[:, c, k * P:(k + 1) * P], ident[:, :])
                    last.then_inc(hT_mm, 1)
                te.wait_ge(weights_in[l], 32)
                for n in range(2 * NC):
                    c, m = n // 2, n % 2
                    te.wait_ge(hT_ready, NC * l + c + 1)
                    if n >= 2:
                        te.wait_ge(proj_read, 2 * NC * l + n - 1)
                    b = 4 + 2 * (n % 2)
                    for hf in range(2):
                        for k in range(KC):
                            last = mm(ps[:, b + hf, 0:D // 2], hT[:, k, c * P:(c + 1) * P],
                                      wts[:, m, k, hf * (D // 2):(hf + 1) * (D // 2)],
                                      start=(k == 0), stop=(k == KC - 1))
                    last.then_inc(proj_mm, 1)

            def sums(l, t, u, par, first):
                if not first:
                    te.wait_ge(sum_saved[l], t - (RING - 1))
                te.wait_ge(prod_ready[l], t + 1)
                for hf in range(2):
                    for j in range(G):
                        lhs = ident[:, :] if l == 0 else diag(par, j)
                        last = mm(ps[:, 2 * u + hf, 0:HALF], lhs, gring[:, u, j, hf * HALF:(hf + 1) * HALF],
                                  start=(j == 0), stop=(j == G - 1))
                last.then_inc(sum_mm[l], 1)

            def item(l, i, u):
                cb = combine_views(heads[l])
                T = te.value_load(items[0:1, 0, ds(i, 1)], min_val=0, max_val=QT - 1)
                C = te.value_load(items[0:1, 1, ds(i, 1)], min_val=0, max_val=NC - 1)
                te.wait_ge(hot_ready[l], i + 1)
                te.wait_ge(comb_const, 2 * l + 2)
                row = vres[:, ds(T, 1), :].rearrange("p a n -> p (a n)")
                third = D // 3
                for k in range(3):
                    mm(psf[:, ds(C * D + k * third, third)], cb["hot"][:, u, :], row[:, k * third:(k + 1) * third],
                       start=False, stop=False, skip_group_check=True)
                dn = row[:, D:ROW] if l == 0 else row[:, D + 1:D + 2]
                mm(psf[:, ds(C * 8 + NC * D, dn.shape[1])], cb["hot"][:, u, :], dn,
                   start=False, stop=False, skip_group_check=True).then_inc(item_mm[l], 1)

            for l in range(2):
                H = heads[l]
                project(l)
                if l == 0:
                    te.wait_ge(proj_read, 2 * NC * (l + 1))
                te.wait_ge(proj_read, 2 * NC * (l + 1))
                if l == 0:
                    for t in range(RING):
                        sums(l, t, t, 0, True)
                    with te.Fori(1, LOOPS) as i:
                        for u in range(RING):
                            sums(l, i * RING + u, u, 0, False)
                    for t in range(LOOPS * RING, QT):
                        sums(l, t, t % RING, 0, False)
                else:
                    SIX = 2 * RING
                    for t in range(SIX):
                        sums(l, t, t % RING, t % 2, t < RING)
                    with te.Fori(1, QT // SIX) as i:
                        for u in range(SIX):
                            sums(l, i * SIX + u, u % RING, u % 2, False)
                    for t in range(QT // SIX * SIX, QT):
                        sums(l, t, t % RING, t % 2, False)

                cb = combine_views(H)
                te.wait_ge(gmax_saved[l], QT)
                te.wait_ge(sum_saved[l], QT)
                for h in range(H):
                    nc.tensor.transpose(psf[0:QT, h * P:(h + 1) * P], gmx(l)[:, :, h], ident[:, :])
                nc.tensor.transpose(ps[0:QT, 2, 0:P], dstq[:, :], ident[:, :]).then_inc(seg_mm, 1)
                te.wait_ge(seg_in, 2 * l + 1)
                for k in range(4):
                    last = nc.tensor.transpose(ps[0:H, 3, k * QT:(k + 1) * QT], cb["edge"][0:QT, k, :], ident[0:QT, 0:QT])
                last.then_inc(seg_mm, 1)
                te.wait_ge(seg_in, 2 * l + 2)
                for k in range(2):
                    last = nc.tensor.transpose(ps[0:QT, 4, k * H:(k + 1) * H], cb["sm"][0:H, :, k], ident[0:H, 0:H])
                last.then_inc(seg_mm, 1)
                te.wait_ge(wT_ready, l + 1)
                for h in range(H):
                    last = nc.tensor.transpose(ps[:, 5, h * QT:(h + 1) * QT], cb["mT"][0:QT, h, :], ident[0:QT, 0:QT])
                last.then_inc(w_mm, 1)
                te.wait_ge(w_ready, l + 1)
                te.wait_ge(comb_const, 2 * l + 1)
                for b in range(8):
                    mm(ps[:, b, :], cb["zrow"][0:1, 0:P], cb["zrow"][0:1, :], start=True, stop=False,
                       skip_group_check=True)
                for k in range(RING):
                    item(l, k, k)
                with te.Fori(1, LOOPS) as i:
                    for u in range(RING):
                        item(l, i * RING + u, u)
                for k in range(LOOPS * RING, ITEMS):
                    item(l, k, k % RING)


_INS = ['x', 'src', 'dst', 'L0_gnn_W1s', 'L0_gnn_b1s', 'L0_gnn_W1d', 'L0_gnn_b1d', 'L0_gnn_attn1', 'L0_gnn_ln1_w',
        'L0_gnn_ln1_b', 'L0_gnn_Wos', 'L0_gnn_bos', 'L0_gnn_Wod', 'L0_gnn_bod', 'L0_gnn_attno', 'L0_gnn_lno_w',
        'L0_gnn_lno_b']


def kernel(**inputs):
    import numpy as _np
    import concourse.bacc as _bacc
    from concourse import mybir as _mybir
    from concourse.bass_utils import run_bass_kernel_spmd as _run

    nc = _bacc.Bacc("TRN2", target_bir_lowering=False, num_devices=1)
    arrays, args = {}, []
    for name in _INS:
        a = _np.ascontiguousarray(inputs[name])
        arrays[f"in_{name}_dram"] = a
        args.append(nc.dram_tensor(f"in_{name}_dram", a.shape, _mybir.dt.from_np(a.dtype), kind="ExternalInput").ap())
    out = nc.dram_tensor("out_0_dram", inputs['x'].shape, _mybir.dt.float32, kind="ExternalOutput").ap()
    gnn_kernel(nc, *args, out)
    r = _run(nc, [arrays], core_ids=[0])
    return r.results[0]["out_0_dram"]
```

```python
import concourse.bass as bass
from concourse import mybir
from contextlib import ExitStack


def gnn_kernel(nc, x, src, dst, W1s, b1s, W1d, b1d, attn1, ln1_w, ln1_b,
               Wos, bos, Wod, bod, attno, lno_w, lno_b, out):
    f32, bf16, i32 = mybir.dt.float32, mybir.dt.bfloat16, mybir.dt.int32
    ALU, ACT, AX = mybir.AluOpType, mybir.ActivationFunctionType, mybir.AxisListType
    ds = bass.ds

    P = 128
    N, D = x.shape
    E = src.shape[0]
    NC = -(-N // P)
    NLAST = N - (NC - 1) * P
    KC = D // P
    H1 = attn1.shape[0]
    G = 4
    QT = -(-((E + (G - 1) * N) // G) // P)
    ROW = D + 8
    HALF = ROW // 2
    EP = 125
    ET = E // EP
    assert EP * ET == E and N <= NC * P and QT * P * G >= E
    LO = 32
    HI = NC * P // LO
    NEG = -1.0e30
    EPS = 1e-5
    RING = 3
    LOOPS = QT // RING
    SIX = 2 * RING
    ITEMS = QT + NC - 1

    src_sorted = nc.dram_tensor("src_sorted", [E + ET, 1], i32).ap()
    src_win = nc.dram_tensor("src_win", [E + 1, G], i32).ap()
    fs_table = [nc.dram_tensor(f"fs_table{l}", [NC * P, ROW], f32).ap() for l in range(2)]
    fd_table = [nc.dram_tensor(f"fd_table{l}", [NC * P, ROW], f32).ap() for l in range(2)]
    h_saved = nc.dram_tensor("h_saved", [P, NC * D], f32).ap()

    ctx = ExitStack()
    with ctx:
        def sb(name, shape, dt=f32):
            return ctx.enter_context(nc.sbuf_tensor(name, shape, dt))

        def sem(name):
            return ctx.enter_context(nc.semaphore(name))

        vres = sb("vres", [P, QT, ROW])
        gring = sb("gring", [P, RING, G, ROW])
        fring = sb("fring", [P, RING, ROW])
        z = sb("z", [P, 2, D])
        a08 = sb("a08", [P, D])
        gmax = sb("gmax", [P, QT, H1])
        mask = sb("mask", [P, QT, G])
        srcq = sb("srcq", [P, QT, G], i32)
        dstrow = sb("dstrow", [P, QT], i32)
        dstq = sb("dstq", [P, QT])
        ident = sb("ident", [P, P])
        slotidx = sb("slotidx", [P, RING, G + 1], i32)
        redu = sb("redu", [P, G, H1])
        lgt = sb("lgt", [P, G, H1])
        lin = sb("lin", [P, RING, G, H1])
        dlt = sb("dlt", [P, RING, G, H1])
        chunkof = sb("chunkof", [P, ITEMS])
        rel = sb("rel", [P, ITEMS])
        picked = sb("picked", [P, QT])
        wsel = sb("wsel", [P, ITEMS])
        items = sb("items", [1, ITEMS + 1, 2], i32)
        flag = sb("flag", [P, 1], i32)
        turn = sb("turn", [1, 3], i32)
        dstT = sb("dstT", [QT, P])
        mnow = sb("mnow", [P, H1])

        ps = ctx.enter_context(nc.psum_tensor("ps", [P, 8, 512], f32))
        psf = ps[:, :, :].rearrange("p b n -> p (b n)")

        vflat = vres[:, :, :].rearrange("p t n -> p (t n)")
        gflat = gring[:, :, :, :].rearrange("p r g n -> p (r g n)")
        fflat = fring[:, :, :].rearrange("p r n -> p (r n)")
        zflat = z[:, :, :].rearrange("p r n -> p (r n)")

        class Carve:
            def __init__(self, flat):
                self.flat, self.at = flat, 0

            def __call__(self, shape, dt=f32):
                n = 1
                for k in shape:
                    n *= k
                words = -(-n * (2 if dt == bf16 else 4) // 4)
                v = self.flat[:, self.at:self.at + words]
                self.at += words
                assert self.at <= self.flat.shape[1]
                if dt != f32:
                    v = v.bitcast(dt)
                v = v[:, 0:n]
                if len(shape) == 2:
                    v = v.rearrange("p (a b) -> p a b", a=shape[0])
                if len(shape) == 3:
                    v = v.rearrange("p (a b c) -> p a b c", a=shape[0], b=shape[1])
                return v

        cv = Carve(vflat)
        xt = cv([NC, D])
        ht = cv([NC, D])
        hT = cv([KC, NC * P])
        tbl = cv([4, ROW])
        tmp = cv([D])
        bias = cv([2, D])
        a02 = cv([D])
        lnwb = cv([2 * D])
        lnw, lnb = lnwb[:, 0:D], lnwb[:, D:2 * D]
        stats = cv([NC, 12])
        mv = cv([NC, 2])
        rstd = cv([NC])
        shift = cv([NC])
        den = cv([NC, H1])
        ones = cv([P])
        tri_strict = cv([P])
        tri_incl = cv([P])
        expneg = cv([NC, D])
        oh_lo = cv([ET, LO], bf16)
        oh_hi = cv([ET, HI], bf16)
        spread = cv([P // LO, P])
        cnt32 = cv([HI])
        srcwin = cv([ET + G - 1], i32)
        win4 = cv([ET, G], i32)
        ch = Carve(lnwb)
        dst_e = ch([ET], i32)
        dst_n = ch([ET], i32)
        digit = ch([2, ET], i32)
        digitf = ch([2, ET])
        unsorted_e = ch([ET])
        src_e = ch([ET], i32)
        nodecnt = ch([1])
        cx = Carve(xt.rearrange("p a b -> p (a b)"))
        joint = cx([NC, P])
        base = cx([NC, P])
        rank = cx([NC, P])
        pos_f = ch([1])
        pos_i = ch([1], i32)
        src_c = ch([1], i32)
        cf = Carve(fflat)
        ohA = cf([2 * NC, P])
        ohB = cf([2 * NC, QT])
        cz = Carve(zflat)
        wB = cz([NC, 3, QT])
        wB2 = cz([NC, QT])
        cnt = cz([2, NC])
        cnt_i = cz([NC], i32)
        tot = cz([2, NC])
        run = cz([2, NC])
        first = cz([2, NC])
        posn = cz([2, NC])
        posi = cz([2 * NC], i32)
        posj = cz([2 * NC], i32)
        pdig = cz([2, 2 * NC])
        zero8 = cz([8])
        imp = cx([4, QT])
        ctot = cx([4, QT])
        crun = cx([4, QT])
        q = cx([4, QT])
        qidx = cz([QT])
        e0 = cx([QT])
        left = cx([QT])
        e0i = gmax[:, :, :].rearrange("p t h -> p (t h)")[:, 0:QT].bitcast(i32)
        iota4 = cz([G])
        zeroQ = cz([QT])
        iota_lo = cz([P])

        def combine_views(H):
            cg = Carve(gflat[:, G * ROW:])
            v = {}
            v["brk"] = cg([H * P + 1])
            v["mT"] = cg([H, P])
            v["fwd"] = cg([H, P])
            assert cg.at <= G * ROW
            v["seg"] = cg([H, P])
            v["outer"] = cg([2, P])
            v["edge"] = cg([4, H])
            v["val"] = cg([QT, 2])
            v["dqe"] = cg([QT, 2])
            v["link"] = cg([2 * QT + 1])
            v["sf"] = cg([QT, 2])
            v["sm"] = cg([QT, 2])
            v["back"] = cg([2, H])
            v["w"] = cg([QT, H])
            v["iota"] = cg([P])
            v["hot"] = cg([RING, P])
            v["zrow"] = cg([512], bf16)
            return v

        wts = gflat[:, 0:2 * KC * D].rearrange("p (m k n) -> p m k n", m=2, k=KC)

        edges_in = sem("edges_in")
        x_in = [sem(f"x_in{k}") for k in range(3)]
        pad_ready = sem("pad_ready")
        params_in = [sem(f"params_in{l}") for l in range(2)]
        attn_in = sem("attn_in")
        ln_in = sem("ln_in")
        weights_in = [[sem(f"weights_in{l}_{m}") for m in range(2)] for l in range(2)]
        consts_ready = sem("consts_ready")
        pool_step = sem("pool_step")
        dve_step = sem("dve_step")
        act_step = sem("act_step")
        digits_ready = sem("digits_ready")
        hist_done = sem("hist_done")
        prep_in = sem("prep_in")
        prep_mm = sem("prep_mm")
        flag_ready = sem("flag_ready")
        src_copied = sem("src_copied")
        base_in = sem("base_in")
        base_mm = sem("base_mm")
        joint_ready = sem("joint_ready")
        joint_mm = sem("joint_mm")
        pos_ready = sem("pos_ready")
        scattered = sem("scattered")
        turn_done = sem("turn_done")
        order_known = sem("order_known")
        win_in = sem("win_in")
        win4_ready = sem("win4_ready")
        win_stored = sem("win_stored")
        e0_ready = sem("e0_ready")
        srcq_in = sem("srcq_in")
        var_ready = sem("var_ready")
        sd_ready = sem("sd_ready")
        h_ready = [sem(f"h_ready{l}") for l in range(2)]
        norm_ready = sem("norm_ready")
        h_stored = sem("h_stored")
        hT_mm = sem("hT_mm")
        hT_ready = sem("hT_ready")
        proj_mm = sem("proj_mm")
        proj_read = sem("proj_read")
        tbl_ready = sem("tbl_ready")
        tbl_stored = [sem(f"tbl_stored{k}") for k in range(4)]
        prep_done = sem("prep_done")
        idx_ready = [sem(f"idx_ready{l}") for l in range(2)]
        rows_in_a = [[sem(f"rows_in_a{l}_{r}") for r in range(RING)] for l in range(2)]
        rows_in_b = [[sem(f"rows_in_b{l}_{r}") for r in range(RING)] for l in range(2)]
        lin_step = [sem(f"lin_step{l}") for l in range(2)]
        lin_ready = [sem(f"lin_ready{l}") for l in range(2)]
        dlt_ready = [sem(f"dlt_ready{l}") for l in range(2)]
        exp_done = [sem(f"exp_done{l}") for l in range(2)]
        prod3_ready = sem("prod3_ready")
        prod_ready = [sem(f"prod_ready{l}") for l in range(2)]
        sum_mm = [sem(f"sum_mm{l}") for l in range(2)]
        sum_saved = [sem(f"sum_saved{l}") for l in range(2)]
        seg_in = sem("seg_in")
        seg_mm = sem("seg_mm")
        z_added = sem("z_added")
        z_used = sem("z_used")
        loop_step = [sem(f"loop_step{l}") for l in range(2)]
        gmax_saved = [sem(f"gmax_saved{l}") for l in range(2)]
        w_arg = sem("w_arg")
        w_mm = sem("w_mm")
        w_ready = sem("w_ready")
        wT_ready = sem("wT_ready")
        comb_const = sem("comb_const")
        hot_ready = [sem(f"hot_ready{l}") for l in range(2)]
        item_mm = [sem(f"item_mm{l}") for l in range(2)]
        mean_ready = sem("mean_ready")
        elu_exp = sem("elu_exp")
        kept_in = sem("kept_in")
        kept_biased = sem("kept_biased")
        y_ready = sem("y_ready")
        y_stored = sem("y_stored")

        heads = (H1, 1)
        ACT_EDGES = (G - 1, G)
        PER = (12, 10)
        params = ((W1s, b1s, W1d, b1d, attn1, ln1_w, ln1_b), (Wos, bos, Wod, bod, attno, lno_w, lno_b))

        class Link:
            def __init__(self, eng, s):
                self.eng, self.s, self.n = eng, s, 0

            def __call__(self, ins):
                self.need(self.note(ins))

            def note(self, ins):
                self.n += 1
                ins.then_inc(self.s, 1)
                return self.n

            def need(self, count):
                self.eng.wait_ge(self.s, count)

        def bc(ap, axis, n):
            v = ap.unsqueeze(axis)
            shape = list(v.shape)
            shape[axis] = n
            return v.to_broadcast(shape)

        def stored_target(l, k):
            per_layer = len([n for n in range(2 * NC) if n % 4 == k])
            return 16 * per_layer * (l + 1)

        def kept(c):
            return fflat[:, c * D:(c + 1) * D] if c < RING else zflat[:, (c - RING) * D:(c - RING + 1) * D]

        def gmx(l):
            return gmax[:, :, :] if l == 0 else gmax[:, :, :].rearrange("p t h -> p (t h)")[:, 0:QT].unsqueeze(2)

        block = ctx.enter_context(nc.Block())

        @block.sync
        def _(sp):
            sp.dma_start(dst_e[0:EP, :], dst.rearrange("(p t) -> p t", t=ET)).then_inc(edges_in, 16)
            sp.wait_ge(consts_ready, 1)
            sp.dma_start(dst_n[0:EP - 1, :], dst[1:1 + (EP - 1) * ET].rearrange("(p t) -> p t", t=ET))\
                .then_inc(edges_in, 16)
            sp.dma_start(dst_n[EP - 1:EP, 0:ET - 1], dst[1 + (EP - 1) * ET:E].rearrange("(a t) -> a t", a=1))\
                .then_inc(edges_in, 16)
            sp.dma_start(src_e[0:EP, :], src.rearrange("(p t) -> p t", t=ET)).then_inc(edges_in, 16)
            sp.dma_start(xt[:, 0, :], x[0:P, :]).then_inc(x_in[0], 16)

            def load_biases(l):
                for to, of in ((bias[:, 0, :], params[l][1]), (bias[:, 1, :], params[l][3])):
                    sp.dma_start(to, of.partition_broadcast(P)).then_inc(params_in[l], 16)

            def load_attention(l):
                sp.dma_start(a08[:, :], params[l][4].rearrange("h d -> (h d)").partition_broadcast(P))\
                    .then_inc(attn_in, 16)

            def load_weights(l, which=(0, 1)):
                for m in which:
                    sp.dma_start(wts[:, m, :, :], params[l][2 * m].rearrange("(k p) n -> p k n", p=P))\
                        .then_inc(weights_in[l][m], 16)

            load_weights(0, (0,))
            sp.dma_start(xt[:, 1:NC - 1, :], x[P:(NC - 1) * P, :].rearrange("(c p) d -> p c d", p=P))\
                .then_inc(x_in[1], 16)
            sp.wait_ge(pad_ready, 1)
            sp.dma_start(xt[0:NLAST, NC - 1, :], x[(NC - 1) * P:N, :]).then_inc(x_in[2], 16)
            load_biases(0)
            load_attention(0)
            load_weights(0, (1,))
            sp.wait_ge(edges_in, 64)
            sp.dma_start(src_sorted[0:E, :].rearrange("(p t) a -> p (t a)", t=ET), src_e[0:EP, :])\
                .then_inc(src_copied, 16)
            sp.dma_start(src_sorted[E:E + ET, :].rearrange("(a t) o -> a (t o)", a=1), srcwin[0:1, 0:ET])\
                .then_inc(src_copied, 16)
            sp.wait_ge(order_known, 1)
            sp.dma_start(srcwin[0:EP, 0:ET], src_sorted[0:E, :].rearrange("(p t) a -> p (t a)", t=ET))\
                .then_inc(win_in, 16)
            sp.dma_start(srcwin[0:EP, ET:ET + G - 1],
                         src_sorted[ET:E + ET, :].rearrange("(p t) a -> p (t a)", t=ET)[:, 0:G - 1])\
                .then_inc(win_in, 16)
            sp.wait_ge(win4_ready, 1)
            sp.dma_start(src_win[0:E, :].rearrange("(p t) g -> p (t g)", t=ET),
                         win4[0:EP, :, :].rearrange("p t g -> p (t g)")).then_inc(win_stored, 16)
            sp.dma_start(src_win[E:E + 1, :], srcwin[EP:EP + 1, 0:G]).then_inc(win_stored, 16)
            sp.wait_ge(h_ready[0], NC)
            sp.dma_start(h_saved, ht[:, :, :].rearrange("p c d -> p (c d)")).then_inc(h_stored, 16)

            for l in range(2):
                for n in range(2 * NC):
                    c, m = n // 2, n % 2
                    to = (fs_table, fd_table)[m][l]
                    sp.wait_ge(tbl_ready, 2 * NC * l + n + 1)
                    sp.dma_start(to[c * P:(c + 1) * P, :], tbl[:, n % 4, :]).then_inc(tbl_stored[n % 4], 16)
                sp.wait_ge(dlt_ready[l], QT)
                if l == 0:
                    load_attention(1)
                    sp.wait_ge(h_stored, 16)
                    sp.dma_start(fflat[:, 0:RING * D], h_saved[:, 0:RING * D]).then_inc(kept_in, 16)
                    sp.dma_start(zflat[:, 0:(NC - RING) * D], h_saved[:, RING * D:NC * D]).then_inc(kept_in, 16)
                else:
                    sp.dma_start(fflat[:, 0:RING * D].rearrange("p (c d) -> p c d", c=RING),
                                 x[0:RING * P, :].rearrange("(c p) d -> p c d", p=P)).then_inc(kept_in, 16)
                    for c in range(RING, NC):
                        k = P if c < NC - 1 else NLAST
                        sp.dma_start(kept(c)[0:k, :], x[c * P:c * P + k, :]).then_inc(kept_in, 16)
                sp.wait_ge(item_mm[l], ITEMS)
                sp.dma_start(lnw, params[l][5].partition_broadcast(P)).then_inc(ln_in, 16)
                sp.dma_start(lnb, params[l][6].partition_broadcast(P)).then_inc(ln_in, 16)
                if l == 0:
                    load_weights(1)
                    load_biases(1)
            for c in range(NC):
                k = P if c < NC - 1 else NLAST
                sp.wait_ge(y_ready, c + 1)
                sp.dma_start(out[c * P:c * P + k, :], xt[0:k, c, :]).then_inc(y_stored, 16)
            sp.wait_ge(y_stored, 16 * NC)

        @block.gpsimd
        def _(po):
            step = Link(po, pool_step)

            def take_wait(k=0):
                return nc.gpsimd.tensor_tensor(turn[:, k + 1:k + 2], turn[:, 0:1], turn[:, 0:1], ALU.add)

            step(nc.gpsimd.memset(turn[:, :], 0))
            step(nc.gpsimd.memset(dst_n[96:P, :], 1 << 20))
            nc.gpsimd.memset(srcwin[:, :], 0).then_inc(consts_ready, 1)
            step(nc.gpsimd.memset(ident[:, :], 0.0))
            step(nc.gpsimd.affine_select(out=ident[:, :], in_=ident[:, :], compare_op=ALU.not_equal, fill=1.0,
                                         base=0, pattern=[[-1, P]], channel_multiplier=1))
            step(nc.gpsimd.memset(spread[0:LO, :, :], 0.0))
            for r in range(P // LO):
                nc.gpsimd.affine_select(out=spread[0:LO, r, :], in_=spread[0:LO, r, :], compare_op=ALU.not_equal,
                                        fill=1.0, base=r * LO, pattern=[[-1, P]], channel_multiplier=1)
            step(nc.gpsimd.memset(ones, 1.0))
            for tri, op in ((tri_strict, ALU.is_gt), (tri_incl, ALU.is_ge)):
                step(nc.gpsimd.affine_select(out=tri, in_=ones, compare_op=op, fill=0.0,
                                             base=0, pattern=[[1, P]], channel_multiplier=-1))
            nc.gpsimd.iota(iota_lo, pattern=[[1, P]], base=0, channel_multiplier=0,
                           allow_small_or_imprecise_dtypes=True)
            nc.gpsimd.iota(iota4, pattern=[[1, G]], base=0, channel_multiplier=0,
                           allow_small_or_imprecise_dtypes=True)
            step(nc.gpsimd.iota(qidx, pattern=[[P, QT]], base=0, channel_multiplier=1,
                                allow_small_or_imprecise_dtypes=True))
            nc.gpsimd.memset(zeroQ, 0.0).then_inc(consts_ready, 1)

            po.wait_ge(src_copied, 32)
            po.wait_ge(flag_ready, 1)
            not_sorted = po.value_load(flag[0:1, 0:1])
            with po.If(not_sorted > 0):
                with po.Fori(0, ET) as i:
                    po.wait_ge(pos_ready, i + 1)
                    take_wait().then_inc(turn_done, 1)
                    po.indirect_dma_start(src_sorted, bass.IndirectOffsetOnAxis(ap=pos_i[0:EP, :], axis=0),
                                          src_c[0:EP, :], None).then_inc(scattered, 16)
                    po.wait_ge(turn_done, i + 1)
                po.wait_ge(scattered, 16 * ET)
                po.sem_inc(order_known, 1)
            with po.Else():
                po.sem_inc(order_known, 1)

            po.wait_ge(win_stored, 32)
            po.wait_ge(e0_ready, 1)
            for t in range(QT):
                po.indirect_dma_start(srcq[:, t, :], None, src_win,
                                      bass.IndirectOffsetOnAxis(ap=e0i[:, t:t + 1], axis=0)).then_inc(srcq_in, 16)
            po.wait_ge(srcq_in, 16 * QT)

            def first_gathers(l):
                assert G * ROW <= KC * D
                for t in range(RING):
                    nc.gpsimd.tensor_copy(slotidx[:, t, 0:G], srcq[:, t, :]).then_inc(idx_ready[l], 1)
                    nc.gpsimd.tensor_copy(slotidx[:, t, G:G + 1], dstrow[:, t:t + 1]).then_inc(idx_ready[l], 1)
                for k in (0, 2):
                    po.wait_ge(tbl_stored[k], stored_target(l, k))
                po.wait_ge(idx_ready[l], 2 * RING)
                take_wait()

                def sources(t):
                    for j in range(G):
                        po.indirect_dma_start(gring[:, t, j, :], None, fs_table[l],
                                              bass.IndirectOffsetOnAxis(ap=slotidx[:, t, j:j + 1], axis=0))\
                            .then_inc((rows_in_a, rows_in_b)[j // 2][l][t], 16)

                def destinations(t):
                    po.indirect_dma_start(fring[:, t, :], None, fd_table[l],
                                          bass.IndirectOffsetOnAxis(ap=slotidx[:, t, G:G + 1], axis=0))\
                        .then_inc(rows_in_a[l][t], 16)

                sources(0)
                for k in (1, 3):
                    po.wait_ge(tbl_stored[k], stored_target(l, k))
                take_wait(1)
                destinations(0)
                destinations(1)
                sources(1)
                linear(l, 0, 0, 0)
                destinations(2)
                sources(2)

            def gathers(l, t, u, trip):
                nc.gpsimd.tensor_copy(slotidx[:, u, 0:G],
                                      srcq[:, ds(t, 1), :].rearrange("p a g -> p (a g)"))\
                    .then_inc(idx_ready[l], 1)
                nc.gpsimd.tensor_copy(slotidx[:, u, G:G + 1], dstrow[:, ds(t, 1)]).then_inc(idx_ready[l], 1)
                po.wait_ge(idx_ready[l], t * 2 + 2)
                po.wait_ge(sum_mm[l], (t - RING) * G + 2)
                take_wait()
                po.indirect_dma_start(fring[:, u, :], None, fd_table[l],
                                      bass.IndirectOffsetOnAxis(ap=slotidx[:, u, G:G + 1], axis=0))\
                    .then_inc(rows_in_a[l][u], 16)
                for j in range(G):
                    if j == 2:
                        po.wait_ge(sum_mm[l], (t - RING + 1) * G)
                        take_wait(1)
                    po.indirect_dma_start(gring[:, u, j, :], None, fs_table[l],
                                          bass.IndirectOffsetOnAxis(ap=slotidx[:, u, j:j + 1], axis=0))\
                        .then_inc((rows_in_a, rows_in_b)[j // 2][l][u], 16)

            def linear(l, t, u, trip):
                H = heads[l]
                po.wait_ge(rows_in_a[l][u], (trip + 1) * 48)
                po.wait_ge(rows_in_b[l][u], (trip + 1) * 32)
                nc.gpsimd.tensor_tensor(lin[:, u, :, 0:H], gring[:, u, :, D:D + H],
                                        bc(fring[:, u, D:D + H], 1, G), ALU.add).then_inc(lin_step[l], 1)
                po.wait_ge(lin_step[l], t + 1)
                po.wait_ge(prep_done, 1)
                mk = mask[:, ds(t, 1), :].rearrange("p a g -> p (a g)")
                nc.gpsimd.tensor_tensor(lin[:, u, :, 0:H], lin[:, u, :, 0:H],
                                        bc(mk, 2, H), ALU.add).then_inc(lin_ready[l], 1)

            def weigh3(t, u):
                po.wait_ge(exp_done[0], t + 1)
                row = gring[:, u, G - 1, 0:D].rearrange("p (h d) -> p h d", h=H1)
                nc.gpsimd.tensor_tensor(row, row, bc(gring[:, u, G - 1, D:D + H1], 2, D // H1), ALU.mult)\
                    .then_inc(prod3_ready, 1)

            for l in range(2):
                first_gathers(l)
                if l == 0:
                    weigh3(0, 0)
                linear(l, 1, 1, 0)
                with po.Fori(1, LOOPS) as i:
                    for u in range(RING):
                        gathers(l, i * RING + u, u, i)
                        if l == 0:
                            weigh3(i * RING + (u - 2), (u - 2) % RING)
                        prev = (u - 1) % RING
                        linear(l, i * RING + (u - 1), prev, i if u else i - 1)
                for t in range(LOOPS * RING, QT):
                    gathers(l, t, t % RING, t // RING)
                    if l == 0:
                        weigh3(t - 2, (t - 2) % RING)
                    linear(l, t - 1, (t - 1) % RING, (t - 1) // RING)
                linear(l, QT - 1, (QT - 1) % RING, (QT - 1) // RING)
                if l == 0:
                    weigh3(QT - 2, (QT - 2) % RING)
                    weigh3(QT - 1, (QT - 1) % RING)

                cb = combine_views(heads[l])
                po.wait_ge(sum_mm[l], (QT - 1) * G)
                nc.gpsimd.memset(cb["zrow"][0:1, :], 0.0).then_inc(comb_const, 1)
                nc.gpsimd.iota(cb["iota"], pattern=[[1, P]], base=0, channel_multiplier=0,
                               allow_small_or_imprecise_dtypes=True).then_inc(comb_const, 1)
            po.wait_ge(ln_in, 64)
            po.wait_ge(kept_in, 32 + 16 * (1 + NC - RING))
            for c in range(NC):
                nc.gpsimd.tensor_tensor(kept(c), kept(c), lnb, ALU.add).then_inc(kept_biased, 1)

        @block.scalar
        def _(act):
            step = Link(act, act_step)

            def sqrt_var(n, of):
                act.wait_ge(var_ready, n)
                nc.scalar.activation(of, of, ACT.Sqrt).then_inc(sd_ready, 1)

            def copy_hT(l, c):
                act.wait_ge(hT_mm, NC * l + c + 1)
                b = 2 * (c % 2)
                nc.scalar.activation(hT[:, :, c * P:(c + 1) * P],
                                     psf[:, b * 512:b * 512 + D].rearrange("p (k n) -> p k n", k=KC),
                                     ACT.Copy).then_inc(hT_ready, 1)

            def weigh(l, t, u):
                H = heads[l]
                act.wait_ge(dlt_ready[l], t + 1)
                if l == 0:
                    nc.scalar.activation(gring[:, u, :, D:D + H], dlt[:, u, :, 0:H], ACT.Exp).then_inc(exp_done[l], 1)
                    act.wait_ge(exp_done[l], t + 1)
                    for j in range(ACT_EDGES[l]):
                        for h in range(H):
                            part = gring[:, u, j, h * (D // H):(h + 1) * (D // H)]
                            last = nc.scalar.activation(part, part, ACT.Copy,
                                                        scale=gring[:, u, j, D + h:D + h + 1])
                        last.then_inc(prod_ready[l], 1)
                else:
                    nc.scalar.activation(dlt[:, u, :, 0:1], dlt[:, u, :, 0:1], ACT.Exp).then_inc(exp_done[l], 1)
                    act.wait_ge(exp_done[l], t + 1)
                    for j in range(G):
                        nc.scalar.activation(gring[:, u, j, :], gring[:, u, j, :], ACT.Copy,
                                             scale=dlt[:, u, j, 0:1]).then_inc(prod_ready[l], 1)

            def save(l, t, u):
                act.wait_ge(sum_mm[l], (t + 1) * G)
                b = 2 * u
                row = vres[:, ds(t, 1), :].rearrange("p a n -> p (a n)")
                nc.scalar.activation(row[:, 0:HALF], ps[:, b, 0:HALF], ACT.Copy)
                nc.scalar.activation(row[:, HALF:ROW], ps[:, b + 1, 0:HALF], ACT.Copy).then_inc(sum_saved[l], 1)

            def h_of(c):
                act.wait_ge(norm_ready, c + 1)
                nc.scalar.activation(ht[:, c, :], xt[:, c, :], ACT.Relu, bias=shift[:, c:c + 1],
                                     scale=rstd[:, c:c + 1]).then_inc(h_ready[0], 1)

            sqrt_var(1, rstd[:, 0:1])
            h_of(0)
            copy_hT(0, 0)
            for c in range(1, NC):
                sqrt_var(c + 1, rstd[:, c:c + 1])
                if c > 1:
                    h_of(c - 1)
            h_of(NC - 1)
            for c in range(1, NC):
                copy_hT(0, c)
            for l in range(2):
                for k in range(4):
                    act.wait_ge(tbl_stored[k], stored_target(l, k))
                weigh(l, 0, 0)
                for t in range(1, RING):
                    weigh(l, t, t)
                    save(l, t - 1, t - 1)
                with act.Fori(1, LOOPS) as i:
                    for u in range(RING):
                        weigh(l, i * RING + u, u)
                        save(l, i * RING + (u - 1), (u - 1) % RING)
                for t in range(LOOPS * RING, QT):
                    weigh(l, t, t % RING)
                    save(l, t - 1, (t - 1) % RING)
                save(l, QT - 1, (QT - 1) % RING)
                cb = combine_views(heads[l])
                act.wait_ge(w_arg, l + 1)
                nc.scalar.activation(cb["mT"][0:QT, :, :], cb["mT"][0:QT, :, :], ACT.Exp).then_inc(wT_ready, 1)
                for c in range(NC):
                    act.wait_ge(mean_ready, NC * l + c + 1)
                    step(nc.scalar.activation(expneg[:, c, :], xt[:, c, :], ACT.Relu, scale=-1.0))
                    nc.scalar.activation(expneg[:, c, :], expneg[:, c, :], ACT.Exp, scale=-1.0).then_inc(elu_exp, 1)
                for c in range(NC):
                    sqrt_var(NC * (l + 1) + c + 1, rstd[:, c:c + 1])
                    if l == 0 and c:
                        copy_hT(1, c - 1)
                if l == 0:
                    copy_hT(1, NC - 1)

        @block.vector
        def _(ve):
            step = Link(ve, dve_step)
            tt, ts = nc.vector.tensor_tensor, nc.vector.tensor_scalar

            def pick(to, of, less):
                part = picked[:, :]
                step(nc.vector.memset(to[:, :], 0.0))
                for c in range(NC):
                    step(ts(part, chunkof[:, c:c + QT], float(c), None, ALU.is_equal))
                    if less:
                        step(nc.vector.scalar_tensor_tensor(part, of, -less * c, part, ALU.add, ALU.mult))
                    else:
                        step(tt(part, of, part, ALU.mult))
                    step(tt(to[:, c:c + QT], to[:, c:c + QT], part, ALU.add))

            def var_of(c):
                for k in range(2):
                    got = step.note(nc.vector.bn_stats(stats[:, c, 6 * k:6 * k + 6],
                                                       xt[:, c, k * (D // 2):(k + 1) * (D // 2)]))
                return got

            def deviation(c):
                ve.wait_ge(x_in[0 if c == 0 else 2 if c == NC - 1 else 1], 16)
                step.need(var_of(c))
                step(nc.vector.bn_aggr(mv[:, c, :], stats[:, c, :]))
                ts(rstd[:, c:c + 1], mv[:, c, 1:2], EPS, None, ALU.add).then_inc(var_ready, 1)

            def normalizer(c):
                ve.wait_ge(sd_ready, c + 1)
                step(nc.vector.reciprocal(rstd[:, c:c + 1], rstd[:, c:c + 1]))
                nc.vector.scalar_tensor_tensor(shift[:, c:c + 1], mv[:, c, 0:1], -1.0, rstd[:, c:c + 1],
                                               ALU.mult, ALU.mult).then_inc(norm_ready, 1)

            nc.vector.memset(xt[96:P, NC - 1, :], 0.0).then_inc(pad_ready, 1)
            step(nc.vector.memset(zero8, 0.0))
            def table_consts(l):
                ve.wait_ge(attn_in, 16 * (l + 1))
                step(ts(a02, a08[:, :], 0.2, None, ALU.mult))
                step(ts(a08[:, :], a08[:, :], 0.8, None, ALU.mult))
                for k in range(4):
                    step(nc.vector.memset(tbl[:, k, D:ROW], 1.0))

            def table(l, n):
                H = heads[l]
                m, k = n % 2, n % 4
                ve.wait_ge(params_in[l], 32)
                if n >= 4:
                    ve.wait_ge(tbl_stored[k], stored_target(l, k) - 16 * (len(range(n, 2 * NC, 4))))
                ve.wait_ge(proj_mm, 2 * NC * l + n + 1)
                b = 4 + 2 * (n % 2)
                for hf in range(2):
                    last = tt(tbl[:, k, hf * (D // 2):(hf + 1) * (D // 2)], ps[:, b + hf, 0:D // 2],
                              bias[:, m, hf * (D // 2):(hf + 1) * (D // 2)], ALU.add)
                    if hf == 0:
                        step.note(last)
                last.then_inc(proj_read, 1)
                ve.wait_ge(proj_read, 2 * NC * l + n + 1)
                step(tt(tmp, tbl[:, k, 0:D], a02, ALU.mult))
                nc.vector.reduce_sum(tbl[:, k, D:D + H], tmp.rearrange("p (h d) -> p h d", h=H),
                                     axis=AX.X).then_inc(tbl_ready, 1)
                ve.wait_ge(tbl_ready, 2 * NC * l + n + 1)

            ve.wait_ge(edges_in, 64)
            ve.wait_ge(consts_ready, 2)

            step(tt(unsorted_e[0:EP, :], dst_e[0:EP, :], dst_n[0:EP, :], ALU.is_gt))
            step(nc.vector.reduce_sum(nodecnt[0:EP, :], unsorted_e[0:EP, :], axis=AX.X))
            step(ts(digit[0:EP, 0, :], dst_e[0:EP, :], LO - 1, None, ALU.bitwise_and))
            step(ts(digit[0:EP, 1, :], dst_e[0:EP, :], LO.bit_length() - 1, None, ALU.logical_shift_right))
            step(nc.vector.tensor_copy(digitf[0:EP, :, :], digit[0:EP, :, :]))
            deviation(0)

            tt(oh_hi[0:EP, :, :], bc(iota_lo[0:EP, 0:HI], 1, ET), bc(digitf[0:EP, 1, :], 2, HI),
               ALU.is_equal).then_inc(digits_ready, 1)
            normalizer(0)
            tt(oh_lo[0:EP, :, :], bc(iota_lo[0:EP, 0:LO], 1, ET), bc(digitf[0:EP, 0, :], 2, LO),
               ALU.is_equal).then_inc(digits_ready, 1)
            for c in range(1, NC):
                deviation(c)
                if c > 1:
                    normalizer(c - 1)
            normalizer(NC - 1)
            table_consts(0)
            table(0, 0)

            ve.wait_ge(hist_done, 1)
            nc.vector.tensor_copy(flag[0:1, :], ps[0:1, 1, 0:1]).then_inc(flag_ready, 1)
            nc.vector.tensor_copy(cnt32[0:LO, :], ps[0:LO, 0, 0:HI]).then_inc(prep_in, 1)
            ve.wait_ge(hist_done, 2)
            step(nc.vector.tensor_copy(cnt[:, 0, :], ps[:, 2, 0:NC]))
            step(ts(cnt_i, cnt[:, 0, :], float(G - 1), None, ALU.add))
            step(ts(cnt_i, cnt_i, G.bit_length() - 1, None, ALU.logical_shift_right))
            nc.vector.tensor_copy(cnt[:, 1, :], cnt_i).then_inc(prep_in, 1)
            ve.wait_ge(prep_mm, 1)
            step(nc.vector.tensor_copy(tot.rearrange("p a b -> p (a b)"), ps[:, 1, 0:2 * NC]))
            for k in range(2):
                step(nc.vector.tensor_tensor_scan(run[:, k, :], tot[:, k, :], zero8[:, 0:NC], 0.0, ALU.add, ALU.add))
            step(tt(run, run, tot, ALU.subtract))
            step(tt(first.rearrange("p a b -> p (a b)"), run.rearrange("p a b -> p (a b)"),
                    ps[:, 3, 0:2 * NC], ALU.add))
            step(tt(posn[:, 0, :], first[:, 1, :], cnt[:, 1, :], ALU.add))
            step(nc.vector.tensor_copy(posn[:, 1, :], first[:, 1, :]))

            ve.wait_ge(h_ready[0], NC)
            ve.wait_ge(flag_ready, 1)
            not_sorted = ve.value_load(flag[0:1, 0:1])
            with ve.If(not_sorted > 0):
                for c in range(NC):
                    ts(rank[:, c, :], ident[:, :], first[:, 0, c:c + 1], None, ALU.mult).then_inc(base_in, 1)
                ve.wait_ge(base_mm, 1)
                nc.vector.tensor_copy(base.rearrange("p a b -> p (a b)"), psf[:, 0:NC * P])\
                    .then_inc(base_in, 1)
                with ve.Fori(0, ET) as i:
                    ve.wait_ge(base_in, NC + 1 + i * 7)
                    ve.wait_ge(base_in, NC + 1)
                    jd = joint[0:EP, :, :].rearrange("p a b -> p (a b)").rearrange("p (a b) -> p a b", a=HI)
                    tt(jd, oh_lo[0:EP, ds(i, 1), :].to_broadcast([EP, HI, LO]),
                       bc(oh_hi[0:EP, ds(i, 1), :].rearrange("p a c -> p (a c)"), 2, LO), ALU.mult).then_inc(joint_ready, 1)
                    ve.wait_ge(joint_mm, i + 1)
                    flat = lambda v: v[0:EP, :, :].rearrange("p a b -> p (a b)")
                    tt(flat(rank), psf[0:EP, 0:NC * P], flat(base), ALU.add).then_inc(base_in, 1)
                    ve.wait_ge(base_in, NC + 2 + i * 7)
                    tt(flat(rank), flat(rank), flat(joint), ALU.mult).then_inc(base_in, 1)
                    ve.wait_ge(base_in, NC + 3 + i * 7)
                    nc.vector.reduce_sum(pos_f[0:EP, :], flat(rank), axis=AX.X).then_inc(base_in, 1)
                    ve.wait_ge(base_in, NC + 4 + i * 7)
                    nc.vector.tensor_copy(pos_i[0:EP, :], pos_f[0:EP, :]).then_inc(base_in, 1)
                    ve.wait_ge(base_in, NC + 5 + i * 7)
                    nc.vector.tensor_copy(src_c[0:EP, :], src_e[0:EP, ds(i, 1)]).then_inc(base_in, 1)
                    ve.wait_ge(base_in, NC + 6 + i * 7)
                    tt(base.rearrange("p a b -> p (a b)"), base.rearrange("p a b -> p (a b)"),
                       psf[:, 1024:1024 + NC * P], ALU.add).then_inc(base_in, 1)
                    ve.wait_ge(base_in, NC + 7 + i * 7)
                    nc.vector.memset(rank[:, 0, 0:1], 0.0).then_inc(base_in, 1)
                    ve.sem_inc(pos_ready, 1)
                    ve.wait_ge(scattered, i * 16 + 16)
            with ve.Else():
                ve.wait_ge(flag_ready, 1)

            step(nc.vector.tensor_copy(posi, posn.rearrange("p a b -> p (a b)")))
            step(ts(posj, posi, P - 1, None, ALU.bitwise_and))
            step(nc.vector.tensor_copy(pdig[:, 0, :], posj))
            step(ts(posi, posi, P.bit_length() - 1, None, ALU.logical_shift_right))
            step(nc.vector.tensor_copy(pdig[:, 1, :], posi))
            step(tt(ohA, bc(iota_lo, 1, 2 * NC), bc(pdig[:, 0, :], 2, P), ALU.is_equal))
            step(tt(ohB, bc(iota_lo[:, 0:QT], 1, 2 * NC), bc(pdig[:, 1, :], 2, QT), ALU.is_equal))
            step(nc.vector.tensor_copy(wB[:, :, 0, :], ohB[:, 0:NC, :]))
            step(tt(wB[:, :, 1, :], ohB[:, 0:NC, :], bc(cnt[:, 0, :], 2, QT), ALU.mult))
            step(tt(wB[:, :, 2, :], ohB[:, 0:NC, :], bc(cnt[:, 1, :], 2, QT), ALU.mult))
            tt(wB2, ohB[:, NC:2 * NC, :], bc(cnt[:, 0, :], 2, QT), ALU.mult).then_inc(prep_in, 1)
            ve.wait_ge(win_in, 32)
            for j in range(G):
                last = nc.vector.tensor_copy(win4[0:EP, :, j], srcwin[0:EP, j:j + ET])
            last.then_inc(win4_ready, 1)
            ve.wait_ge(prep_mm, 2)
            step(nc.vector.tensor_copy(imp[:, 0:3, :].rearrange("p a b -> p (a b)"), ps[:, 0, 0:3 * QT]))
            nc.vector.tensor_copy(imp[:, 3, :], ps[:, 1, 0:QT]).then_inc(prep_in, 1)
            ve.wait_ge(prep_mm, 3)
            step(nc.vector.tensor_copy(ctot.rearrange("p a b -> p (a b)"), ps[:, 2, 0:4 * QT]))
            for k in range(4):
                step(nc.vector.tensor_tensor_scan(crun[:, k, :], ctot[:, k, :], zeroQ, 0.0, ALU.add, ALU.add))
            step(tt(crun, crun, ctot, ALU.subtract))
            step(tt(q.rearrange("p a b -> p (a b)"), crun.rearrange("p a b -> p (a b)"), ps[:, 3, 0:4 * QT], ALU.add))
            step(nc.vector.tensor_copy(dstq[:, :], q[:, 0, :]))
            step(ts(dstrow[:, :], q[:, 0, :], float(N - 1), None, ALU.min))
            step(tt(e0, qidx, q[:, 2, :], ALU.subtract))
            step(ts(e0, e0, float(G), None, ALU.mult))
            step(tt(e0, e0, q[:, 1, :], ALU.add))
            step(tt(left, q[:, 3, :], e0, ALU.subtract))
            ts(e0i, e0, float(E), None, ALU.min).then_inc(e0_ready, 1)
            table(0, 1)
            step(tt(mask[:, :, :], bc(iota4, 1, QT), bc(left, 2, G), ALU.is_ge))
            step(ts(mask[:, :, :], mask[:, :, :], NEG, None, ALU.mult))
            step(ts(posi[:, 0:NC], run[:, 1, :], float(QT * P - 1), None, ALU.min))
            step(ts(posi[:, 0:NC], posi[:, 0:NC], P.bit_length() - 1, None, ALU.logical_shift_right))
            step(nc.vector.tensor_copy(pdig[:, 0, 0:NC], posi[:, 0:NC]))
            step(tt(pdig[:, 0, 0:NC], pdig[:, 0, 0:NC], iota_lo[:, 0:NC], ALU.add))
            step(ts(chunkof[:, :], iota_lo[:, 0:ITEMS], pdig[:, 0, 1:2], None, ALU.is_ge))
            for c in range(2, NC):
                step(nc.vector.scalar_tensor_tensor(chunkof[:, :], iota_lo[:, 0:ITEMS], pdig[:, 0, c:c + 1],
                                                    chunkof[:, :], ALU.is_ge, ALU.add))
            step(nc.vector.tensor_copy(items[0:1, 0:ITEMS, 1], chunkof[0:1, :]))
            step(tt(items[0:1, 0:ITEMS, 0], iota_lo[0:1, 0:ITEMS], chunkof[0:1, :], ALU.subtract))
            pick(rel, dstq[:, :], float(P))
            nc.vector.memset(redu[:, :, :], 0.0).then_inc(prep_done, 1)
            def logits(l, t, u, trip, first=False):
                H = heads[l]
                per = PER[l]
                base = t * per - (0 if first else 2)
                k = [0]

                def mark(ins):
                    k[0] += 1
                    ins.then_inc(loop_step[l], 1)
                    return k[0]

                def need(count):
                    ve.wait_ge(loop_step[l], base + count)

                def add(j):
                    return mark(tt(z[:, j % 2, :], gring[:, u, j, 0:D], fring[:, u, 0:D], ALU.add))

                def weigh(j):
                    kw = dict(accum_out=redu[:, j, 0:1]) if l else {}
                    if j < G - 1 or l:
                        return mark(nc.vector.scalar_tensor_tensor(z[:, j % 2, :], z[:, j % 2, :], 0.0, a08[:, :],
                                                                   ALU.max, ALU.mult, **kw))
                    halves = lambda v: v.rearrange("p (h n) -> p h n", h=2)
                    ve.wait_ge(z_added, t + 1)
                    nc.vector.scalar_tensor_tensor(halves(z[:, j % 2, :]), ps[:, 6:8, 0:D // 2], 0.0, halves(a08[:, :]),
                                                   ALU.max, ALU.mult, **kw).then_inc(z_used, 1)

                def total(j):
                    return mark(nc.vector.tensor_reduce(redu[:, j, :], z[:, j % 2, :].rearrange("p (h d) -> p h d", h=H),
                                                        axis=AX.X, op=ALU.add))

                ago = not first
                tl, ul = t - 1, (u - 1) % RING

                def logit():
                    ve.wait_ge(lin_ready[l], tl + 1)
                    return mark(tt(lgt[:, :, 0:H], redu[:, :, 0:H], lin[:, ul, :, 0:H], ALU.add))

                def largest():
                    return mark(nc.vector.tensor_reduce(mnow[:, 0:H], lgt[:, :, 0:H].rearrange("p g h -> p h g"),
                                                        axis=AX.X, op=ALU.max))

                ve.wait_ge(rows_in_a[l][u], (trip + 1) * 48)
                if ago:
                    need(0)
                a1 = add(1)
                if ago:
                    n_logit = logit()
                a0 = add(0)
                if ago:
                    need(n_logit)
                    n_max = largest()
                need(a1)
                b1 = weigh(1)
                if ago:
                    need(n_max)
                    finish(l, tl, ul)
                need(a0)
                b0 = weigh(0)
                if l == 0:
                    need(b1)
                    c1 = total(1)
                    need(b0)
                    c0 = total(0)
                    ve.wait_ge(rows_in_b[l][u], (trip + 1) * 32)
                    need(c0)
                    a2 = add(2)
                    weigh(3)
                    need(a2)
                    b2 = weigh(2)
                    ve.wait_ge(z_used, t + 1)
                    total(3)
                    need(b2)
                    total(2)
                else:
                    ve.wait_ge(rows_in_b[l][u], (trip + 1) * 32)
                    need(b1)
                    a3 = add(3)
                    need(b0)
                    a2 = add(2)
                    need(a3)
                    weigh(3)
                    need(a2)
                    weigh(2)
                assert k[0] == per - (2 if first else 0)

            def finish(l, t, u):
                H = heads[l]
                tt(dlt[:, u, :, 0:H], lgt[:, :, 0:H], bc(mnow[:, 0:H], 1, G), ALU.subtract).then_inc(dlt_ready[l], 1)
                nc.vector.tensor_copy(gmx(l)[:, ds(t, 1), :].rearrange("p a h -> p (a h)"), mnow[:, 0:H])\
                    .then_inc(gmax_saved[l], 1)

            def segments(l):
                H = heads[l]
                cb = combine_views(H)
                T = QT
                dq = dstT[0:T, :]
                brk = cb["brk"]
                b3 = brk[0:T, 0:H * P].rearrange("p (h n) -> p h n", h=H)
                ve.wait_ge(seg_mm, 4 * l + 1)
                step(nc.vector.tensor_copy(dq, ps[0:T, 2, 0:P]))
                ve.wait_ge(sum_mm[l], (QT - 2) * G)
                step(nc.vector.memset(brk[0:T, :], 1.0))
                step(tt(b3[:, :, 1:P], bc(dq[:, 1:P], 1, H), bc(dq[:, 0:P - 1], 1, H), ALU.not_equal))
                step(ts(brk[0:T, :], brk[0:T, :], NEG, None, ALU.mult))
                ve.wait_ge(seg_mm, 4 * l + 2)
                step(nc.vector.tensor_copy(cb["mT"][0:T, :, :].rearrange("p h n -> p (h n)"), psf[0:T, 3072:3072 + H * P]))
                fl = lambda v: v[0:T, :, :].rearrange("p h n -> p (h n)")
                step(nc.vector.tensor_tensor_scan(fl(cb["fwd"]), brk[0:T, 0:H * P], fl(cb["mT"]), NEG, ALU.add, ALU.max))
                ve.wait_ge(sum_mm[l], (QT - 1) * G)
                step(nc.vector.tensor_tensor_scan(fl(cb["seg"])[:, ::-1], brk[0:T, 1:H * P + 1][:, ::-1],
                                                  fl(cb["fwd"])[:, ::-1], NEG, ALU.add, ALU.max))
                for k, at in ((0, 0), (1, P - 1)):
                    step(ts(cb["outer"][0:T, k, :], dq, dq[:, at:at + 1], NEG, ALU.not_equal, ALU.mult))
                    step(nc.vector.tensor_copy(cb["edge"][0:T, k, :], cb["seg"][0:T, :, at]))
                    last = nc.vector.tensor_copy(cb["edge"][0:T, 2 + k, :], dq[:, at:at + 1].to_broadcast([T, H]))
                    if k == 0:
                        step(last)
                last.then_inc(seg_in, 1)
                ve.wait_ge(seg_mm, 4 * l + 3)
                for k in range(2):
                    step(nc.vector.tensor_copy(cb["val"][0:H, :, k], ps[0:H, 5, k * T:(k + 1) * T]))
                    step(nc.vector.tensor_copy(cb["dqe"][0:H, :, k], ps[0:H, 5, (2 + k) * T:(3 + k) * T]))
                fe = lambda v: v[0:H, :, :].rearrange("p t k -> p (t k)")
                link = cb["link"]
                step(nc.vector.memset(link[0:H, :], 1.0))
                step(tt(link[0:H, 1:2 * T], fe(cb["dqe"])[:, 1:2 * T], fe(cb["dqe"])[:, 0:2 * T - 1], ALU.not_equal))
                step(ts(link[0:H, :], link[0:H, :], NEG, None, ALU.mult))
                step(nc.vector.tensor_tensor_scan(fe(cb["sf"]), link[0:H, 0:2 * T], fe(cb["val"]), NEG, ALU.add, ALU.max))
                nc.vector.tensor_tensor_scan(fe(cb["sm"])[:, ::-1], link[0:H, 1:2 * T + 1][:, ::-1],
                                             fe(cb["sf"])[:, ::-1], NEG, ALU.add, ALU.max).then_inc(seg_in, 1)
                ve.wait_ge(seg_mm, 4 * l + 4)
                step(nc.vector.tensor_copy(cb["back"][0:T, :, :].rearrange("p k h -> p (k h)"), ps[0:T, 5, 0:2 * H]))
                for k in range(2):
                    step(tt(cb["fwd"][0:T, :, :], bc(cb["outer"][0:T, k, :], 1, H), bc(cb["back"][0:T, k, :], 2, P), ALU.add))
                    step(tt(cb["seg"][0:T, :, :], cb["seg"][0:T, :, :], cb["fwd"][0:T, :, :], ALU.max))
                tt(cb["mT"][0:T, :, :], cb["mT"][0:T, :, :], cb["seg"][0:T, :, :], ALU.subtract).then_inc(w_arg, 1)
                ve.wait_ge(w_mm, l + 1)
                nc.vector.tensor_copy(cb["w"].rearrange("p t h -> p h t"),
                                      ps[:, 5, P:P + H * T].rearrange("p (h t) -> p h t", h=H)).then_inc(w_ready, 1)
                ve.wait_ge(w_ready, l + 1)
                if l:
                    pick(wsel, cb["w"].rearrange("p t h -> p (t h)"), 0.0)

            def hot(l, i, u, first, scale_tile):
                H = heads[l]
                cb = combine_views(H)
                if scale_tile and l == 0:
                    row = vres[:, ds(i, 1), :].rearrange("p a n -> p (a n)")
                    wt = cb["w"][:, ds(i, 1), :].rearrange("p a h -> p (a h)")
                    fe = row[:, 0:D].rearrange("p (h d) -> p h d", h=H)
                    ve.wait_ge(w_ready, l + 1)
                    tt(fe, fe, bc(wt, 2, D // H), ALU.mult)
                    tt(row[:, D:ROW], row[:, D:ROW], wt, ALU.mult)
                if not first:
                    ve.wait_ge(item_mm[l], i - (RING - 1))
                ve.wait_ge(comb_const, 2 * l + 2)
                if l == 0:
                    last = ts(cb["hot"][:, u, :], cb["iota"], rel[:, ds(i, 1)], None, ALU.is_equal)
                else:
                    last = ts(cb["hot"][:, u, :], cb["iota"], rel[:, ds(i, 1)], wsel[:, ds(i, 1)],
                              ALU.is_equal, ALU.mult)
                last.then_inc(hot_ready[l], 1)

            def nodes(l):
                H = heads[l]
                ve.wait_ge(item_mm[l], ITEMS)
                dcol = psf[:, NC * D:NC * D + NC * 8].rearrange("p (c h) -> p c h", h=8)[:, :, 0:H]
                dn = den[:, :, 0:H]
                step(ts(dn, dcol, 1e-30, None, ALU.max))
                step(nc.vector.reciprocal(dn, dn))
                for c in range(NC):
                    pc = psf[:, c * D:(c + 1) * D].rearrange("p (h d) -> p h d", h=H)
                    tt(xt[:, c, :].rearrange("p (h d) -> p h d", h=H), pc, bc(dn[:, c, :], 2, D // H), ALU.mult)\
                        .then_inc(mean_ready, 1)
                ve.wait_ge(kept_in, (32, 32 + 16 * (1 + NC - RING))[l])
                for c in range(NC + 1):
                    b = c - 1
                    if c < NC:
                        v = xt[:, c, :]
                        ve.wait_ge(mean_ready, NC * l + c + 1)
                        ve.wait_ge(elu_exp, NC * l + c + 1)
                        now = step.note(nc.vector.scalar_tensor_tensor(v, v, 0.0, expneg[:, c, :], ALU.max, ALU.add))
                    if c:
                        w = xt[:, b, :]
                        ve.wait_ge(sd_ready, NC * (l + 1) + b + 1)
                        ago = step.note(nc.vector.reciprocal(rstd[:, b:c], rstd[:, b:c]))
                    if c < NC:
                        step.need(now)
                        if l == 0:
                            now = step.note(nc.vector.scalar_tensor_tensor(v, v, -1.0, kept(c), ALU.add, ALU.add))
                        else:
                            now = step.note(ts(v, v, -1.0, None, ALU.add))
                    if c:
                        step.need(ago)
                        ago = step.note(ts(w, w, mv[:, b, 0:1], rstd[:, b:c], ALU.subtract, ALU.mult))
                    if c < NC:
                        step.need(now)
                        now = var_of(c)
                    if c:
                        ve.wait_ge(ln_in, 32 * (l + 1))
                        step.need(ago)
                        ago = step.note(tt(w, w, lnw, ALU.mult))
                    if c < NC:
                        step.need(now)
                        now = step.note(nc.vector.bn_aggr(mv[:, c, :], stats[:, c, :]))
                    if c:
                        step.need(ago)
                        if l == 0:
                            tt(ht[:, b, :], w, lnb, ALU.add).then_inc(h_ready[1], 1)
                        else:
                            ve.wait_ge(kept_biased, b + 1)
                            tt(w, w, kept(b), ALU.add).then_inc(y_ready, 1)
                    if c < NC:
                        step.need(now)
                        ts(rstd[:, c:c + 1], mv[:, c, 1:2], EPS, None, ALU.add).then_inc(var_ready, 1)
                    if l == 0 and c >= NC - 2 and c < NC:
                        if c == NC - 2:
                            table_consts(1)
                        table(1, c - (NC - 2))

            for l in range(2):
                for n in range(2, 2 * NC):
                    table(l, n)
                for t in range(RING):
                    logits(l, t, t, 0, t == 0)
                with ve.Fori(1, LOOPS) as i:
                    for u in range(RING):
                        logits(l, i * RING + u, u, i)
                for t in range(LOOPS * RING, QT):
                    logits(l, t, t % RING, t // RING)
                H, u, n = heads[l], (QT - 1) % RING, QT * PER[l] - 2
                ve.wait_ge(loop_step[l], n)
                ve.wait_ge(lin_ready[l], QT)
                tt(lgt[:, :, 0:H], redu[:, :, 0:H], lin[:, u, :, 0:H], ALU.add).then_inc(loop_step[l], 1)
                ve.wait_ge(loop_step[l], n + 1)
                nc.vector.tensor_reduce(mnow[:, 0:H], lgt[:, :, 0:H].rearrange("p g h -> p h g"),
                                        axis=AX.X, op=ALU.max).then_inc(loop_step[l], 1)
                ve.wait_ge(loop_step[l], n + 2)
                finish(l, QT - 1, u)
                segments(l)
                for k in range(RING):
                    hot(l, k, k, True, True)
                with ve.Fori(1, LOOPS) as i:
                    for u in range(RING):
                        hot(l, i * RING + u, u, False, True)
                for k in range(LOOPS * RING, ITEMS):
                    hot(l, k, k % RING, False, k < QT)
                nodes(l)

        @block.tensor
        def _(te):
            mm = nc.tensor.matmul

            def transposes(l, c):
                te.wait_ge(h_ready[l], c + 1)
                if c >= 2:
                    te.wait_ge(hT_ready, NC * l + c - 1)
                for k in range(KC):
                    b = 2 * (c % 2) * 512 + k * P
                    last = nc.tensor.transpose(psf[:, b:b + P], ht[:, c, k * P:(k + 1) * P], ident[:, :])
                last.then_inc(hT_mm, 1)

            def project(l, n):
                c, m = n // 2, n % 2
                te.wait_ge(weights_in[l][m], 16)
                te.wait_ge(hT_ready, NC * l + c + 1)
                if n >= 2:
                    te.wait_ge(proj_read, 2 * NC * l + n - 1)
                b = 4 + 2 * (n % 2)
                for hf in range(2):
                    for k in range(KC):
                        last = mm(ps[:, b + hf, 0:D // 2], hT[:, k, c * P:(c + 1) * P],
                                  wts[:, m, k, hf * (D // 2):(hf + 1) * (D // 2)],
                                  start=(k == 0), stop=(k == KC - 1))
                last.then_inc(proj_mm, 1)

            te.wait_ge(consts_ready, 2)
            transposes(0, 0)
            project(0, 0)
            transposes(0, 1)
            te.wait_ge(hT_ready, 2)

            te.wait_ge(digits_ready, 2)
            for k in range(ET):
                mm(ps[0:LO, 0, 0:HI], oh_lo[0:EP, k, :], oh_hi[0:EP, k, :], start=(k == 0), stop=(k == ET - 1))
            mm(ps[:, 1, 0:1], ones[0:EP, :], nodecnt[0:EP, :], start=True, stop=True).then_inc(hist_done, 1)
            te.wait_ge(prep_in, 1)
            for r in range(P // LO):
                last = mm(ps[:, 2, 0:NC], spread[0:LO, r, :], cnt32[0:LO, r::P // LO],
                          start=(r == 0), stop=(r == P // LO - 1))
            last.then_inc(hist_done, 1)
            te.wait_ge(prep_in, 2)
            c2 = cnt.rearrange("p a b -> p (a b)")
            mm(ps[:, 1, 0:2 * NC], ones, c2, start=True, stop=True)
            mm(ps[:, 3, 0:2 * NC], tri_strict, c2, start=True, stop=True).then_inc(prep_mm, 1)

            te.wait_ge(flag_ready, 1)
            not_sorted = te.value_load(flag[0:1, 0:1])
            with te.If(not_sorted > 0):
                te.wait_ge(base_in, NC)
                for c in range(NC):
                    last = mm(psf[:, c * P:(c + 1) * P], ones, rank[:, c, :], start=True, stop=True)
                last.then_inc(base_mm, 1)
                with te.Fori(0, ET) as i:
                    te.wait_ge(joint_ready, i + 1)
                    te.wait_ge(base_in, NC + 1)
                    fj = joint[0:EP, :, :].rearrange("p a b -> p (a b)")
                    for lhs, at, m in ((tri_strict[0:EP, 0:EP], 0, EP), (ones[0:EP, :], 1024, P)):
                        mm(psf[0:m, at:at + 512], lhs, fj[:, 0:512], start=True, stop=True)
                        last = mm(psf[0:m, at + 512:at + NC * P], lhs, fj[:, 512:NC * P], start=True, stop=True)
                    last.then_inc(joint_mm, 1)
            with te.Else():
                te.wait_ge(flag_ready, 1)

            project(0, 1)
            te.wait_ge(prep_in, 3)
            for c in range(NC):
                mm(ps[:, 0, 0:3 * QT], ohA[:, c, :], wB[:, c, :, :].rearrange("p a b -> p (a b)"),
                   start=(c == 0), stop=(c == NC - 1))
            for c in range(NC):
                last = mm(ps[:, 1, 0:QT], ohA[:, NC + c, :], wB2[:, c, :], start=(c == 0), stop=(c == NC - 1))
            last.then_inc(prep_mm, 1)
            te.wait_ge(prep_in, 4)
            fi = imp.rearrange("p a b -> p (a b)")
            mm(ps[:, 2, 0:4 * QT], ones, fi, start=True, stop=True)
            mm(ps[:, 3, 0:4 * QT], tri_incl, fi, start=True, stop=True).then_inc(prep_mm, 1)
            project(0, 2)
            te.wait_ge(e0_ready, 1)
            transposes(0, 2)

            def add_rows(l, t, u, trip, first):
                if l:
                    return
                te.wait_ge(rows_in_a[l][u], (trip + 1) * 48)
                te.wait_ge(rows_in_b[l][u], (trip + 1) * 32)
                if not first:
                    te.wait_ge(z_used, t)
                for hf in range(2):
                    at = slice(hf * (D // 2), (hf + 1) * (D // 2))
                    mm(ps[:, 6 + hf, 0:D // 2], ident[:, :], gring[:, u, G - 1, at], start=True, stop=False)
                    last = mm(ps[:, 6 + hf, 0:D // 2], ident[:, :], fring[:, u, at], start=False, stop=True)
                last.then_inc(z_added, 1)

            def sums(l, t, u, first):
                if not first:
                    te.wait_ge(sum_saved[l], t - (RING - 1))
                for j in range(G):
                    if j < ACT_EDGES[l]:
                        te.wait_ge(prod_ready[l], t * ACT_EDGES[l] + (j + 1))
                    else:
                        te.wait_ge(prod3_ready, t + 1)
                    for hf in range(2):
                        last = mm(ps[:, 2 * u + hf, 0:HALF], ident[:, :], gring[:, u, j, hf * HALF:(hf + 1) * HALF],
                                  start=(j == 0), stop=(j == G - 1), skip_group_check=True)
                    last.then_inc(sum_mm[l], 1)

            def item_trip(l, i0, n):
                why = "the items are made on the chip within these bounds"
                _, where = nc.values_load_multi_w_load_instructions(
                    items[0:1, ds(i0, n), :].rearrange("p i k -> p (i k)"), engines=(mybir.EngineType.PE,),
                    min_val=0, max_val=QT - 1, skip_runtime_bounds_check_because=why)
                for u in range(n):
                    C = nc.s_assert_within(where[2 * u + 1], 0, NC - 1, skip_runtime_bounds_check_because=why)
                    item(l, i0 + u, u % RING, where[2 * u], C)

            def item(l, i, u, T, C):
                cb = combine_views(heads[l])
                te.wait_ge(hot_ready[l], i + 1)
                te.wait_ge(comb_const, 2 * l + 2)
                row = vres[:, ds(T, 1), :].rearrange("p a n -> p (a n)")
                third = D // 3
                for k in range(3):
                    mm(psf[:, ds(C * D + k * third, third)], cb["hot"][:, u, :], row[:, k * third:(k + 1) * third],
                       start=False, stop=False, skip_group_check=True)
                dn = row[:, D:ROW] if l == 0 else row[:, D + 1:D + 2]
                mm(psf[:, ds(C * 8 + NC * D, dn.shape[1])], cb["hot"][:, u, :], dn,
                   start=False, stop=False, skip_group_check=True).then_inc(item_mm[l], 1)

            for l in range(2):
                H = heads[l]
                if l:
                    transposes(l, 0)
                for n in range((3, 0)[l], 2 * NC):
                    project(l, n)
                    if n % 2 == 0 and n // 2 + 1 < NC:
                        transposes(l, n // 2 + 1)
                te.wait_ge(proj_read, 2 * NC * (l + 1))
                assert QT % RING
                add_rows(l, 0, 0, 0, True)
                for t in range(RING):
                    add_rows(l, t + 1, (t + 1) % RING, (t + 1) // RING, False)
                    sums(l, t, t, True)
                with te.Fori(1, LOOPS) as i:
                    for u in range(RING):
                        add_rows(l, i * RING + (u + 1), (u + 1) % RING, i + (u + 1) // RING, False)
                        sums(l, i * RING + u, u, False)
                cb = combine_views(H)
                assert QT == LOOPS * RING + 1
                te.wait_ge(sum_saved[l], QT - 2)
                nc.tensor.transpose(ps[0:QT, 2, 0:P], dstq[:, :], ident[:, :]).then_inc(seg_mm, 1)
                te.wait_ge(gmax_saved[l], QT)
                if l == 0:
                    te.wait_ge(z_used, QT)
                for h in range(H):
                    last = nc.tensor.transpose(psf[0:QT, 3072 + h * P:3072 + (h + 1) * P], gmx(l)[:, :, h], ident[:, :])
                last.then_inc(seg_mm, 1)
                sums(l, QT - 1, 0, False)
                te.wait_ge(sum_saved[l], QT)
                te.wait_ge(seg_in, 2 * l + 1)
                for k in range(4):
                    last = nc.tensor.transpose(ps[0:H, 5, k * QT:(k + 1) * QT], cb["edge"][0:QT, k, :], ident[0:QT, 0:QT])
                last.then_inc(seg_mm, 1)
                te.wait_ge(seg_in, 2 * l + 2)
                for k in range(2):
                    last = nc.tensor.transpose(ps[0:QT, 5, k * H:(k + 1) * H], cb["sm"][0:H, :, k], ident[0:H, 0:H])
                last.then_inc(seg_mm, 1)
                te.wait_ge(comb_const, 2 * l + 1)

                def clear(b):
                    mm(ps[:, b, :], cb["zrow"][0:1, 0:P], cb["zrow"][0:1, :], start=True, stop=False,
                       skip_group_check=True)

                for b in (0, 1, 2, 3, 4, 6, 7):
                    clear(b)
                te.wait_ge(wT_ready, l + 1)
                for h in range(H):
                    last = nc.tensor.transpose(ps[:, 5, P + h * QT:P + (h + 1) * QT], cb["mT"][0:QT, h, :], ident[0:QT, 0:QT])
                last.then_inc(w_mm, 1)
                te.wait_ge(w_ready, l + 1)
                clear(5)
                item_trip(l, 0, SIX)
                with te.Fori(1, ITEMS // SIX) as i:
                    item_trip(l, i * SIX, SIX)
                item_trip(l, ITEMS // SIX * SIX, ITEMS % SIX)


_INS = ['x', 'src', 'dst', 'L0_gnn_W1s', 'L0_gnn_b1s', 'L0_gnn_W1d', 'L0_gnn_b1d', 'L0_gnn_attn1', 'L0_gnn_ln1_w',
        'L0_gnn_ln1_b', 'L0_gnn_Wos', 'L0_gnn_bos', 'L0_gnn_Wod', 'L0_gnn_bod', 'L0_gnn_attno', 'L0_gnn_lno_w',
        'L0_gnn_lno_b']


def kernel(**inputs):
    import numpy as _np
    import concourse.bacc as _bacc
    from concourse import mybir as _mybir
    from concourse.bass_utils import run_bass_kernel_spmd as _run

    nc = _bacc.Bacc("TRN2", target_bir_lowering=False, num_devices=1)
    arrays, args = {}, []
    for name in _INS:
        a = _np.ascontiguousarray(inputs[name])
        arrays[f"in_{name}_dram"] = a
        args.append(nc.dram_tensor(f"in_{name}_dram", a.shape, _mybir.dt.from_np(a.dtype), kind="ExternalInput").ap())
    out = nc.dram_tensor("out_0_dram", inputs['x'].shape, _mybir.dt.float32, kind="ExternalOutput").ap()
    gnn_kernel(nc, *args, out)
    r = _run(nc, [arrays], core_ids=[0])
    return r.results[0]["out_0_dram"]
```

```python
import concourse.bass as bass
from concourse import mybir
from contextlib import ExitStack


def gnn_kernel(nc, x, src, dst, W1s, b1s, W1d, b1d, attn1, ln1_w, ln1_b,
               Wos, bos, Wod, bod, attno, lno_w, lno_b, out):
    f32, bf16, i32 = mybir.dt.float32, mybir.dt.bfloat16, mybir.dt.int32
    ALU, ACT, AX = mybir.AluOpType, mybir.ActivationFunctionType, mybir.AxisListType
    ds = bass.ds

    P = 128
    N, D = x.shape
    E = src.shape[0]
    NC = -(-N // P)
    NLAST = N - (NC - 1) * P
    KC = D // P
    H1 = attn1.shape[0]
    G = 4
    QT = -(-((E + (G - 1) * N) // G) // P)
    ROW = D + 8
    HALF = ROW // 2
    EP = 125
    ET = E // EP
    assert EP * ET == E and N <= NC * P and QT * P * G >= E
    LO = 32
    HI = NC * P // LO
    NEG = -1.0e30
    EPS = 1e-5
    RING = 3
    LOOPS = QT // RING
    SIX = 2 * RING
    ITEMS = QT + NC - 1

    src_sorted = nc.dram_tensor("src_sorted", [E + ET, 1], i32).ap()
    src_win = nc.dram_tensor("src_win", [E + 1, G], i32).ap()
    fs_table = [nc.dram_tensor(f"fs_table{l}", [NC * P, ROW], f32).ap() for l in range(2)]
    fd_table = [nc.dram_tensor(f"fd_table{l}", [NC * P, ROW], f32).ap() for l in range(2)]
    h_saved = nc.dram_tensor("h_saved", [P, NC * D], f32).ap()

    ctx = ExitStack()
    with ctx:
        def sb(name, shape, dt=f32):
            return ctx.enter_context(nc.sbuf_tensor(name, shape, dt))

        def sem(name):
            return ctx.enter_context(nc.semaphore(name))

        vres = sb("vres", [P, QT, ROW])
        gring = sb("gring", [P, RING, G, ROW])
        fring = sb("fring", [P, RING, ROW])
        z = sb("z", [P, 2, D])
        a08 = sb("a08", [P, D])
        gmax = sb("gmax", [P, QT, H1])
        mask = sb("mask", [P, QT, G])
        srcq = sb("srcq", [P, QT, G], i32)
        dstrow = sb("dstrow", [P, QT], i32)
        dstq = sb("dstq", [P, QT])
        ident = sb("ident", [P, P])
        slotidx = sb("slotidx", [P, RING, G + 1], i32)
        redu = sb("redu", [P, G, H1])
        lgt = sb("lgt", [P, G, H1])
        lin = sb("lin", [P, RING, G, H1])
        dlt = sb("dlt", [P, RING, G, H1])
        chunkof = sb("chunkof", [P, ITEMS])
        rel = sb("rel", [P, ITEMS])
        picked = sb("picked", [P, QT])
        wsel = sb("wsel", [P, ITEMS])
        items = sb("items", [1, ITEMS + 1, 2], i32)
        flag = sb("flag", [P, 1], i32)
        turn = sb("turn", [1, 4], i32)
        dstT = sb("dstT", [QT, P])

        ps = ctx.enter_context(nc.psum_tensor("ps", [P, 8, 512], f32))
        psf = ps[:, :, :].rearrange("p b n -> p (b n)")

        vflat = vres[:, :, :].rearrange("p t n -> p (t n)")
        gflat = gring[:, :, :, :].rearrange("p r g n -> p (r g n)")
        fflat = fring[:, :, :].rearrange("p r n -> p (r n)")
        zflat = z[:, :, :].rearrange("p r n -> p (r n)")

        class Carve:
            def __init__(self, flat):
                self.flat, self.at = flat, 0

            def __call__(self, shape, dt=f32):
                n = 1
                for k in shape:
                    n *= k
                words = -(-n * (2 if dt == bf16 else 4) // 4)
                v = self.flat[:, self.at:self.at + words]
                self.at += words
                assert self.at <= self.flat.shape[1]
                if dt != f32:
                    v = v.bitcast(dt)
                v = v[:, 0:n]
                if len(shape) == 2:
                    v = v.rearrange("p (a b) -> p a b", a=shape[0])
                if len(shape) == 3:
                    v = v.rearrange("p (a b c) -> p a b c", a=shape[0], b=shape[1])
                return v

        cv = Carve(vflat)
        xt = cv([NC, D])
        ht = cv([NC, D])
        hT = cv([KC, NC * P])
        tbl = cv([4, ROW])
        tmp = cv([D])
        bias = cv([2, D])
        a02 = cv([D])
        lnwb = cv([2 * D])
        lnw, lnb = lnwb[:, 0:D], lnwb[:, D:2 * D]
        stats = cv([NC, 12])
        mv = cv([NC, 2])
        rstd = cv([NC])
        shift = cv([NC])
        den = cv([NC, H1])
        ones = cv([P])
        tri_strict = cv([P])
        tri_incl = cv([P])
        expneg = cv([NC, D])
        oh_lo = cv([ET, LO], bf16)
        oh_hi = cv([ET, HI], bf16)
        spread = cv([P // LO, P])
        cnt32 = cv([HI])
        srcwin = cv([ET + G - 1], i32)
        win4 = cv([ET, G], i32)
        ch = Carve(lnwb)
        dst_e = ch([ET], i32)
        dst_n = ch([ET], i32)
        digit = ch([2, ET], i32)
        digitf = ch([2, ET])
        unsorted_e = ch([ET])
        src_e = ch([ET], i32)
        nodecnt = ch([1])
        cx = Carve(xt.rearrange("p a b -> p (a b)"))
        joint = cx([NC, P])
        base = cx([NC, P])
        rank = cx([NC, P])
        pos_f = ch([1])
        pos_i = ch([1], i32)
        src_c = ch([1], i32)
        cf = Carve(fflat)
        ohA = cf([2 * NC, P])
        ohB = cf([2 * NC, QT])
        cz = Carve(zflat)
        wB = cz([NC, 3, QT])
        wB2 = cz([NC, QT])
        cnt = cz([2, NC])
        cnt_i = cz([NC], i32)
        tot = cz([2, NC])
        run = cz([2, NC])
        first = cz([2, NC])
        posn = cz([2, NC])
        posi = cz([2 * NC], i32)
        posj = cz([2 * NC], i32)
        pdig = cz([2, 2 * NC])
        zero8 = cz([8])
        imp = cx([4, QT])
        ctot = cx([4, QT])
        crun = cx([4, QT])
        q = cx([4, QT])
        qidx = cz([QT])
        e0 = cx([QT])
        left = cx([QT])
        e0i = gmax[:, :, :].rearrange("p t h -> p (t h)")[:, 0:QT].bitcast(i32)
        iota4 = cz([G])
        zeroQ = cz([QT])
        iota_lo = cz([P])

        def combine_views(H):
            cg = Carve(gflat[:, G * ROW:2 * G * ROW])
            v = {}
            v["brk"] = cg([H * P + 1])
            v["fwd"] = cg([H, P])
            v["outer"] = cg([2, P])
            v["change"] = cg([P + 1])
            v["edgeq"] = cg([2, H])
            v["edge"] = cg([2, H])
            v["dqe"] = cg([QT, 2])
            v["link"] = cg([2 * QT + 1])
            v["val"] = cg([QT, 2])
            v["sf"] = cg([QT, 2])
            v["sm"] = cg([QT, 2])
            v["back"] = cg([2, H])
            v["iota"] = cg([P])
            cg = Carve(gflat[:, 2 * G * ROW:])
            v["mT"] = cg([H, P])
            v["seg"] = cg([H, P])
            v["w"] = cg([QT, H])
            v["hot"] = cg([RING, P])
            v["zrow"] = cg([512], bf16)
            return v

        wts = gflat[:, 0:2 * KC * D].rearrange("p (m k n) -> p m k n", m=2, k=KC)

        edges_in = sem("edges_in")
        x_in = [sem(f"x_in{k}") for k in range(3)]
        pad_ready = sem("pad_ready")
        params_in = [sem(f"params_in{l}") for l in range(2)]
        attn_in = sem("attn_in")
        ln_in = sem("ln_in")
        weights_in = [[sem(f"weights_in{l}_{m}") for m in range(2)] for l in range(2)]
        consts_ready = sem("consts_ready")
        pool_step = sem("pool_step")
        dve_step = sem("dve_step")
        act_step = sem("act_step")
        digits_ready = sem("digits_ready")
        hist_done = sem("hist_done")
        prep_in = sem("prep_in")
        prep_mm = sem("prep_mm")
        flag_ready = sem("flag_ready")
        src_copied = sem("src_copied")
        base_in = sem("base_in")
        base_mm = sem("base_mm")
        joint_ready = sem("joint_ready")
        joint_mm = sem("joint_mm")
        pos_ready = sem("pos_ready")
        scattered = sem("scattered")
        turn_done = sem("turn_done")
        order_known = sem("order_known")
        win_in = sem("win_in")
        win4_ready = sem("win4_ready")
        win_stored = sem("win_stored")
        e0_ready = sem("e0_ready")
        dst_mm = sem("dst_mm")
        srcq_in = sem("srcq_in")
        var_ready = sem("var_ready")
        sd_ready = sem("sd_ready")
        h_ready = [sem(f"h_ready{l}") for l in range(2)]
        norm_ready = sem("norm_ready")
        h_stored = sem("h_stored")
        hT_mm = sem("hT_mm")
        hT_ready = sem("hT_ready")
        proj_mm = sem("proj_mm")
        proj_read = sem("proj_read")
        tbl_ready = sem("tbl_ready")
        tbl_stored = [sem(f"tbl_stored{k}") for k in range(4)]
        prep_done = sem("prep_done")
        idx_ready = [sem(f"idx_ready{l}") for l in range(2)]
        rows_in_a = [[sem(f"rows_in_a{l}_{r}") for r in range(RING)] for l in range(2)]
        rows_in_b = [[sem(f"rows_in_b{l}_{r}") for r in range(RING)] for l in range(2)]
        lin_step = [sem(f"lin_step{l}") for l in range(2)]
        lin_ready = [sem(f"lin_ready{l}") for l in range(2)]
        dlt_ready = [sem(f"dlt_ready{l}") for l in range(2)]
        exp_done = [sem(f"exp_done{l}") for l in range(2)]
        prod3_ready = sem("prod3_ready")
        prod_ready = [sem(f"prod_ready{l}") for l in range(2)]
        sum_mm = [sem(f"sum_mm{l}") for l in range(2)]
        sum_saved = [sem(f"sum_saved{l}") for l in range(2)]
        seg_in = sem("seg_in")
        seg_mm = sem("seg_mm")
        z_ready = sem("z_ready")
        folded = sem("folded")
        loop_step = [sem(f"loop_step{l}") for l in range(2)]
        w_arg = sem("w_arg")
        w_mm = sem("w_mm")
        w_ready = sem("w_ready")
        wT_ready = sem("wT_ready")
        comb_const = sem("comb_const")
        hot_ready = [sem(f"hot_ready{l}") for l in range(2)]
        item_mm = [sem(f"item_mm{l}") for l in range(2)]
        mean_ready = sem("mean_ready")
        elu_exp = sem("elu_exp")
        kept_in = sem("kept_in")
        kept_biased = sem("kept_biased")
        shift_ready = sem("shift_ready")
        normed = sem("normed")
        scaled = sem("scaled")
        y_ready = sem("y_ready")
        y_stored = sem("y_stored")

        heads = (H1, 1)
        ACT_EDGES = (G - 1, G)
        PER = (12, 10)
        LATE = (3, 2)
        FOLD = 6
        params = ((W1s, b1s, W1d, b1d, attn1, ln1_w, ln1_b), (Wos, bos, Wod, bod, attno, lno_w, lno_b))

        class Link:
            def __init__(self, eng, s):
                self.eng, self.s, self.n = eng, s, 0

            def __call__(self, ins):
                self.need(self.note(ins))

            def note(self, ins):
                self.n += 1
                ins.then_inc(self.s, 1)
                return self.n

            def need(self, count):
                self.eng.wait_ge(self.s, count)

        def bc(ap, axis, n):
            v = ap.unsqueeze(axis)
            shape = list(v.shape)
            shape[axis] = n
            return v.to_broadcast(shape)

        def stored_target(l, k):
            per_layer = len([n for n in range(2 * NC) if n % 4 == k])
            return 16 * per_layer * (l + 1)

        def kept(c):
            return fflat[:, c * D:(c + 1) * D] if c < RING else zflat[:, (c - RING) * D:(c - RING + 1) * D]

        def gmx(l):
            return gmax[:, :, :] if l == 0 else gmax[:, :, :].rearrange("p t h -> p (t h)")[:, 0:QT].unsqueeze(2)

        block = ctx.enter_context(nc.Block())

        @block.sync
        def _(sp):
            sp.dma_start(dst_e[0:EP, :], dst.rearrange("(p t) -> p t", t=ET)).then_inc(edges_in, 16)
            sp.wait_ge(consts_ready, 1)
            sp.dma_start(dst_n[0:EP - 1, :], dst[1:1 + (EP - 1) * ET].rearrange("(p t) -> p t", t=ET))\
                .then_inc(edges_in, 16)
            sp.dma_start(dst_n[EP - 1:EP, 0:ET - 1], dst[1 + (EP - 1) * ET:E].rearrange("(a t) -> a t", a=1))\
                .then_inc(edges_in, 16)
            sp.dma_start(src_e[0:EP, :], src.rearrange("(p t) -> p t", t=ET)).then_inc(edges_in, 16)
            sp.dma_start(xt[:, 0, :], x[0:P, :]).then_inc(x_in[0], 16)

            def load_biases(l):
                for to, of in ((bias[:, 0, :], params[l][1]), (bias[:, 1, :], params[l][3])):
                    sp.dma_start(to, of.partition_broadcast(P)).then_inc(params_in[l], 16)

            def load_attention(l):
                sp.dma_start(a08[:, :], params[l][4].rearrange("h d -> (h d)").partition_broadcast(P))\
                    .then_inc(attn_in, 16)

            def load_weights(l, which=(0, 1)):
                for m in which:
                    sp.dma_start(wts[:, m, :, :], params[l][2 * m].rearrange("(k p) n -> p k n", p=P))\
                        .then_inc(weights_in[l][m], 16)

            load_weights(0, (0,))
            sp.dma_start(xt[:, 1:NC - 1, :], x[P:(NC - 1) * P, :].rearrange("(c p) d -> p c d", p=P))\
                .then_inc(x_in[1], 16)
            sp.wait_ge(pad_ready, 1)
            sp.dma_start(xt[0:NLAST, NC - 1, :], x[(NC - 1) * P:N, :]).then_inc(x_in[2], 16)
            load_biases(0)
            load_attention(0)
            load_weights(0, (1,))
            sp.wait_ge(edges_in, 64)
            sp.dma_start(src_sorted[0:E, :].rearrange("(p t) a -> p (t a)", t=ET), src_e[0:EP, :])\
                .then_inc(src_copied, 16)
            sp.dma_start(src_sorted[E:E + ET, :].rearrange("(a t) o -> a (t o)", a=1), srcwin[0:1, 0:ET])\
                .then_inc(src_copied, 16)
            sp.wait_ge(order_known, 1)
            sp.dma_start(srcwin[0:EP, 0:ET], src_sorted[0:E, :].rearrange("(p t) a -> p (t a)", t=ET))\
                .then_inc(win_in, 16)
            sp.dma_start(srcwin[0:EP, ET:ET + G - 1],
                         src_sorted[ET:E + ET, :].rearrange("(p t) a -> p (t a)", t=ET)[:, 0:G - 1])\
                .then_inc(win_in, 16)
            sp.wait_ge(win4_ready, 1)
            sp.dma_start(src_win[0:E, :].rearrange("(p t) g -> p (t g)", t=ET),
                         win4[0:EP, :, :].rearrange("p t g -> p (t g)")).then_inc(win_stored, 16)
            sp.dma_start(src_win[E:E + 1, :], srcwin[EP:EP + 1, 0:G]).then_inc(win_stored, 16)
            sp.wait_ge(h_ready[0], NC)
            sp.dma_start(h_saved, ht[:, :, :].rearrange("p c d -> p (c d)")).then_inc(h_stored, 16)

            for l in range(2):
                for n in range(2 * NC):
                    c, m = n // 2, n % 2
                    to = (fs_table, fd_table)[m][l]
                    sp.wait_ge(tbl_ready, 2 * NC * l + n + 1)
                    sp.dma_start(to[c * P:(c + 1) * P, :], tbl[:, n % 4, :]).then_inc(tbl_stored[n % 4], 16)
                sp.wait_ge(dlt_ready[l], QT)
                if l == 0:
                    load_attention(1)
                    sp.wait_ge(h_stored, 16)
                    sp.dma_start(fflat[:, 0:RING * D], h_saved[:, 0:RING * D]).then_inc(kept_in, 16)
                    sp.dma_start(zflat[:, 0:(NC - RING) * D], h_saved[:, RING * D:NC * D]).then_inc(kept_in, 16)
                else:
                    sp.dma_start(fflat[:, 0:RING * D].rearrange("p (c d) -> p c d", c=RING),
                                 x[0:RING * P, :].rearrange("(c p) d -> p c d", p=P)).then_inc(kept_in, 16)
                    for c in range(RING, NC):
                        k = P if c < NC - 1 else NLAST
                        sp.dma_start(kept(c)[0:k, :], x[c * P:c * P + k, :]).then_inc(kept_in, 16)
                sp.wait_ge(item_mm[l], ITEMS)
                sp.dma_start(lnw, params[l][5].partition_broadcast(P)).then_inc(ln_in, 16)
                sp.dma_start(lnb, params[l][6].partition_broadcast(P)).then_inc(ln_in, 16)
                if l == 0:
                    load_weights(1)
                    load_biases(1)
            for c in range(NC):
                k = P if c < NC - 1 else NLAST
                sp.wait_ge(y_ready, c + 1)
                sp.dma_start(out[c * P:c * P + k, :], xt[0:k, c, :]).then_inc(y_stored, 16)
            sp.wait_ge(y_stored, 16 * NC)

        @block.gpsimd
        def _(po):
            step = Link(po, pool_step)

            def take_wait(k=0):
                return nc.gpsimd.tensor_tensor(turn[:, k + 1:k + 2], turn[:, 0:1], turn[:, 0:1], ALU.add)

            step(nc.gpsimd.memset(turn[:, :], 0))
            step(nc.gpsimd.memset(dst_n[96:P, :], 1 << 20))
            nc.gpsimd.memset(srcwin[:, :], 0).then_inc(consts_ready, 1)
            step(nc.gpsimd.memset(ident[:, :], 0.0))
            step(nc.gpsimd.affine_select(out=ident[:, :], in_=ident[:, :], compare_op=ALU.not_equal, fill=1.0,
                                         base=0, pattern=[[-1, P]], channel_multiplier=1))
            step(nc.gpsimd.memset(spread[0:LO, :, :], 0.0))
            for r in range(P // LO):
                nc.gpsimd.affine_select(out=spread[0:LO, r, :], in_=spread[0:LO, r, :], compare_op=ALU.not_equal,
                                        fill=1.0, base=r * LO, pattern=[[-1, P]], channel_multiplier=1)
            step(nc.gpsimd.memset(ones, 1.0))
            for tri, op in ((tri_strict, ALU.is_gt), (tri_incl, ALU.is_ge)):
                step(nc.gpsimd.affine_select(out=tri, in_=ones, compare_op=op, fill=0.0,
                                             base=0, pattern=[[1, P]], channel_multiplier=-1))
            nc.gpsimd.iota(iota_lo, pattern=[[1, P]], base=0, channel_multiplier=0,
                           allow_small_or_imprecise_dtypes=True)
            nc.gpsimd.iota(iota4, pattern=[[1, G]], base=0, channel_multiplier=0,
                           allow_small_or_imprecise_dtypes=True)
            step(nc.gpsimd.iota(qidx, pattern=[[P, QT]], base=0, channel_multiplier=1,
                                allow_small_or_imprecise_dtypes=True))
            nc.gpsimd.memset(zeroQ, 0.0).then_inc(consts_ready, 1)

            po.wait_ge(src_copied, 32)
            po.wait_ge(flag_ready, 1)
            not_sorted = po.value_load(flag[0:1, 0:1])
            with po.If(not_sorted > 0):
                with po.Fori(0, ET) as i:
                    po.wait_ge(pos_ready, i + 1)
                    take_wait().then_inc(turn_done, 1)
                    po.indirect_dma_start(src_sorted, bass.IndirectOffsetOnAxis(ap=pos_i[0:EP, :], axis=0),
                                          src_c[0:EP, :], None).then_inc(scattered, 16)
                    po.wait_ge(turn_done, i + 1)
                po.wait_ge(scattered, 16 * ET)
                po.sem_inc(order_known, 1)
            with po.Else():
                po.sem_inc(order_known, 1)

            po.wait_ge(win_stored, 32)
            po.wait_ge(e0_ready, 1)
            for t in range(QT):
                po.indirect_dma_start(srcq[:, t, :], None, src_win,
                                      bass.IndirectOffsetOnAxis(ap=e0i[:, t:t + 1], axis=0)).then_inc(srcq_in, 16)
            po.wait_ge(srcq_in, 16 * QT)

            def first_gathers(l):
                assert G * ROW <= KC * D
                for t in range(RING):
                    nc.gpsimd.tensor_copy(slotidx[:, t, 0:G], srcq[:, t, :]).then_inc(idx_ready[l], 1)
                    nc.gpsimd.tensor_copy(slotidx[:, t, G:G + 1], dstrow[:, t:t + 1]).then_inc(idx_ready[l], 1)
                for k in (0, 2):
                    po.wait_ge(tbl_stored[k], stored_target(l, k))
                po.wait_ge(idx_ready[l], 2 * RING)
                take_wait()

                def sources(t):
                    for j in range(G):
                        po.indirect_dma_start(gring[:, t, j, :], None, fs_table[l],
                                              bass.IndirectOffsetOnAxis(ap=slotidx[:, t, j:j + 1], axis=0))\
                            .then_inc((rows_in_a, rows_in_b)[j // 2][l][t], 16)

                def destinations(t):
                    po.indirect_dma_start(fring[:, t, :], None, fd_table[l],
                                          bass.IndirectOffsetOnAxis(ap=slotidx[:, t, G:G + 1], axis=0))\
                        .then_inc(rows_in_a[l][t], 16)

                sources(0)
                for k in (1, 3):
                    po.wait_ge(tbl_stored[k], stored_target(l, k))
                take_wait(1)
                destinations(0)
                destinations(1)
                sources(1)
                linear(l, 0, 0, 0)
                destinations(2)
                sources(2)

            def gathers(l, t, u, trip):
                nc.gpsimd.tensor_copy(slotidx[:, u, 0:G],
                                      srcq[:, ds(t, 1), :].rearrange("p a g -> p (a g)"))\
                    .then_inc(idx_ready[l], 1)
                nc.gpsimd.tensor_copy(slotidx[:, u, G:G + 1], dstrow[:, ds(t, 1)]).then_inc(idx_ready[l], 1)
                po.wait_ge(idx_ready[l], t * 2 + 2)
                po.wait_ge(dlt_ready[l], t - (RING - 1))
                take_wait()
                po.indirect_dma_start(fring[:, u, :], None, fd_table[l],
                                      bass.IndirectOffsetOnAxis(ap=slotidx[:, u, G:G + 1], axis=0))\
                    .then_inc(rows_in_a[l][u], 16)
                for j in range(G):
                    if j % 2 == 0:
                        po.wait_ge(sum_mm[l], (t - RING) * G + (j + 2))
                        take_wait(1 + j // 2)
                    po.indirect_dma_start(gring[:, u, j, :], None, fs_table[l],
                                          bass.IndirectOffsetOnAxis(ap=slotidx[:, u, j:j + 1], axis=0))\
                        .then_inc((rows_in_a, rows_in_b)[j // 2][l][u], 16)

            def linear(l, t, u, trip):
                H = heads[l]
                po.wait_ge(rows_in_a[l][u], (trip + 1) * 48)
                po.wait_ge(rows_in_b[l][u], (trip + 1) * 32)
                nc.gpsimd.tensor_tensor(lin[:, u, :, 0:H], gring[:, u, :, D:D + H],
                                        bc(fring[:, u, D:D + H], 1, G), ALU.add).then_inc(lin_step[l], 1)
                po.wait_ge(lin_step[l], t + 1)
                po.wait_ge(prep_done, 1)
                mk = mask[:, ds(t, 1), :].rearrange("p a g -> p (a g)")
                nc.gpsimd.tensor_tensor(lin[:, u, :, 0:H], lin[:, u, :, 0:H],
                                        bc(mk, 2, H), ALU.add).then_inc(lin_ready[l], 1)

            def weigh3(t, u):
                po.wait_ge(exp_done[0], t + 1)
                row = gring[:, u, G - 1, 0:D].rearrange("p (h d) -> p h d", h=H1)
                nc.gpsimd.tensor_tensor(row, row, bc(gring[:, u, G - 1, D:D + H1], 2, D // H1), ALU.mult)\
                    .then_inc(prod3_ready, 1)

            for l in range(2):
                first_gathers(l)
                if l == 0:
                    weigh3(0, 0)
                linear(l, 1, 1, 0)
                with po.Fori(1, LOOPS) as i:
                    for u in range(RING):
                        gathers(l, i * RING + u, u, i)
                        if l == 0:
                            weigh3(i * RING + (u - 2), (u - 2) % RING)
                        prev = (u - 1) % RING
                        linear(l, i * RING + (u - 1), prev, i if u else i - 1)
                for t in range(LOOPS * RING, QT):
                    gathers(l, t, t % RING, t // RING)
                    if l == 0:
                        weigh3(t - 2, (t - 2) % RING)
                    linear(l, t - 1, (t - 1) % RING, (t - 1) // RING)
                linear(l, QT - 1, (QT - 1) % RING, (QT - 1) // RING)
                if l == 0:
                    weigh3(QT - 2, (QT - 2) % RING)
                    weigh3(QT - 1, (QT - 1) % RING)

                cb = combine_views(heads[l])
                po.wait_ge(sum_mm[l], (QT - 1) * G)
                nc.gpsimd.memset(cb["zrow"][0:1, :], 0.0).then_inc(comb_const, 1)
                nc.gpsimd.iota(cb["iota"], pattern=[[1, P]], base=0, channel_multiplier=0,
                               allow_small_or_imprecise_dtypes=True).then_inc(comb_const, 1)
            po.wait_ge(ln_in, 64)
            po.wait_ge(kept_in, 32 + 16 * (1 + NC - RING))
            for c in range(NC):
                nc.gpsimd.tensor_tensor(kept(c), kept(c), lnb, ALU.add).then_inc(kept_biased, 1)
                if c:
                    po.wait_ge(normed, c)
                    nc.gpsimd.tensor_tensor(xt[:, c - 1, :], xt[:, c - 1, :], lnw, ALU.mult).then_inc(scaled, 1)

        @block.scalar
        def _(act):
            step = Link(act, act_step)

            def sqrt_var(n, of):
                act.wait_ge(var_ready, n)
                nc.scalar.activation(of, of, ACT.Sqrt).then_inc(sd_ready, 1)

            def copy_hT(l, c):
                act.wait_ge(hT_mm, NC * l + c + 1)
                b = 2 * (c % 2)
                nc.scalar.activation(hT[:, :, c * P:(c + 1) * P],
                                     psf[:, b * 512:b * 512 + D].rearrange("p (k n) -> p k n", k=KC),
                                     ACT.Copy).then_inc(hT_ready, 1)

            def weigh(l, t, u):
                H = heads[l]
                act.wait_ge(dlt_ready[l], t + 1)
                if l == 0:
                    nc.scalar.activation(gring[:, u, :, D:D + H], dlt[:, u, :, 0:H], ACT.Exp).then_inc(exp_done[l], 1)
                    act.wait_ge(exp_done[l], t + 1)
                    for j in range(ACT_EDGES[l]):
                        for h in range(H):
                            part = gring[:, u, j, h * (D // H):(h + 1) * (D // H)]
                            last = nc.scalar.activation(part, part, ACT.Copy,
                                                        scale=gring[:, u, j, D + h:D + h + 1])
                        last.then_inc(prod_ready[l], 1)
                else:
                    nc.scalar.activation(dlt[:, u, :, 0:1], dlt[:, u, :, 0:1], ACT.Exp).then_inc(exp_done[l], 1)
                    act.wait_ge(exp_done[l], t + 1)
                    for j in range(G):
                        nc.scalar.activation(gring[:, u, j, :], gring[:, u, j, :], ACT.Copy,
                                             scale=dlt[:, u, j, 0:1]).then_inc(prod_ready[l], 1)

            def save(l, t, u):
                act.wait_ge(sum_mm[l], (t + 1) * G)
                b = 2 * u
                row = vres[:, ds(t, 1), :].rearrange("p a n -> p (a n)")
                nc.scalar.activation(row[:, 0:HALF], ps[:, b, 0:HALF], ACT.Copy)
                nc.scalar.activation(row[:, HALF:ROW], ps[:, b + 1, 0:HALF], ACT.Copy).then_inc(sum_saved[l], 1)

            def h_of(c):
                act.wait_ge(norm_ready, c + 1)
                nc.scalar.activation(ht[:, c, :], xt[:, c, :], ACT.Relu, bias=shift[:, c:c + 1],
                                     scale=rstd[:, c:c + 1]).then_inc(h_ready[0], 1)

            sqrt_var(1, rstd[:, 0:1])
            h_of(0)
            copy_hT(0, 0)
            for c in range(1, NC):
                sqrt_var(c + 1, rstd[:, c:c + 1])
                if c > 1:
                    h_of(c - 1)
            h_of(NC - 1)
            for c in range(1, NC):
                copy_hT(0, c)
            for l in range(2):
                for k in range(4):
                    act.wait_ge(tbl_stored[k], stored_target(l, k))
                weigh(l, 0, 0)
                for t in range(1, RING):
                    weigh(l, t, t)
                    save(l, t - 1, t - 1)
                with act.Fori(1, LOOPS) as i:
                    for u in range(RING):
                        weigh(l, i * RING + u, u)
                        save(l, i * RING + (u - 1), (u - 1) % RING)
                for t in range(LOOPS * RING, QT):
                    weigh(l, t, t % RING)
                    save(l, t - 1, (t - 1) % RING)
                save(l, QT - 1, (QT - 1) % RING)
                cb = combine_views(heads[l])
                act.wait_ge(w_arg, l + 1)
                nc.scalar.activation(cb["mT"][0:QT, :, :], cb["mT"][0:QT, :, :], ACT.Exp).then_inc(wT_ready, 1)
                def elu_part(c):
                    act.wait_ge(mean_ready, NC * l + c + 1)
                    step(nc.scalar.activation(expneg[:, c, :], xt[:, c, :], ACT.Relu, scale=-1.0))
                    nc.scalar.activation(expneg[:, c, :], expneg[:, c, :], ACT.Exp, scale=-1.0).then_inc(elu_exp, 1)

                ahead = (3, NC)[l]
                for c in range(ahead):
                    elu_part(c)
                for c in range(NC):
                    sqrt_var(NC * (l + 1) + c + 1, rstd[:, c:c + 1])
                    if l and c < NC - 1:
                        act.wait_ge(shift_ready, c + 1)
                        nc.scalar.activation(xt[:, c, :], xt[:, c, :], ACT.Identity, bias=shift[:, c:c + 1],
                                             scale=rstd[:, c:c + 1]).then_inc(normed, 1)
                    if c == 0:
                        for later in range(ahead, NC):
                            elu_part(later)
                    elif l == 0:
                        copy_hT(1, c - 1)
                if l == 0:
                    copy_hT(1, NC - 1)

        @block.vector
        def _(ve):
            step = Link(ve, dve_step)
            tt, ts = nc.vector.tensor_tensor, nc.vector.tensor_scalar

            def pick(to, of, less):
                part = picked[:, :]
                step(nc.vector.memset(to[:, :], 0.0))
                for c in range(NC):
                    step(ts(part, chunkof[:, c:c + QT], float(c), None, ALU.is_equal))
                    if less:
                        step(nc.vector.scalar_tensor_tensor(part, of, -less * c, part, ALU.add, ALU.mult))
                    else:
                        step(tt(part, of, part, ALU.mult))
                    step(tt(to[:, c:c + QT], to[:, c:c + QT], part, ALU.add))

            def var_of(c):
                for k in range(2):
                    got = step.note(nc.vector.bn_stats(stats[:, c, 6 * k:6 * k + 6],
                                                       xt[:, c, k * (D // 2):(k + 1) * (D // 2)]))
                return got

            def deviation(c):
                ve.wait_ge(x_in[0 if c == 0 else 2 if c == NC - 1 else 1], 16)
                step.need(var_of(c))
                step(nc.vector.bn_aggr(mv[:, c, :], stats[:, c, :]))
                ts(rstd[:, c:c + 1], mv[:, c, 1:2], EPS, None, ALU.add).then_inc(var_ready, 1)

            def normalizer(c):
                ve.wait_ge(sd_ready, c + 1)
                step(nc.vector.reciprocal(rstd[:, c:c + 1], rstd[:, c:c + 1]))
                nc.vector.scalar_tensor_tensor(shift[:, c:c + 1], mv[:, c, 0:1], -1.0, rstd[:, c:c + 1],
                                               ALU.mult, ALU.mult).then_inc(norm_ready, 1)

            nc.vector.memset(xt[96:P, NC - 1, :], 0.0).then_inc(pad_ready, 1)
            step(nc.vector.memset(zero8, 0.0))
            def table_consts(l):
                ve.wait_ge(attn_in, 16 * (l + 1))
                step(ts(a02, a08[:, :], 0.2, None, ALU.mult))
                step(ts(a08[:, :], a08[:, :], 0.8, None, ALU.mult))
                for k in range(4):
                    step(nc.vector.memset(tbl[:, k, D:ROW], 1.0))

            def table(l, n):
                H = heads[l]
                m, k = n % 2, n % 4
                ve.wait_ge(params_in[l], 32)
                if n >= 4:
                    ve.wait_ge(tbl_stored[k], stored_target(l, k) - 16 * (len(range(n, 2 * NC, 4))))
                ve.wait_ge(proj_mm, 2 * NC * l + n + 1)
                b = 4 + 2 * (n % 2)
                for hf in range(2):
                    last = tt(tbl[:, k, hf * (D // 2):(hf + 1) * (D // 2)], ps[:, b + hf, 0:D // 2],
                              bias[:, m, hf * (D // 2):(hf + 1) * (D // 2)], ALU.add)
                    if hf == 0:
                        step.note(last)
                last.then_inc(proj_read, 1)
                ve.wait_ge(proj_read, 2 * NC * l + n + 1)
                step(tt(tmp, tbl[:, k, 0:D], a02, ALU.mult))
                nc.vector.reduce_sum(tbl[:, k, D:D + H], tmp.rearrange("p (h d) -> p h d", h=H),
                                     axis=AX.X).then_inc(tbl_ready, 1)
                ve.wait_ge(tbl_ready, 2 * NC * l + n + 1)

            ve.wait_ge(edges_in, 64)
            ve.wait_ge(consts_ready, 2)

            step(tt(unsorted_e[0:EP, :], dst_e[0:EP, :], dst_n[0:EP, :], ALU.is_gt))
            step(nc.vector.reduce_sum(nodecnt[0:EP, :], unsorted_e[0:EP, :], axis=AX.X))
            step(ts(digit[0:EP, 0, :], dst_e[0:EP, :], LO - 1, None, ALU.bitwise_and))
            step(ts(digit[0:EP, 1, :], dst_e[0:EP, :], LO.bit_length() - 1, None, ALU.logical_shift_right))
            step(nc.vector.tensor_copy(digitf[0:EP, :, :], digit[0:EP, :, :]))
            deviation(0)

            tt(oh_hi[0:EP, :, :], bc(iota_lo[0:EP, 0:HI], 1, ET), bc(digitf[0:EP, 1, :], 2, HI),
               ALU.is_equal).then_inc(digits_ready, 1)
            normalizer(0)
            tt(oh_lo[0:EP, :, :], bc(iota_lo[0:EP, 0:LO], 1, ET), bc(digitf[0:EP, 0, :], 2, LO),
               ALU.is_equal).then_inc(digits_ready, 1)
            for c in range(1, NC):
                deviation(c)
                if c > 1:
                    normalizer(c - 1)
            normalizer(NC - 1)
            table_consts(0)
            table(0, 0)

            ve.wait_ge(hist_done, 1)
            nc.vector.tensor_copy(flag[0:1, :], ps[0:1, 1, 0:1]).then_inc(flag_ready, 1)
            nc.vector.tensor_copy(cnt32[0:LO, :], ps[0:LO, 0, 0:HI]).then_inc(prep_in, 1)
            ve.wait_ge(hist_done, 2)
            step(nc.vector.tensor_copy(cnt[:, 0, :], ps[:, 2, 0:NC]))
            step(ts(cnt_i, cnt[:, 0, :], float(G - 1), None, ALU.add))
            step(ts(cnt_i, cnt_i, G.bit_length() - 1, None, ALU.logical_shift_right))
            nc.vector.tensor_copy(cnt[:, 1, :], cnt_i).then_inc(prep_in, 1)
            ve.wait_ge(prep_mm, 1)
            step(nc.vector.tensor_copy(tot.rearrange("p a b -> p (a b)"), ps[:, 1, 0:2 * NC]))
            for k in range(2):
                step(nc.vector.tensor_tensor_scan(run[:, k, :], tot[:, k, :], zero8[:, 0:NC], 0.0, ALU.add, ALU.add))
            step(tt(run, run, tot, ALU.subtract))
            step(tt(first.rearrange("p a b -> p (a b)"), run.rearrange("p a b -> p (a b)"),
                    ps[:, 3, 0:2 * NC], ALU.add))
            step(tt(posn[:, 0, :], first[:, 1, :], cnt[:, 1, :], ALU.add))
            step(nc.vector.tensor_copy(posn[:, 1, :], first[:, 1, :]))

            ve.wait_ge(h_ready[0], NC)
            ve.wait_ge(flag_ready, 1)
            not_sorted = ve.value_load(flag[0:1, 0:1])
            with ve.If(not_sorted > 0):
                for c in range(NC):
                    ts(rank[:, c, :], ident[:, :], first[:, 0, c:c + 1], None, ALU.mult).then_inc(base_in, 1)
                ve.wait_ge(base_mm, 1)
                nc.vector.tensor_copy(base.rearrange("p a b -> p (a b)"), psf[:, 0:NC * P])\
                    .then_inc(base_in, 1)
                with ve.Fori(0, ET) as i:
                    ve.wait_ge(base_in, NC + 1 + i * 7)
                    ve.wait_ge(base_in, NC + 1)
                    jd = joint[0:EP, :, :].rearrange("p a b -> p (a b)").rearrange("p (a b) -> p a b", a=HI)
                    tt(jd, oh_lo[0:EP, ds(i, 1), :].to_broadcast([EP, HI, LO]),
                       bc(oh_hi[0:EP, ds(i, 1), :].rearrange("p a c -> p (a c)"), 2, LO), ALU.mult).then_inc(joint_ready, 1)
                    ve.wait_ge(joint_mm, i + 1)
                    flat = lambda v: v[0:EP, :, :].rearrange("p a b -> p (a b)")
                    tt(flat(rank), psf[0:EP, 0:NC * P], flat(base), ALU.add).then_inc(base_in, 1)
                    ve.wait_ge(base_in, NC + 2 + i * 7)
                    tt(flat(rank), flat(rank), flat(joint), ALU.mult).then_inc(base_in, 1)
                    ve.wait_ge(base_in, NC + 3 + i * 7)
                    nc.vector.reduce_sum(pos_f[0:EP, :], flat(rank), axis=AX.X).then_inc(base_in, 1)
                    ve.wait_ge(base_in, NC + 4 + i * 7)
                    nc.vector.tensor_copy(pos_i[0:EP, :], pos_f[0:EP, :]).then_inc(base_in, 1)
                    ve.wait_ge(base_in, NC + 5 + i * 7)
                    nc.vector.tensor_copy(src_c[0:EP, :], src_e[0:EP, ds(i, 1)]).then_inc(base_in, 1)
                    ve.wait_ge(base_in, NC + 6 + i * 7)
                    tt(base.rearrange("p a b -> p (a b)"), base.rearrange("p a b -> p (a b)"),
                       psf[:, 1024:1024 + NC * P], ALU.add).then_inc(base_in, 1)
                    ve.wait_ge(base_in, NC + 7 + i * 7)
                    nc.vector.memset(rank[:, 0, 0:1], 0.0).then_inc(base_in, 1)
                    ve.sem_inc(pos_ready, 1)
                    ve.wait_ge(scattered, i * 16 + 16)
            with ve.Else():
                ve.wait_ge(flag_ready, 1)

            step(nc.vector.tensor_copy(posi, posn.rearrange("p a b -> p (a b)")))
            step(ts(posj, posi, P - 1, None, ALU.bitwise_and))
            step(nc.vector.tensor_copy(pdig[:, 0, :], posj))
            step(ts(posi, posi, P.bit_length() - 1, None, ALU.logical_shift_right))
            step(nc.vector.tensor_copy(pdig[:, 1, :], posi))
            step(tt(ohA, bc(iota_lo, 1, 2 * NC), bc(pdig[:, 0, :], 2, P), ALU.is_equal))
            step(tt(ohB, bc(iota_lo[:, 0:QT], 1, 2 * NC), bc(pdig[:, 1, :], 2, QT), ALU.is_equal))
            step(nc.vector.tensor_copy(wB[:, :, 0, :], ohB[:, 0:NC, :]))
            step(tt(wB[:, :, 1, :], ohB[:, 0:NC, :], bc(cnt[:, 0, :], 2, QT), ALU.mult))
            step(tt(wB[:, :, 2, :], ohB[:, 0:NC, :], bc(cnt[:, 1, :], 2, QT), ALU.mult))
            tt(wB2, ohB[:, NC:2 * NC, :], bc(cnt[:, 0, :], 2, QT), ALU.mult).then_inc(prep_in, 1)
            ve.wait_ge(win_in, 32)
            for j in range(G):
                last = nc.vector.tensor_copy(win4[0:EP, :, j], srcwin[0:EP, j:j + ET])
            last.then_inc(win4_ready, 1)
            ve.wait_ge(prep_mm, 2)
            step(nc.vector.tensor_copy(imp[:, 0:3, :].rearrange("p a b -> p (a b)"), ps[:, 0, 0:3 * QT]))
            nc.vector.tensor_copy(imp[:, 3, :], ps[:, 1, 0:QT]).then_inc(prep_in, 1)
            ve.wait_ge(prep_mm, 3)
            step(nc.vector.tensor_copy(ctot.rearrange("p a b -> p (a b)"), ps[:, 2, 0:4 * QT]))
            for k in range(4):
                step(nc.vector.tensor_tensor_scan(crun[:, k, :], ctot[:, k, :], zeroQ, 0.0, ALU.add, ALU.add))
            step(tt(crun, crun, ctot, ALU.subtract))
            step(tt(q.rearrange("p a b -> p (a b)"), crun.rearrange("p a b -> p (a b)"), ps[:, 3, 0:4 * QT], ALU.add))
            step(nc.vector.tensor_copy(dstq[:, :], q[:, 0, :]))
            step(ts(dstrow[:, :], q[:, 0, :], float(N - 1), None, ALU.min))
            step(tt(e0, qidx, q[:, 2, :], ALU.subtract))
            step(ts(e0, e0, float(G), None, ALU.mult))
            step(tt(e0, e0, q[:, 1, :], ALU.add))
            step(tt(left, q[:, 3, :], e0, ALU.subtract))
            ts(e0i, e0, float(E), None, ALU.min).then_inc(e0_ready, 1)
            table(0, 1)
            step(tt(mask[:, :, :], bc(iota4, 1, QT), bc(left, 2, G), ALU.is_ge))
            step(ts(mask[:, :, :], mask[:, :, :], NEG, None, ALU.mult))
            step(ts(posi[:, 0:NC], run[:, 1, :], float(QT * P - 1), None, ALU.min))
            step(ts(posi[:, 0:NC], posi[:, 0:NC], P.bit_length() - 1, None, ALU.logical_shift_right))
            step(nc.vector.tensor_copy(pdig[:, 0, 0:NC], posi[:, 0:NC]))
            step(tt(pdig[:, 0, 0:NC], pdig[:, 0, 0:NC], iota_lo[:, 0:NC], ALU.add))
            step(ts(chunkof[:, :], iota_lo[:, 0:ITEMS], pdig[:, 0, 1:2], None, ALU.is_ge))
            for c in range(2, NC):
                step(nc.vector.scalar_tensor_tensor(chunkof[:, :], iota_lo[:, 0:ITEMS], pdig[:, 0, c:c + 1],
                                                    chunkof[:, :], ALU.is_ge, ALU.add))
            step(nc.vector.tensor_copy(items[0:1, 0:ITEMS, 1], chunkof[0:1, :]))
            step(tt(items[0:1, 0:ITEMS, 0], iota_lo[0:1, 0:ITEMS], chunkof[0:1, :], ALU.subtract))
            pick(rel, dstq[:, :], float(P))
            ve.wait_ge(dst_mm, 1)
            step(nc.vector.tensor_copy(dstT[:, :], ps[0:QT, 2, 0:P]))
            nc.vector.memset(redu[:, :, :], 0.0).then_inc(prep_done, 1)
            def logits(l, t, u, trip, first=False):
                H = heads[l]
                per = PER[l]
                base = t * per - (0 if first else LATE[l])
                k = [0]

                def mark(ins):
                    k[0] += 1
                    ins.then_inc(loop_step[l], 1)
                    return k[0]

                def need(count):
                    ve.wait_ge(loop_step[l], base + count)

                def add(j):
                    return mark(tt(z[:, j % 2, :], gring[:, u, j, 0:D], fring[:, u, 0:D], ALU.add))

                def weigh(j):
                    kw = dict(accum_out=redu[:, j, 0:1]) if l else {}
                    ins = nc.vector.scalar_tensor_tensor(z[:, j % 2, :], z[:, j % 2, :], 0.0, a08[:, :],
                                                         ALU.max, ALU.mult, **kw)
                    if l or j % 2 == 0:
                        return mark(ins)
                    ins.then_inc(z_ready, 1)

                def folded_total(j):
                    return mark(add_folded(j))

                def total(j):
                    return mark(nc.vector.tensor_reduce(redu[:, j, :], z[:, j % 2, :].rearrange("p (h d) -> p h d", h=H),
                                                        axis=AX.X, op=ALU.add))

                ago = not first
                tl, ul = t - 1, (u - 1) % RING

                def logit():
                    ve.wait_ge(lin_ready[l], tl + 1)
                    return mark(tt(lgt[:, :, 0:H], redu[:, :, 0:H], lin[:, ul, :, 0:H], ALU.add))

                def largest():
                    return mark(nc.vector.tensor_reduce(maxima(l, tl), lgt[:, :, 0:H].rearrange("p g h -> p h g"),
                                                        axis=AX.X, op=ALU.max))

                ve.wait_ge(rows_in_a[l][u], (trip + 1) * 48)
                if l == 0:
                    if ago:
                        ve.wait_ge(folded, t * 2)
                    a1 = add(1)
                    if ago:
                        n_late = folded_total(3)
                        need(0)
                    a0 = add(0)
                    if ago:
                        need(n_late)
                        n_late = logit()
                    need(a1)
                    weigh(1)
                    if ago:
                        need(n_late)
                        n_late = largest()
                    need(a0)
                    b0 = weigh(0)
                    if ago:
                        need(n_late)
                        finish(l, tl, ul)
                    need(b0)
                    c0 = total(0)
                    ve.wait_ge(rows_in_b[l][u], (trip + 1) * 32)
                    ve.wait_ge(folded, t * 2 + 1)
                    a3 = add(3)
                    folded_total(1)
                    need(c0)
                    a2 = add(2)
                    need(a3)
                    weigh(3)
                    need(a2)
                    b2 = weigh(2)
                    need(b2)
                    total(2)
                else:
                    if ago:
                        need(0)
                    a1 = add(1)
                    if ago:
                        n_late = logit()
                    a0 = add(0)
                    if ago:
                        need(n_late)
                        n_late = largest()
                    need(a1)
                    b1 = weigh(1)
                    if ago:
                        need(n_late)
                        finish(l, tl, ul)
                    need(a0)
                    b0 = weigh(0)
                    ve.wait_ge(rows_in_b[l][u], (trip + 1) * 32)
                    need(b1)
                    a3 = add(3)
                    need(b0)
                    a2 = add(2)
                    need(a3)
                    weigh(3)
                    need(a2)
                    weigh(2)
                assert k[0] == per - (LATE[l] if first else 0)

            def add_folded(j):
                return nc.vector.tensor_reduce(redu[:, j, :], ps[:, 6 + j // 2, 0:D // FOLD].rearrange("p (h n) -> p h n", h=H1),
                                               axis=AX.X, op=ALU.add)

            def finish(l, t, u):
                H = heads[l]
                tt(dlt[:, u, :, 0:H], lgt[:, :, 0:H], bc(maxima(l, t), 1, G), ALU.subtract).then_inc(dlt_ready[l], 1)

            def maxima(l, t):
                return gmx(l)[:, ds(t, 1), :].rearrange("p a h -> p (a h)")

            def segments(l):
                H = heads[l]
                cb = combine_views(H)
                T = QT
                dq = dstT[:, :]
                brk, change, link = cb["brk"], cb["change"], cb["link"]
                fl = lambda v: v[0:T, :, :].rearrange("p h n -> p (h n)")
                fe = lambda v: v[0:H, :, :].rearrange("p t k -> p (t k)")
                mx = psf[0:T, 3072:3072 + H * P]
                ve.wait_ge(sum_mm[l], (QT - 2) * G)
                step(nc.vector.memset(change[0:T, :], 1.0))
                step(tt(change[0:T, 1:P], dq[:, 1:P], dq[:, 0:P - 1], ALU.not_equal))
                step(ts(change[0:T, :], change[0:T, :], NEG, None, ALU.mult))
                for k, at in ((0, 0), (1, P - 1)):
                    last = nc.vector.tensor_copy(cb["edgeq"][0:T, k, :], dq[:, at:at + 1].to_broadcast([T, H]))
                    if k == 0:
                        step.note(last)
                last.then_inc(seg_in, 1)
                step.note(nc.vector.tensor_copy(brk[0:T, 0:H * P].rearrange("p (h n) -> p h n", h=H),
                                                bc(change[0:T, 0:P], 1, H)))
                step.note(nc.vector.tensor_copy(brk[0:T, H * P:H * P + 1], change[0:T, P:P + 1]))
                for k, at in ((0, 0), (1, P - 1)):
                    got = step.note(ts(cb["outer"][0:T, k, :], dq, dq[:, at:at + 1], NEG, ALU.not_equal, ALU.mult))
                step.need(got)
                ve.wait_ge(seg_mm, 4 * l + 1)
                step(nc.vector.tensor_tensor_scan(fl(cb["fwd"]), brk[0:T, 0:H * P], mx, NEG, ALU.add, ALU.max))
                ve.wait_ge(sum_mm[l], (QT - 1) * G)
                step(nc.vector.tensor_tensor_scan(fl(cb["seg"])[:, ::-1], brk[0:T, 1:H * P + 1][:, ::-1],
                                                  fl(cb["fwd"])[:, ::-1], NEG, ALU.add, ALU.max))
                step.note(nc.vector.tensor_copy(cb["edge"][0:T, 0, :], cb["seg"][0:T, :, 0]))
                nc.vector.tensor_copy(cb["edge"][0:T, 1, :], cb["seg"][0:T, :, P - 1]).then_inc(seg_in, 1)
                ve.wait_ge(seg_mm, 4 * l + 2)
                step.note(nc.vector.memset(link[0:H, :], 1.0))
                for k in range(2):
                    got = step.note(nc.vector.tensor_copy(cb["dqe"][0:H, :, k], ps[0:H, 3, k * T:(k + 1) * T]))
                step.need(got)
                step(tt(link[0:H, 1:2 * T], fe(cb["dqe"])[:, 1:2 * T], fe(cb["dqe"])[:, 0:2 * T - 1], ALU.not_equal))
                step.note(ts(link[0:H, :], link[0:H, :], NEG, None, ALU.mult))
                ve.wait_ge(seg_mm, 4 * l + 3)
                for k in range(2):
                    got = step.note(nc.vector.tensor_copy(cb["val"][0:H, :, k], ps[0:H, 2, k * T:(k + 1) * T]))
                step.need(got)
                step(nc.vector.tensor_tensor_scan(fe(cb["sf"]), link[0:H, 0:2 * T], fe(cb["val"]), NEG, ALU.add, ALU.max))
                nc.vector.tensor_tensor_scan(fe(cb["sm"])[:, ::-1], link[0:H, 1:2 * T + 1][:, ::-1],
                                             fe(cb["sf"])[:, ::-1], NEG, ALU.add, ALU.max).then_inc(seg_in, 1)
                ve.wait_ge(seg_mm, 4 * l + 4)
                step(nc.vector.tensor_copy(cb["back"][0:T, :, :].rearrange("p k h -> p (k h)"), ps[0:T, 2, 256:256 + 2 * H]))
                for k in range(2):
                    if k:
                        step.need(got)
                    for h in range(H):
                        seg = cb["seg"][0:T, h, :]
                        got = step.note(nc.vector.scalar_tensor_tensor(seg, cb["outer"][0:T, k, :], cb["back"][0:T, k, h:h + 1],
                                                                       seg, ALU.add, ALU.max))
                step.need(got)
                tt(fl(cb["mT"]), mx, fl(cb["seg"]), ALU.subtract).then_inc(w_arg, 1)
                ve.wait_ge(w_mm, l + 1)
                nc.vector.tensor_copy(cb["w"].rearrange("p t h -> p h t"),
                                      ps[:, 5, 0:H * T].rearrange("p (h t) -> p h t", h=H)).then_inc(w_ready, 1)
                ve.wait_ge(w_ready, l + 1)
                if l:
                    pick(wsel, cb["w"].rearrange("p t h -> p (t h)"), 0.0)

            def hot(l, i, u, first, scale_tile):
                H = heads[l]
                cb = combine_views(H)
                if scale_tile and l == 0:
                    row = vres[:, ds(i, 1), :].rearrange("p a n -> p (a n)")
                    wt = cb["w"][:, ds(i, 1), :].rearrange("p a h -> p (a h)")
                    fe = row[:, 0:D].rearrange("p (h d) -> p h d", h=H)
                    ve.wait_ge(w_ready, l + 1)
                    tt(fe, fe, bc(wt, 2, D // H), ALU.mult)
                    tt(row[:, D:ROW], row[:, D:ROW], wt, ALU.mult)
                if not first:
                    ve.wait_ge(item_mm[l], i - (RING - 1))
                ve.wait_ge(comb_const, 2 * l + 2)
                if l == 0:
                    last = ts(cb["hot"][:, u, :], cb["iota"], rel[:, ds(i, 1)], None, ALU.is_equal)
                else:
                    last = ts(cb["hot"][:, u, :], cb["iota"], rel[:, ds(i, 1)], wsel[:, ds(i, 1)],
                              ALU.is_equal, ALU.mult)
                last.then_inc(hot_ready[l], 1)

            def nodes(l):
                H = heads[l]
                ve.wait_ge(item_mm[l], ITEMS)
                dcol = psf[:, NC * D:NC * D + NC * 8].rearrange("p (c h) -> p c h", h=8)[:, :, 0:H]
                dn = den[:, :, 0:H]
                step(ts(dn, dcol, 1e-30, None, ALU.max))
                step(nc.vector.reciprocal(dn, dn))

                def mean(c):
                    pc = psf[:, c * D:(c + 1) * D].rearrange("p (h d) -> p h d", h=H)
                    tt(xt[:, c, :].rearrange("p (h d) -> p h d", h=H), pc, bc(dn[:, c, :], 2, D // H), ALU.mult)\
                        .then_inc(mean_ready, 1)

                mean(0)
                mean(1)
                ve.wait_ge(kept_in, (32, 32 + 16 * (1 + NC - RING))[l])
                for c in range(NC + 1):
                    b = c - 1
                    here = l == 0 or b == NC - 1
                    w = xt[:, max(b, 0), :]
                    if c < NC:
                        v = xt[:, c, :]
                        ve.wait_ge(mean_ready, NC * l + c + 1)
                        ve.wait_ge(elu_exp, NC * l + c + 1)
                        now = step.note(nc.vector.scalar_tensor_tensor(v, v, 0.0, expneg[:, c, :], ALU.max, ALU.add))
                    if c and here:
                        ve.wait_ge(sd_ready, NC * (l + 1) + b + 1)
                        ago = step.note(nc.vector.reciprocal(rstd[:, b:c], rstd[:, b:c]))
                    if c < NC:
                        step.need(now)
                        if l == 0:
                            now = step.note(nc.vector.scalar_tensor_tensor(v, v, -1.0, kept(c), ALU.add, ALU.add))
                        else:
                            now = step.note(ts(v, v, -1.0, None, ALU.add))
                    for later in (((2, 3), (4,)), ((2, 3, 4), ()))[l][c] if c < 2 else ():
                        mean(later)
                    if c and here:
                        step.need(ago)
                        ago = step.note(ts(w, w, mv[:, b, 0:1], rstd[:, b:c], ALU.subtract, ALU.mult))
                    if c < NC:
                        step.need(now)
                        now = var_of(c)
                    if c and not here:
                        ve.wait_ge(sd_ready, NC * (l + 1) + b + 1)
                        step(nc.vector.reciprocal(rstd[:, b:c], rstd[:, b:c]))
                        nc.vector.scalar_tensor_tensor(shift[:, b:c], mv[:, b, 0:1], -1.0, rstd[:, b:c],
                                                       ALU.mult, ALU.mult).then_inc(shift_ready, 1)
                    if c and here:
                        ve.wait_ge(ln_in, 32 * (l + 1))
                        step.need(ago)
                        ago = step.note(tt(w, w, lnw, ALU.mult))
                    if l and c >= 2:
                        ve.wait_ge(kept_biased, c - 1)
                        ve.wait_ge(scaled, c - 1)
                        tt(xt[:, c - 2, :], xt[:, c - 2, :], kept(c - 2), ALU.add).then_inc(y_ready, 1)
                    if c < NC:
                        step.need(now)
                        now = step.note(nc.vector.bn_aggr(mv[:, c, :], stats[:, c, :]))
                    if c and here:
                        step.need(ago)
                        if l == 0:
                            tt(ht[:, b, :], w, lnb, ALU.add).then_inc(h_ready[1], 1)
                        else:
                            ve.wait_ge(kept_biased, NC)
                            tt(w, w, kept(b), ALU.add).then_inc(y_ready, 1)
                    if c < NC:
                        step.need(now)
                        ts(rstd[:, c:c + 1], mv[:, c, 1:2], EPS, None, ALU.add).then_inc(var_ready, 1)
                    if l == 0 and c >= NC - 2 and c < NC:
                        if c == NC - 2:
                            table_consts(1)
                        table(1, c - (NC - 2))

            for l in range(2):
                for n in range(2, 2 * NC):
                    table(l, n)
                for t in range(RING):
                    logits(l, t, t, 0, t == 0)
                with ve.Fori(1, LOOPS) as i:
                    for u in range(RING):
                        logits(l, i * RING + u, u, i)
                for t in range(LOOPS * RING, QT):
                    logits(l, t, t % RING, t // RING)
                H, u, n = heads[l], (QT - 1) % RING, QT * PER[l] - 2
                if l == 0:
                    ve.wait_ge(folded, QT * 2)
                    add_folded(3).then_inc(loop_step[l], 1)
                ve.wait_ge(loop_step[l], n)
                ve.wait_ge(lin_ready[l], QT)
                tt(lgt[:, :, 0:H], redu[:, :, 0:H], lin[:, u, :, 0:H], ALU.add).then_inc(loop_step[l], 1)
                ve.wait_ge(loop_step[l], n + 1)
                nc.vector.tensor_reduce(maxima(l, QT - 1), lgt[:, :, 0:H].rearrange("p g h -> p h g"),
                                        axis=AX.X, op=ALU.max).then_inc(loop_step[l], 1)
                ve.wait_ge(loop_step[l], n + 2)
                finish(l, QT - 1, u)
                segments(l)
                for k in range(RING):
                    hot(l, k, k, True, True)
                with ve.Fori(1, LOOPS) as i:
                    for u in range(RING):
                        hot(l, i * RING + u, u, False, True)
                for k in range(LOOPS * RING, ITEMS):
                    hot(l, k, k % RING, False, k < QT)
                nodes(l)

        @block.tensor
        def _(te):
            mm = nc.tensor.matmul

            def transposes(l, c):
                te.wait_ge(h_ready[l], c + 1)
                if c >= 2:
                    te.wait_ge(hT_ready, NC * l + c - 1)
                for k in range(KC):
                    b = 2 * (c % 2) * 512 + k * P
                    last = nc.tensor.transpose(psf[:, b:b + P], ht[:, c, k * P:(k + 1) * P], ident[:, :])
                last.then_inc(hT_mm, 1)

            def project(l, n):
                c, m = n // 2, n % 2
                te.wait_ge(weights_in[l][m], 16)
                te.wait_ge(hT_ready, NC * l + c + 1)
                if n >= 2:
                    te.wait_ge(proj_read, 2 * NC * l + n - 1)
                b = 4 + 2 * (n % 2)
                for hf in range(2):
                    for k in range(KC):
                        last = mm(ps[:, b + hf, 0:D // 2], hT[:, k, c * P:(c + 1) * P],
                                  wts[:, m, k, hf * (D // 2):(hf + 1) * (D // 2)],
                                  start=(k == 0), stop=(k == KC - 1))
                last.then_inc(proj_mm, 1)

            te.wait_ge(consts_ready, 2)
            transposes(0, 0)
            project(0, 0)
            transposes(0, 1)
            te.wait_ge(hT_ready, 2)

            te.wait_ge(digits_ready, 2)
            for k in range(ET):
                mm(ps[0:LO, 0, 0:HI], oh_lo[0:EP, k, :], oh_hi[0:EP, k, :], start=(k == 0), stop=(k == ET - 1))
            mm(ps[:, 1, 0:1], ones[0:EP, :], nodecnt[0:EP, :], start=True, stop=True).then_inc(hist_done, 1)
            te.wait_ge(prep_in, 1)
            for r in range(P // LO):
                last = mm(ps[:, 2, 0:NC], spread[0:LO, r, :], cnt32[0:LO, r::P // LO],
                          start=(r == 0), stop=(r == P // LO - 1))
            last.then_inc(hist_done, 1)
            te.wait_ge(prep_in, 2)
            c2 = cnt.rearrange("p a b -> p (a b)")
            mm(ps[:, 1, 0:2 * NC], ones, c2, start=True, stop=True)
            mm(ps[:, 3, 0:2 * NC], tri_strict, c2, start=True, stop=True).then_inc(prep_mm, 1)

            te.wait_ge(flag_ready, 1)
            not_sorted = te.value_load(flag[0:1, 0:1])
            with te.If(not_sorted > 0):
                te.wait_ge(base_in, NC)
                for c in range(NC):
                    last = mm(psf[:, c * P:(c + 1) * P], ones, rank[:, c, :], start=True, stop=True)
                last.then_inc(base_mm, 1)
                with te.Fori(0, ET) as i:
                    te.wait_ge(joint_ready, i + 1)
                    te.wait_ge(base_in, NC + 1)
                    fj = joint[0:EP, :, :].rearrange("p a b -> p (a b)")
                    for lhs, at, m in ((tri_strict[0:EP, 0:EP], 0, EP), (ones[0:EP, :], 1024, P)):
                        mm(psf[0:m, at:at + 512], lhs, fj[:, 0:512], start=True, stop=True)
                        last = mm(psf[0:m, at + 512:at + NC * P], lhs, fj[:, 512:NC * P], start=True, stop=True)
                    last.then_inc(joint_mm, 1)
            with te.Else():
                te.wait_ge(flag_ready, 1)

            project(0, 1)
            te.wait_ge(prep_in, 3)
            for c in range(NC):
                mm(ps[:, 0, 0:3 * QT], ohA[:, c, :], wB[:, c, :, :].rearrange("p a b -> p (a b)"),
                   start=(c == 0), stop=(c == NC - 1))
            for c in range(NC):
                last = mm(ps[:, 1, 0:QT], ohA[:, NC + c, :], wB2[:, c, :], start=(c == 0), stop=(c == NC - 1))
            last.then_inc(prep_mm, 1)
            te.wait_ge(prep_in, 4)
            fi = imp.rearrange("p a b -> p (a b)")
            mm(ps[:, 2, 0:4 * QT], ones, fi, start=True, stop=True)
            mm(ps[:, 3, 0:4 * QT], tri_incl, fi, start=True, stop=True).then_inc(prep_mm, 1)
            project(0, 2)
            te.wait_ge(e0_ready, 1)
            nc.tensor.transpose(ps[0:QT, 2, 0:P], dstq[:, :], ident[:, :]).then_inc(dst_mm, 1)
            transposes(0, 2)

            def fold(t, half):
                te.wait_ge(z_ready, t * 2 + (1 + half))
                parts = z[:, 1, :].rearrange("p (h f n) -> p f h n", h=H1, f=FOLD)
                to = ps[:, 6 + half, 0:D // FOLD].rearrange("p (h n) -> p h n", h=H1)
                for f in range(FOLD):
                    last = mm(to, ident[:, :], parts[:, f, :, :], start=(f == 0), stop=(f == FOLD - 1))
                last.then_inc(folded, 1)

            def add_edge(l, t, u, j, first=False):
                if j == 0 and not first:
                    te.wait_ge(sum_saved[l], t - (RING - 1))
                if j < ACT_EDGES[l]:
                    te.wait_ge(prod_ready[l], t * ACT_EDGES[l] + (j + 1))
                else:
                    te.wait_ge(prod3_ready, t + 1)
                for hf in range(2):
                    last = mm(ps[:, 2 * u + hf, 0:HALF], ident[:, :], gring[:, u, j, hf * HALF:(hf + 1) * HALF],
                              start=(j == 0), stop=(j == G - 1), skip_group_check=True)
                last.then_inc(sum_mm[l], 1)

            def sums(l, t, u, first=False):
                if l == 0:
                    fold(t + 1, 0)
                if not (first and u == 0):
                    add_edge(l, t - 1, (u - 1) % RING, G - 1)
                add_edge(l, t, u, 0, first)
                if l == 0:
                    fold(t + 1, 1)
                add_edge(l, t, u, 1)
                add_edge(l, t, u, 2)

            def item_trip(l, i0, n):
                why = "the items are made on the chip within these bounds"
                _, where = nc.values_load_multi_w_load_instructions(
                    items[0:1, ds(i0, n), :].rearrange("p i k -> p (i k)"), engines=(mybir.EngineType.PE,),
                    min_val=0, max_val=QT - 1, skip_runtime_bounds_check_because=why)
                for u in range(n):
                    C = nc.s_assert_within(where[2 * u + 1], 0, NC - 1, skip_runtime_bounds_check_because=why)
                    item(l, i0 + u, u % RING, where[2 * u], C)

            def item(l, i, u, T, C):
                cb = combine_views(heads[l])
                te.wait_ge(hot_ready[l], i + 1)
                te.wait_ge(comb_const, 2 * l + 2)
                row = vres[:, ds(T, 1), :].rearrange("p a n -> p (a n)")
                third = D // 3
                for k in range(3):
                    mm(psf[:, ds(C * D + k * third, third)], cb["hot"][:, u, :], row[:, k * third:(k + 1) * third],
                       start=False, stop=False, skip_group_check=True)
                dn = row[:, D:ROW] if l == 0 else row[:, D + 1:D + 2]
                mm(psf[:, ds(C * 8 + NC * D, dn.shape[1])], cb["hot"][:, u, :], dn,
                   start=False, stop=False, skip_group_check=True).then_inc(item_mm[l], 1)

            for l in range(2):
                H = heads[l]
                if l:
                    transposes(l, 0)
                for n in range((3, 0)[l], 2 * NC):
                    project(l, n)
                    if l == 0 and n == 4:
                        te.wait_ge(prep_done, 1)
                    if n % 2 == 0 and n // 2 + 1 < NC:
                        transposes(l, n // 2 + 1)
                te.wait_ge(proj_read, 2 * NC * (l + 1))
                if l == 0:
                    fold(0, 0)
                    fold(0, 1)
                for t in range(RING):
                    sums(l, t, t, True)
                with te.Fori(1, LOOPS) as i:
                    for u in range(RING):
                        sums(l, i * RING + u, u)

                add_edge(l, QT - 2, (QT - 2) % RING, G - 1)
                cb = combine_views(H)
                assert QT == LOOPS * RING + 1
                te.wait_ge(dlt_ready[l], QT)
                for h in range(H):
                    last = nc.tensor.transpose(psf[0:QT, 3072 + h * P:3072 + (h + 1) * P], gmx(l)[:, :, h], ident[:, :])
                last.then_inc(seg_mm, 1)
                te.wait_ge(sum_saved[l], QT - 2)
                te.wait_ge(seg_in, 3 * l + 1)
                for k in range(2):
                    last = nc.tensor.transpose(ps[0:H, 3, k * QT:(k + 1) * QT], cb["edgeq"][0:QT, k, :], ident[0:QT, 0:QT])
                last.then_inc(seg_mm, 1)
                add_edge(l, QT - 1, 0, 0)
                add_edge(l, QT - 1, 0, 1)
                te.wait_ge(seg_in, 3 * l + 2)
                for k in range(2):
                    last = nc.tensor.transpose(ps[0:H, 2, k * QT:(k + 1) * QT], cb["edge"][0:QT, k, :], ident[0:QT, 0:QT])
                last.then_inc(seg_mm, 1)
                add_edge(l, QT - 1, 0, 2)
                add_edge(l, QT - 1, 0, 3)
                te.wait_ge(seg_in, 3 * l + 3)
                for k in range(2):
                    last = nc.tensor.transpose(ps[0:QT, 2, 256 + k * H:256 + (k + 1) * H], cb["sm"][0:H, :, k], ident[0:H, 0:H])
                last.then_inc(seg_mm, 1)
                te.wait_ge(comb_const, 2 * l + 1)
                te.wait_ge(sum_saved[l], QT)

                def clear(b):
                    mm(ps[:, b, :], cb["zrow"][0:1, 0:P], cb["zrow"][0:1, :], start=True, stop=False,
                       skip_group_check=True)

                for b in (0, 1, 3, 4):
                    clear(b)
                te.wait_ge(wT_ready, l + 1)
                for h in range(H):
                    last = nc.tensor.transpose(ps[:, 5, h * QT:(h + 1) * QT], cb["mT"][0:QT, h, :], ident[0:QT, 0:QT])
                last.then_inc(w_mm, 1)
                for b in (2, 6, 7):
                    clear(b)
                te.wait_ge(w_ready, l + 1)
                clear(5)
                item_trip(l, 0, SIX)
                with te.Fori(1, ITEMS // SIX) as i:
                    item_trip(l, i * SIX, SIX)
                item_trip(l, ITEMS // SIX * SIX, ITEMS % SIX)


_INS = ['x', 'src', 'dst', 'L0_gnn_W1s', 'L0_gnn_b1s', 'L0_gnn_W1d', 'L0_gnn_b1d', 'L0_gnn_attn1', 'L0_gnn_ln1_w',
        'L0_gnn_ln1_b', 'L0_gnn_Wos', 'L0_gnn_bos', 'L0_gnn_Wod', 'L0_gnn_bod', 'L0_gnn_attno', 'L0_gnn_lno_w',
        'L0_gnn_lno_b']


def kernel(**inputs):
    import numpy as _np
    import concourse.bacc as _bacc
    from concourse import mybir as _mybir
    from concourse.bass_utils import run_bass_kernel_spmd as _run

    nc = _bacc.Bacc("TRN2", target_bir_lowering=False, num_devices=1)
    arrays, args = {}, []
    for name in _INS:
        a = _np.ascontiguousarray(inputs[name])
        arrays[f"in_{name}_dram"] = a
        args.append(nc.dram_tensor(f"in_{name}_dram", a.shape, _mybir.dt.from_np(a.dtype), kind="ExternalInput").ap())
    out = nc.dram_tensor("out_0_dram", inputs['x'].shape, _mybir.dt.float32, kind="ExternalOutput").ap()
    gnn_kernel(nc, *args, out)
    r = _run(nc, [arrays], core_ids=[0])
    return r.results[0]["out_0_dram"]
```
